# Optimizing a Trainium2 kernel written in Bass

```python
import numpy as np
import jax
import jax.numpy as jnp

def _softmax(x, axis=-1):
    return jax.nn.softmax(x, axis=axis)

def _gelu(x):
    return jax.nn.gelu(x, approximate=True)

def _silu(x):
    return jax.nn.silu(x)

def _sigmoid(x):
    return jax.nn.sigmoid(x)

def _layernorm(x, axis=-1, eps=1e-05):
    m = jnp.mean(x, axis=axis, keepdims=True)
    v = jnp.var(x, axis=axis, keepdims=True)
    return (x - m) / jnp.sqrt(v + eps)

def _scatter_add(tgt, idx, src, axis=0):
    return tgt.at[idx].add(src)

def _segment_sum(src, seg, n):
    return jax.ops.segment_sum(src, seg, n)
kernel_name = 'mk_early_fusion_d1_tok_img4096_r4_e81023'

def setup_inputs(seed: int=0):
    np.random.seed(seed)
    _w = jnp.asarray

    def _rec_inputs():
        import jax
        import jax.numpy as jnp
        _rk = jax.random.key(seed)
        x = -0.00348982 + 0.707501 * jax.random.normal(jax.random.fold_in(_rk, 1), (16, 128, 64, 2), jnp.float32)
        txt = 6.73332e-06 + 0.02 * jax.random.normal(jax.random.fold_in(_rk, 2), (16, 32, 1024), jnp.float32)
        return (x, txt)
    x, txt = _rec_inputs()

    def _L0_tok_setup():
        import jax, jax.numpy as jnp
        import numpy as np
        H, N, S, CH, LEN = (128, 64, 128, 1, 1024)

        def _s4d_kernel(log_dt, C, B, inv_A_real, A_imag, L):
            dt = jnp.exp(log_dt)
            Cc = C[..., 0] + 1j * C[..., 1]
            Bc = B[..., 0] + 1j * B[..., 1]
            A = -jnp.exp(inv_A_real) + 1j * A_imag
            rep = H // A.shape[0]
            A = jnp.tile(A, (rep, 1))
            Bc = jnp.tile(Bc, (rep, 1))
            dtA = A * dt[:, None]
            Cc = Bc[None, :, :] * Cc
            Cc = Cc * (jnp.exp(dtA) - 1.0) / A
            ell = jnp.arange(L, dtype=jnp.float32)
            V = jnp.exp(dtA[:, :, None] * ell)
            K = 2.0 * jnp.einsum('chn,hnl->chl', Cc, V).real
            return K.astype(jnp.float32)
        key = jax.random.key(seed)
        k1, k2 = jax.random.split(key, 2)
        log_dt = jax.random.uniform(k1, (H,), minval=float(np.log(0.001)), maxval=float(np.log(0.1))).astype(jnp.float32)
        inv_A_real = jnp.full((S, N), float(np.log(0.5)), dtype=jnp.float32)
        A_imag = jnp.tile((np.pi * jnp.arange(N, dtype=jnp.float32))[None, :], (S, 1))
        B = jnp.stack([jnp.ones((S, N), jnp.float32), jnp.zeros((S, N), jnp.float32)], axis=-1)
        C = (jax.random.normal(k2, (CH, H, N, 2)) * 0.5 ** 0.5).astype(jnp.float32)
        return {'log_dt': log_dt, 'C': C, 'B': B, 'inv_A_real': inv_A_real, 'A_imag': A_imag, 'L': LEN}
    _L0_tok_all = _L0_tok_setup()
    _L0_tok_in = {k: v for k, v in _L0_tok_all.items() if k in ('log_dt', 'B', 'inv_A_real', 'A_imag')}
    del _L0_tok_all

    def _L0_attn_setup():
        import jax, jax.numpy as jnp
        import numpy as np
        import math
        DIM = 1024
        N_HEADS = 32
        N_KV_HEADS = 8
        HEAD_DIM = DIM // N_HEADS
        N_REP = N_HEADS // N_KV_HEADS
        ROPE_BASE = 10000.0

        def apply_rotary_emb(x):
            b, s, h, d = x.shape
            inv_freq = 1.0 / ROPE_BASE ** (jnp.arange(0, d, 2, dtype=jnp.float32) / d)
            pos = jnp.arange(s, dtype=jnp.float32)
            ang = pos[:, None] * inv_freq[None, :]
            cos = jnp.cos(ang)[None, :, None, :]
            sin = jnp.sin(ang)[None, :, None, :]
            xr = x.reshape(b, s, h, d // 2, 2)
            x0, x1 = (xr[..., 0], xr[..., 1])
            out = jnp.stack([x0 * cos - x1 * sin, x0 * sin + x1 * cos], axis=-1)
            return out.reshape(b, s, h, d)
        key = jax.random.key(seed)
        ks = jax.random.split(key, 5)
        sc = 1.0 / math.sqrt(DIM)
        return {'x': jax.random.normal(ks[0], (2, 512, DIM), dtype=jnp.float32), 'Wq': jax.random.normal(ks[1], (DIM, N_HEADS * HEAD_DIM), dtype=jnp.float32) * sc, 'Wk': jax.random.normal(ks[2], (DIM, N_KV_HEADS * HEAD_DIM), dtype=jnp.float32) * sc, 'Wv': jax.random.normal(ks[3], (DIM, N_KV_HEADS * HEAD_DIM), dtype=jnp.float32) * sc, 'Wo': jax.random.normal(ks[4], (N_HEADS * HEAD_DIM, DIM), dtype=jnp.float32) * sc}
    _L0_attn_all = _L0_attn_setup()
    _L0_attn_in = {k: v for k, v in _L0_attn_all.items() if k in ('Wq', 'Wk', 'Wv', 'Wo')}
    del _L0_attn_all

    def _L0_ffn_setup():
        import jax, jax.numpy as jnp
        import numpy as np

        @jax.custom_vjp
        def ste_sign(w):
            return jnp.sign(w)

        def _ste_fwd(w):
            return (jnp.sign(w), w)

        def _ste_bwd(w, g):
            mask = ((w > -1) & (w < 1)).astype(g.dtype)
            return (g * mask,)
        ste_sign.defvjp(_ste_fwd, _ste_bwd)
        key = jax.random.key(seed)
        k = jax.random.split(key, 6)
        B, S, H, O, E = (4, 512, 1024, 1024, 8)
        return {'x': jax.random.normal(k[0], (B, S, H), dtype=jnp.float32), 'weight': jax.random.normal(k[1], (O, H), dtype=jnp.float32) * 0.02, 'bias': jax.random.normal(k[2], (O,), dtype=jnp.float32) * 0.02, 'gate_w': jax.random.normal(k[3], (E, H), dtype=jnp.float32) * 0.02, 'in_channel_scale': jax.random.normal(k[4], (E, H), dtype=jnp.float32), 'out_channel_scale': jax.random.normal(k[5], (E, O), dtype=jnp.float32)}
    _L0_ffn_all = _L0_ffn_setup()
    _L0_ffn_in = {k: v for k, v in _L0_ffn_all.items() if k in ('weight', 'bias', 'gate_w', 'in_channel_scale', 'out_channel_scale')}
    del _L0_ffn_all
    return {'x': x, 'txt': txt, 'L0_tok_log_dt': _L0_tok_in['log_dt'], 'L0_tok_B': _L0_tok_in['B'], 'L0_tok_inv_A_real': _L0_tok_in['inv_A_real'], 'L0_tok_A_imag': _L0_tok_in['A_imag'], 'L0_attn_Wq': _L0_attn_in['Wq'], 'L0_attn_Wk': _L0_attn_in['Wk'], 'L0_attn_Wv': _L0_attn_in['Wv'], 'L0_attn_Wo': _L0_attn_in['Wo'], 'L0_ffn_weight': _L0_ffn_in['weight'], 'L0_ffn_bias': _L0_ffn_in['bias'], 'L0_ffn_gate_w': _L0_ffn_in['gate_w'], 'L0_ffn_in_channel_scale': _L0_ffn_in['in_channel_scale'], 'L0_ffn_out_channel_scale': _L0_ffn_in['out_channel_scale']}

def reference(x, txt, L0_tok_log_dt, L0_tok_B, L0_tok_inv_A_real, L0_tok_A_imag, L0_attn_Wq, L0_attn_Wk, L0_attn_Wv, L0_attn_Wo, L0_ffn_weight, L0_ffn_bias, L0_ffn_gate_w, L0_ffn_in_channel_scale, L0_ffn_out_channel_scale):
    import jax
    import jax.numpy as jnp

    def _L0_tok_ref(log_dt, C, B, inv_A_real, A_imag, L):
        import jax, jax.numpy as jnp
        import numpy as np
        H, N, S, CH, LEN = (128, 64, 128, 1, 1024)

        def _s4d_kernel(log_dt, C, B, inv_A_real, A_imag, L):
            dt = jnp.exp(log_dt)
            Cc = C[..., 0] + 1j * C[..., 1]
            Bc = B[..., 0] + 1j * B[..., 1]
            A = -jnp.exp(inv_A_real) + 1j * A_imag
            rep = H // A.shape[0]
            A = jnp.tile(A, (rep, 1))
            Bc = jnp.tile(Bc, (rep, 1))
            dtA = A * dt[:, None]
            Cc = Bc[None, :, :] * Cc
            Cc = Cc * (jnp.exp(dtA) - 1.0) / A
            ell = jnp.arange(L, dtype=jnp.float32)
            V = jnp.exp(dtA[:, :, None] * ell)
            K = 2.0 * jnp.einsum('chn,hnl->chl', Cc, V).real
            return K.astype(jnp.float32)
        return _s4d_kernel(log_dt, C, B, inv_A_real, A_imag, L)

    def _L0_attn_ref(x, Wq, Wk, Wv, Wo):
        import jax, jax.numpy as jnp
        import numpy as np
        import math
        DIM = 1024
        N_HEADS = 32
        N_KV_HEADS = 8
        HEAD_DIM = DIM // N_HEADS
        N_REP = N_HEADS // N_KV_HEADS
        ROPE_BASE = 10000.0

        def apply_rotary_emb(x):
            b, s, h, d = x.shape
            inv_freq = 1.0 / ROPE_BASE ** (jnp.arange(0, d, 2, dtype=jnp.float32) / d)
            pos = jnp.arange(s, dtype=jnp.float32)
            ang = pos[:, None] * inv_freq[None, :]
            cos = jnp.cos(ang)[None, :, None, :]
            sin = jnp.sin(ang)[None, :, None, :]
            xr = x.reshape(b, s, h, d // 2, 2)
            x0, x1 = (xr[..., 0], xr[..., 1])
            out = jnp.stack([x0 * cos - x1 * sin, x0 * sin + x1 * cos], axis=-1)
            return out.reshape(b, s, h, d)
        b, s, _ = x.shape
        xq = (x @ Wq).reshape(b, s, N_HEADS, HEAD_DIM)
        xk = (x @ Wk).reshape(b, s, N_KV_HEADS, HEAD_DIM)
        xv = (x @ Wv).reshape(b, s, N_KV_HEADS, HEAD_DIM)
        xq = apply_rotary_emb(xq)
        xk = apply_rotary_emb(xk)
        xk = jnp.repeat(xk, N_REP, axis=2)
        xv = jnp.repeat(xv, N_REP, axis=2)
        scores = jnp.einsum('bqhd,bkhd->bhqk', xq, xk) / math.sqrt(HEAD_DIM)
        causal = jnp.tril(jnp.ones((s, s), dtype=bool))
        scores = jnp.where(causal[None, None], scores, -jnp.inf)
        probs = jax.nn.softmax(scores.astype(jnp.float32), axis=-1).astype(xq.dtype)
        out = jnp.einsum('bhqk,bkhd->bqhd', probs, xv).reshape(b, s, N_HEADS * HEAD_DIM)
        return out @ Wo

    def _L0_ffn_ref(x, weight, bias, gate_w, in_channel_scale, out_channel_scale):
        import jax, jax.numpy as jnp
        import numpy as np

        @jax.custom_vjp
        def ste_sign(w):
            return jnp.sign(w)

        def _ste_fwd(w):
            return (jnp.sign(w), w)

        def _ste_bwd(w, g):
            mask = ((w > -1) & (w < 1)).astype(g.dtype)
            return (g * mask,)
        ste_sign.defvjp(_ste_fwd, _ste_bwd)
        B, S, H = x.shape
        xf = x.reshape(-1, H)
        router_logits = xf @ gate_w.T
        routing = jax.nn.softmax(router_logits.astype(jnp.float32), axis=1).astype(x.dtype)
        in_scale = routing @ in_channel_scale
        out_scale = routing @ out_channel_scale
        wb = ste_sign(weight)
        out = xf * in_scale @ wb.T * out_scale + bias
        return out.reshape(B, S, -1)
    h = _L0_tok_ref(L0_tok_log_dt, x, L0_tok_B, L0_tok_inv_A_real, L0_tok_A_imag, 1024)
    h = jnp.concatenate([h, txt], axis=1)
    h = h + _L0_attn_ref(_layernorm(h, axis=-1), L0_attn_Wq, L0_attn_Wk, L0_attn_Wv, L0_attn_Wo)
    h = h + _L0_ffn_ref(_layernorm(h, axis=-1), L0_ffn_weight, L0_ffn_bias, L0_ffn_gate_w, L0_ffn_in_channel_scale, L0_ffn_out_channel_scale)
    return h

_drawn_inputs = setup_inputs


def setup_inputs(seed=0):
    import zlib

    import numpy as np

    out = dict(_drawn_inputs(seed))
    spreads = {'L0_tok_inv_A_real': (-0.6931471824645996, 0.2)}
    factors = {'L0_ffn_bias': 8.0}
    for name, (base, spread) in spreads.items():
        noise = np.random.default_rng([zlib.crc32(name.encode()), seed]).standard_normal(out[name].shape)
        drawn = base * np.exp(spread * noise) if base else spread * noise
        out[name] = jnp.asarray(drawn.astype(out[name].dtype))
    for name, factor in factors.items():
        out[name] = (out[name] * factor).astype(out[name].dtype)
    return out
```

```python
import concourse.bass as bass
from concourse import mybir
from contextlib import ExitStack
import numpy as np

F32 = mybir.dt.float32
F16 = mybir.dt.float16
BF16 = mybir.dt.bfloat16
I32 = mybir.dt.int32
ALU = mybir.AluOpType
ACT = mybir.ActivationFunctionType
AX = mybir.AxisListType

P = 128
HEADS = 128
CH = 16
MODES = 64
LEN = 1024
JL = 128
IH = LEN // JL
ROUND = 12582912.0
TURN = 6.283184
HC = 8


def s4d_block(nc, par_d, xr_d, xi_d, digit_d, phase_d, h_d):
    with ExitStack() as ctx:
        def sb(name, shape, dt=F32):
            return ctx.enter_context(nc.sbuf_tensor(name, shape, dt))

        def sem(name):
            return ctx.enter_context(nc.semaphore(name))

        par = sb("s4_par", [P, 5, HEADS])
        xr = sb("s4_xr", [P, HEADS, CH])
        xi = sb("s4_xi", [P, HEADS, CH])
        digit = sb("s4_digit", [P, JL + IH])
        phase = sb("s4_phase", [P, 4])
        dt_ = sb("s4_dt", [P, HEADS])
        ea = sb("s4_ea", [P, HEADS])
        decay = sb("s4_decay", [P, HEADS])
        turns = sb("s4_turns", [P, HEADS])
        ez = sb("s4_ez", [P, HEADS])
        small = sb("s4_small", [P, 12, HEADS])
        smalli = sb("s4_smalli", [P, HEADS], I32)
        pamp = sb("s4_pamp", [P, HEADS, IH])
        y1 = sb("s4_y1", [P, HEADS, IH])
        y2 = sb("s4_y2", [P, HEADS, IH])
        low = sb("s4_low", [P, HEADS, JL])
        whole = sb("s4_whole", [P, HC, JL])
        ang = sb("s4_ang", [P, 2, HC, JL])
        lowp = sb("s4_lowp", [P, 2, HC, JL])
        g1 = sb("s4_g1", [P, 2, HC, IH, CH])
        g2 = sb("s4_g2", [P, 2, HC, IH, CH])
        ptmp = g1[:, :, :, :, :].rearrange("p s h i c -> p (s h i c)").rearrange("p (a h i) -> p a h i", a=2, i=IH)
        pang = g2[:, :, :, :, :].rearrange("p s h i c -> p (s h i c)").rearrange("p (a h i) -> p a h i", a=2, i=IH)
        hall = sb("s4_hall", [P, IH * CH, HEADS])
        ps = [[ctx.enter_context(nc.psum_tensor(f"s4_ps{s}{b}", [P, 4, P], F32)) for b in range(2)] for s in range(2)]

        loaded, loaded_x = sem("s4_loaded"), sem("s4_loaded_x")
        chain = sem("s4_chain")
        expo_in, expo_out = sem("s4_expo_in"), sem("s4_expo_out")
        low_amp = sem("s4_low_amp")
        trig_in, trig_out = sem("s4_trig_in"), sem("s4_trig_out")
        chunk_step = sem("s4_chunk_step")
        y_ready = sem("s4_y_ready")
        ang_in, ang_out = sem("s4_ang_in"), sem("s4_ang_out")
        gi_ready = sem("s4_gi_ready")
        ps_full = [[sem(f"s4_ps_full{s}{b}") for b in range(2)] for s in range(2)]
        ops_free = [ps_full[s][1] for s in range(2)]
        copied = [sem("s4_copied_vector"), sem("s4_copied_scalar")]
        stored = sem("s4_stored")
        block = ctx.enter_context(nc.Block())
        NCHUNK = HEADS // HC

        def copy_out(copy, q, s, b):
            copy(hall[:, :, bass.ds(q * HC + 4 * b, 4)], ps[s][b][:, :, :].rearrange("p h c -> p c h")).then_inc(copied[b], 1)

        @block.sync
        def _(sp):
            sp.dma_start(par[:, :, :], par_d).then_inc(loaded, 16)
            sp.dma_start(digit[:, :], digit_d).then_inc(loaded, 16)
            sp.dma_start(phase[:, :], phase_d).then_inc(loaded, 16)
            sp.dma_start(xr[:, :, :], xr_d).then_inc(loaded_x, 16)
            sp.dma_start(xi[:, :, :], xi_d).then_inc(loaded_x, 16)
            sp.wait_ge(copied[0], NCHUNK + 1)
            sp.wait_ge(copied[1], NCHUNK + 1)
            for pr in range(CH // 2):
                for b in range(2):
                    sp.dma_start(h_d[pr, :, :, b, :], hall[:, 2 * pr + b:IH * CH:CH, :]).then_inc(stored, 16)
            sp.wait_ge(stored, 16 * CH)

        @block.vector
        def _(dve):
            done = [0]

            def link(ins):
                done[0] += 1
                ins.then_inc(chain, 1)
                dve.wait_ge(chain, done[0])

            v = nc.vector
            t = [small[:, k, :] for k in range(12)]

            def exact_exp(out, x):
                a, b, c = t[0], t[1], t[2]
                link(v.tensor_scalar(a, x, 88.0, -87.0, ALU.min, ALU.max))
                link(v.tensor_scalar(b, a, 1.4426950408889634, ROUND, ALU.mult, ALU.add))
                link(v.tensor_scalar(b, b, ROUND, None, ALU.subtract))
                link(v.scalar_tensor_tensor(a, b, -0.693145751953125, a, ALU.mult, ALU.add))
                link(v.scalar_tensor_tensor(a, b, -1.42860682030941723e-6, a, ALU.mult, ALU.add))
                link(v.tensor_scalar(c, a, 1.0 / 5040, None, ALU.mult))
                for k in (720, 120, 24, 6, 2, 1):
                    link(v.scalar_tensor_tensor(c, c, 1.0 / k, a, ALU.add, ALU.mult))
                link(v.tensor_scalar(c, c, 1.0, None, ALU.add))
                link(v.tensor_scalar(b, b, 127.0, 8388608.0, ALU.add, ALU.mult))
                link(v.tensor_copy(smalli[:, :], b))
                link(v.tensor_tensor(out, c, smalli[:, :].bitcast(F32), ALU.mult))

            dve.wait_ge(loaded, 48)
            exact_exp(dt_[:, :], par[:, 0, :])
            exact_exp(ea[:, :], par[:, 1, :])
            link(v.scalar_tensor_tensor(decay[:, :], ea[:, :], -1.0, dt_[:, :], ALU.mult, ALU.mult))
            v.tensor_tensor(pamp[:, :, :], decay[:, :].unsqueeze(2).broadcast_to([P, HEADS, IH]),
                            digit[:, JL:].unsqueeze(1).broadcast_to([P, HEADS, IH]), ALU.mult).then_inc(expo_in, 1)
            link(v.tensor_tensor(turns[:, :], par[:, 2, :], dt_[:, :], ALU.mult))
            link(v.tensor_scalar(turns[:, :], turns[:, :], float(1 / (2 * np.pi)), None, ALU.mult))
            link(v.tensor_scalar(t[3], turns[:, :], ROUND, None, ALU.add))
            link(v.scalar_tensor_tensor(t[3], t[3], ROUND, turns[:, :], ALU.subtract, ALU.subtract))
            link(v.tensor_scalar(turns[:, :], t[3], -1.0, None, ALU.mult))

            def fraction(out, y, shift):
                link(v.tensor_scalar(out, y, shift, ROUND, ALU.add, ALU.add))
                return v.scalar_tensor_tensor(out, out, ROUND, y, ALU.subtract, ALU.subtract)

            fraction(t[4], turns[:, :], 0.0).then_inc(trig_in, 1)
            fraction(t[5], turns[:, :], 0.25).then_inc(trig_in, 1)
            link(v.tensor_tensor(ptmp[:, 0, :, :], turns[:, :].unsqueeze(2).broadcast_to([P, HEADS, IH]),
                                 digit[:, JL:].unsqueeze(1).broadcast_to([P, HEADS, IH]), ALU.mult))
            fraction(pang[:, 0, :, :], ptmp[:, 0, :, :], 0.0).then_inc(trig_in, 1)
            fraction(pang[:, 1, :, :], ptmp[:, 0, :, :], 0.25).then_inc(trig_in, 1)
            exact_exp(ez[:, :], decay[:, :])
            link(v.tensor_tensor(t[6], ea[:, :], ea[:, :], ALU.mult))
            link(v.tensor_tensor(t[7], par[:, 2, :], par[:, 2, :], ALU.mult))
            link(v.tensor_tensor(t[6], t[6], t[7], ALU.add))
            link(v.reciprocal(t[6], t[6]))

            dve.wait_ge(trig_out, 2)
            zr, zi, br, bi = t[8], t[9], par[:, 3, :], par[:, 4, :]
            link(v.tensor_tensor(zr, ez[:, :], t[5], ALU.mult))
            link(v.tensor_tensor(zi, ez[:, :], t[4], ALU.mult))
            link(v.tensor_scalar(zr, zr, 1.0, None, ALU.subtract))
            link(v.tensor_tensor(t[0], br, zr, ALU.mult))
            link(v.tensor_tensor(t[1], bi, zi, ALU.mult))
            link(v.tensor_tensor(t[10], t[0], t[1], ALU.subtract))
            link(v.tensor_tensor(t[0], br, zi, ALU.mult))
            link(v.tensor_tensor(t[1], bi, zr, ALU.mult))
            link(v.tensor_tensor(t[11], t[0], t[1], ALU.add))
            link(v.tensor_tensor(t[0], t[11], par[:, 2, :], ALU.mult))
            link(v.tensor_tensor(t[1], t[10], ea[:, :], ALU.mult))
            link(v.tensor_tensor(t[0], t[0], t[1], ALU.subtract))
            link(v.scalar_tensor_tensor(t[8], t[0], 2.0, t[6], ALU.mult, ALU.mult))
            link(v.tensor_tensor(t[0], t[11], ea[:, :], ALU.mult))
            link(v.tensor_tensor(t[1], t[10], par[:, 2, :], ALU.mult))
            link(v.tensor_tensor(t[0], t[0], t[1], ALU.add))
            link(v.scalar_tensor_tensor(t[9], t[0], -2.0, t[6], ALU.mult, ALU.mult))
            dve.wait_ge(trig_out, 4)
            dve.wait_ge(expo_out, 1)
            fr = t[8].unsqueeze(2).broadcast_to([P, HEADS, IH])
            fi = t[9].unsqueeze(2).broadcast_to([P, HEADS, IH])
            psin, pcos = pang[:, 0, :, :], pang[:, 1, :, :]
            link(v.tensor_tensor(psin, psin, pamp[:, :, :], ALU.mult))
            link(v.tensor_tensor(pcos, pcos, pamp[:, :, :], ALU.mult))
            a, b = ptmp[:, 0, :, :], ptmp[:, 1, :, :]
            link(v.tensor_tensor(a, pcos, fr, ALU.mult))
            link(v.tensor_tensor(b, psin, fi, ALU.mult))
            link(v.tensor_tensor(y1[0:MODES, :, :], a[0:MODES], b[0:MODES], ALU.subtract))
            link(v.tensor_tensor(y2[MODES:P, :, :], b[MODES:P], a[MODES:P], ALU.subtract))
            link(v.tensor_tensor(a, pcos, fi, ALU.mult))
            link(v.tensor_tensor(b, psin, fr, ALU.mult))
            link(v.tensor_tensor(a, a, b, ALU.add))
            link(v.tensor_scalar(y2[0:MODES, :, :], a[0:MODES], -1.0, None, ALU.mult))
            v.tensor_scalar(y1[MODES:P, :, :], a[MODES:P], -1.0, None, ALU.mult).then_inc(y_ready, 1)
            dve.wait_ge(y_ready, 1)
            dve.wait_ge(loaded_x, 32)
            with dve.Fori(0, NCHUNK // 2) as it:
                steps = [0]

                def step(ins):
                    steps[0] += 1
                    ins.then_inc(chunk_step, 1)
                    dve.wait_ge(chunk_step, 10 * it + steps[0])

                for s in range(2):
                    q = 2 * it + s
                    hs = bass.ds(q * HC, HC)
                    step(v.tensor_tensor(whole[:, :, :], turns[:, hs].unsqueeze(2).broadcast_to([P, HC, JL]),
                                         digit[:, 0:JL].unsqueeze(1).broadcast_to([P, HC, JL]), ALU.mult))
                    step(v.tensor_scalar(ang[:, s], whole[:, :, :], phase[:, 0:1], ROUND, ALU.add, ALU.add))
                    v.scalar_tensor_tensor(ang[:, s], ang[:, s], ROUND, whole[:, :, :], ALU.subtract, ALU.subtract).then_inc(ang_in, 1)
                    dve.wait_ge(ops_free[s], it + 1)
                    step(v.tensor_tensor(g1[:, s], xr[:, hs, :].unsqueeze(2).broadcast_to([P, HC, IH, CH]),
                                         y1[:, hs, :].unsqueeze(3).broadcast_to([P, HC, IH, CH]), ALU.mult))
                    dve.wait_ge(gi_ready, q + 1)
                    step(v.tensor_tensor(g1[:, s], g1[:, s], g2[:, s], ALU.add))
                    dve.wait_ge(ang_out, q + 1)
                    step(v.tensor_tensor(lowp[:, s], low[:, hs, :], ang[:, s], ALU.mult))
                    dve.wait_ge(ps_full[s][0], it + 1)
                    copy_out(v.tensor_copy, q, s, 0)
                assert steps[0] == 10

        @block.gpsimd
        def _(pool):
            for s in (*ops_free, *copied):
                pool.sem_inc(s, 1)
            pool.wait_ge(y_ready, 1)
            pool.wait_ge(loaded_x, 32)
            with pool.Fori(0, NCHUNK // 2) as it:
                for s in range(2):
                    q = 2 * it + s
                    hs = bass.ds(q * HC, HC)
                    pool.wait_ge(ops_free[s], it + 1)
                    nc.gpsimd.tensor_tensor(g2[:, s], xi[:, hs, :].unsqueeze(2).broadcast_to([P, HC, IH, CH]),
                                            y2[:, hs, :].unsqueeze(3).broadcast_to([P, HC, IH, CH]), ALU.mult).then_inc(gi_ready, 1)

        @block.scalar
        def _(act):
            s_ = nc.scalar
            act.wait_ge(expo_in, 1)
            s_.activation(pamp[:, :, :], pamp[:, :, :], ACT.Exp).then_inc(expo_out, 1)
            with act.Fori(0, HEADS // 4) as it:
                for k in range(4):
                    s_.activation(low[:, bass.ds(4 * it + k, 1), :], digit[:, 0:JL].unsqueeze(1), ACT.Exp,
                                  scale=decay[:, bass.ds(4 * it + k, 1)]).then_inc(low_amp, 1)
            act.wait_ge(trig_in, 4)
            for k, tile in enumerate((small[:, 4, :], small[:, 5, :], pang[:, 0, :, :], pang[:, 1, :, :])):
                if k % 2:
                    s_.activation(tile, tile, ACT.Sin, scale=-TURN, bias=phase[:, 3:4]).then_inc(trig_out, 1)
                else:
                    s_.activation(tile, tile, ACT.Sin, scale=-TURN).then_inc(trig_out, 1)
            with act.Fori(0, NCHUNK // 2) as it:
                for s in range(2):
                    q = 2 * it + s
                    act.wait_ge(ang_in, q + 1)
                    s_.activation(ang[:, s], ang[:, s], ACT.Sin, scale=-TURN, bias=phase[:, 1:2]).then_inc(ang_out, 1)
                    act.wait_ge(ps_full[s][1], it + 2)
                    copy_out(s_.copy, q, s, 1)

        @block.tensor
        def _(pe):
            with pe.Fori(0, NCHUNK // 2) as it:
                for s in range(2):
                    q = 2 * it + s
                    pe.wait_ge(chunk_step, 10 * it + 5 * s + 5)
                    for b in range(2):
                        pe.wait_ge(copied[b], q + 1)
                        for k in range(4):
                            last = nc.tensor.matmul(ps[s][b][:, k, :], lowp[:, s, 4 * b + k, :],
                                                    g1[:, s, 4 * b + k].rearrange("p i c -> p (i c)"), start=True, stop=True)
                        last.then_inc(ps_full[s][b], 1)

DIM, T, NPAIR, KB = 1024, 320, 8, 8
NQ, NKV, HD = 32, 8, 32
EXPERTS = 8
EPS = 1e-5
XS = 32.0
SHIFT = 4096.0
QKB = 5
A0, A1, BT = slice(0, 128), slice(128, 256), slice(256, 320)

USES = (["mean1", "var1"] + [f"qk{j}{ab}" for j in (4, 0, 1, 2, 3) for ab in "ab"] + ["v01", "v2", "maxT"]
        + ["atA00", "atA01", "atA10", "atA11", "atB"] + [f"o{m}" for m in range(8)] + ["mean2", "var2", "gate", "routT"]
        + [f"in{m}" for m in range(8)] + [f"{x}{m}" for m in range(8) for x in ("os", "f")])
BANKS = 4
CREDIT = 1
assert len(USES) % BANKS == 0
TURNS = len(USES) // BANKS
SCALED = ("q", "k", "v", "o", "gate", "in", "out")


def rest(nc, D, h_d, out_d):
    with ExitStack() as ctx:
        def sb(name, shape, dt=F32):
            return ctx.enter_context(nc.sbuf_tensor(name, shape, dt))

        def sem(name):
            return ctx.enter_context(nc.semaphore(name))

        wqk = sb("wqk", [P, 2, KB, QKB * 256], F16)
        wv = sb("wv", [P, 2, KB, 256], F16)
        wo = sb("wo", [P, 2, KB, DIM], F16)
        wf = sb("wf", [P, KB, DIM], F16)
        wg = sb("wg", [P, 2, KB, EXPERTS], F16)
        experts = sb("experts", [4 * EXPERTS, 2, DIM], F16)
        inv = sb("inv", [P, 8])
        fac = sb("fac", [P, 8])
        bias = sb("bias", [P, KB])
        cosT, sinT = sb("cosT", [P, T]), sb("sinT", [P, T])
        ident = sb("ident", [P, P])
        ident16 = sb("ident16", [P, P], F16)
        identb = sb("identb", [P, P], BF16)
        maskA = sb("maskA", [P, P], BF16)
        maskB = sb("maskB", [P, 160], BF16)
        avg = sb("avg", [P, P])
        consts = sb("consts", [P, 8])
        weights_block(nc, D, locals())
        pairs_block(nc, D, h_d, out_d, locals())


def weights_block(nc, D, W):
    with ExitStack() as ctx:
        def sb(name, shape, dt=F32):
            return ctx.enter_context(nc.sbuf_tensor(name, shape, dt))

        def sem(name):
            return ctx.enter_context(nc.semaphore(name))

        raw = sb("raw", [P, KB, 1024])
        raw2 = sb("raw2", [P, KB, 1024])
        rawg = sb("rawg", [P, KB, EXPERTS])
        rawe = sb("rawe", [4 * EXPERTS, 2, DIM])
        emask = sb("emask", [P, 2 * P + P + 160])
        mx = sb("wl_largest", [P, 8])
        mxa = sb("wl_largest_all", [P, 8])
        scale = sb("scale", [P, 8])
        ehi = sb("ehi", [4 * EXPERTS, 2, DIM], F16)
        elo = sb("elo", [4 * EXPERTS, 2, DIM], F16)
        wqk, wv, wo, wf, wg, experts, inv, fac = (W[n] for n in ("wqk", "wv", "wo", "wf", "wg", "experts", "inv", "fac"))
        consts = W["consts"]
        ld_c, ld_a, ld_b, ld_e = sem("wl_const"), sem("wl_raw"), sem("wl_raw2"), sem("wl_experts")
        chain, mx_ready, all_ready = sem("wl_chain"), sem("wl_mx"), sem("wl_all")
        sc_ready, hi_ready, lo_ready, sign_ready = sem("wl_scale"), sem("wl_hi"), sem("wl_lo"), sem("wl_sign")
        block = ctx.enter_context(nc.Block())
        raw_t = {"q": (raw, 1024), "k": (raw2, 256), "v": (raw2, 256), "o": (raw, 1024)}

        @block.sync
        def _(sp):
            sp.dma_start(raw[:, :, :], D["wq"]).then_inc(ld_a, 16)
            sp.dma_start(raw2[:, :, 0:256], D["wk"]).then_inc(ld_b, 16)
            sp.dma_start(raw2[:, :, 256:512], D["wv"]).then_inc(ld_b, 16)
            sp.dma_start(rawg[:, :, :], D["wg"]).then_inc(ld_e, 16)
            sp.dma_start(rawe[:, :, :], D["we"]).then_inc(ld_e, 16)
            sp.dma_start(consts[:, :], D["consts"]).then_inc(ld_e, 16)
            sp.dma_start(emask[:, :], D["masks"]).then_inc(ld_c, 16)
            sp.dma_start(W["cosT"][:, :], D["cos"]).then_inc(ld_c, 16)
            sp.dma_start(W["sinT"][:, :], D["sin"]).then_inc(ld_c, 16)
            sp.dma_start(W["bias"][:, :], D["bias"]).then_inc(ld_c, 16)
            sp.wait_ge(lo_ready, 3)
            sp.dma_start(raw[:, :, :], D["wo"]).then_inc(ld_a, 16)
            sp.dma_start(raw2[:, :, :], D["wf"]).then_inc(ld_b, 16)

        @block.gpsimd
        def _(pool):
            for n, cols in ((1, slice(0, 3)), (2, slice(4, 7)), (3, slice(3, 4))):
                pool.wait_ge(mx_ready, n)
                nc.gpsimd.partition_all_reduce(mxa[:, cols], mx[:, cols], P, bass.bass_isa.ReduceOp.max).then_inc(all_ready, 1)

        @block.scalar
        def _(act):
            def hi(dst, src, k):
                nc.scalar.activation(dst, src, ACT.Copy, scale=scale[:, k:k + 1]).then_inc(hi_ready, 1)

            act.wait_ge(sc_ready, 1)
            hi(wqk[:, 0, :, 0:1024], raw[:, :, :], 0)
            hi(wqk[:, 0, :, 1024:1280], raw2[:, :, 0:256], 1)
            hi(wv[:, 0], raw2[:, :, 256:512], 2)
            act.wait_ge(sc_ready, 2)
            hi(wg[:, 0], rawg[:, :, :], 4)
            for e in range(2):
                nc.scalar.activation(ehi[:, e], rawe[:, e], ACT.Copy, scale=scale[0:32, 5 + e:6 + e]).then_inc(hi_ready, 1)
            act.wait_ge(ld_b, 48)
            nc.scalar.activation(wf[:, :, :], raw2[:, :, :], ACT.Sign).then_inc(sign_ready, 1)
            act.wait_ge(sc_ready, 3)
            hi(wo[:, 0], raw[:, :, :], 3)

        @block.vector
        def _(dve):
            v = nc.vector
            done = [0]

            def link(ins):
                done[0] += 1
                ins.then_inc(chain, 1)
                dve.wait_ge(chain, done[0])

            def largest(k, src, rows=slice(0, P)):
                return v.tensor_reduce(mx[rows, k:k + 1], src, AX.XY if len(src.shape) > 2 else AX.X, ALU.max, apply_absolute_value=True)

            def scales(cols):
                link(v.tensor_scalar(mxa[:, cols], mxa[:, cols], 1e-30, 1e30, ALU.max, ALU.min))
                link(v.tensor_scalar(inv[:, cols].bitcast(I32), mxa[:, cols].bitcast(I32), 0x7F800000, None, ALU.bitwise_and))
                v.tensor_scalar(scale[:, cols].bitcast(I32), inv[:, cols].bitcast(I32), -1.0, float(254 << 23), ALU.mult, ALU.add).then_inc(sc_ready, 1)

            def lo(dst, src, hi_, k, rows=slice(0, P)):
                return v.scalar_tensor_tensor(dst, src, scale[rows, k:k + 1], hi_, ALU.mult, ALU.subtract)

            link(v.memset(mx[:, :], 0.0))
            dve.wait_ge(ld_a, 16)
            link(largest(0, raw[:, :, :]))
            dve.wait_ge(ld_b, 32)
            link(largest(1, raw2[:, :, 0:256]))
            largest(2, raw2[:, :, 256:512]).then_inc(mx_ready, 1)
            dve.wait_ge(ld_e, 48)
            link(largest(4, rawg[:, :, :]))
            link(largest(5, rawe[:, 0], slice(0, 32)))
            largest(6, rawe[:, 1], slice(0, 32)).then_inc(mx_ready, 1)
            dve.wait_ge(all_ready, 1)
            scales(slice(0, 3))
            dve.wait_ge(all_ready, 2)
            scales(slice(4, 7))
            dve.wait_ge(sc_ready, 2)
            link(v.tensor_scalar(fac[:, 0:1], inv[:, 0:1], inv[:, 1:2], float(HD ** -0.5), ALU.mult, ALU.mult))
            link(v.tensor_scalar(fac[:, 2:3], inv[:, 4:5], 1.0 / XS, None, ALU.mult))
            link(v.tensor_scalar(fac[:, 3:4], inv[:, 5:6], inv[:, 6:7], 1.0 / XS, ALU.mult, ALU.mult))
            dve.wait_ge(ld_c, 64)
            v.tensor_copy(W["ident"][:, :], emask[:, 0:P])
            v.tensor_copy(W["ident16"][:, :], emask[:, 0:P])
            v.tensor_copy(W["identb"][:, :], emask[:, 0:P])
            v.tensor_copy(W["avg"][:, :], emask[:, P:2 * P])
            v.tensor_copy(W["maskA"][:, :], emask[:, 2 * P:3 * P])
            v.tensor_copy(W["maskB"][:, :], emask[:, 3 * P:])
            dve.wait_ge(hi_ready, 1)
            lo(wqk[:, 1, :, 0:1024], raw[:, :, :], wqk[:, 0, :, 0:1024], 0).then_inc(lo_ready, 1)
            dve.wait_ge(hi_ready, 2)
            lo(wqk[:, 1, :, 1024:1280], raw2[:, :, 0:256], wqk[:, 0, :, 1024:1280], 1).then_inc(lo_ready, 1)
            dve.wait_ge(hi_ready, 3)
            lo(wv[:, 1], raw2[:, :, 256:512], wv[:, 0], 2).then_inc(lo_ready, 1)
            dve.wait_ge(hi_ready, 4)
            link(lo(wg[:, 1], rawg[:, :, :], wg[:, 0], 4))
            dve.wait_ge(hi_ready, 6)
            for e in range(2):
                link(lo(elo[:, e], rawe[:, e], ehi[:, e], 5 + e, slice(0, 32)))
            link(v.tensor_scalar(elo[:, :, :], elo[:, :, :], consts[0:32, 2:3], None, ALU.mult))
            link(v.scalar_tensor_tensor(experts[:, :, :], ehi[:, :, :], consts[0:32, 1:2], elo[:, :, :], ALU.mult, ALU.add))
            dve.wait_ge(ld_a, 32)
            largest(3, raw[:, :, :]).then_inc(mx_ready, 1)
            dve.wait_ge(all_ready, 3)
            scales(slice(3, 4))
            dve.wait_ge(sc_ready, 3)
            link(v.tensor_scalar(fac[:, 1:2], inv[:, 2:3], inv[:, 3:4], None, ALU.mult))
            dve.wait_ge(hi_ready, 7)
            link(lo(wo[:, 1], raw[:, :, :], wo[:, 0], 3))
            dve.wait_ge(sign_ready, 1)

        @block.tensor
        def _(pe):
            pass


def pairs_block(nc, D, h_d, out_d, W):
    with ExitStack() as ctx:
        def sb(name, shape, dt=F32):
            return ctx.enter_context(nc.sbuf_tensor(name, shape, dt))

        def sem(name):
            return ctx.enter_context(nc.semaphore(name))

        wqk, wv, wo, wf, wg, experts, fac, bias = (W[n] for n in ("wqk", "wv", "wo", "wf", "wg", "experts", "fac", "bias"))
        cosT, sinT, ident, ident16, identb, maskA, maskB, avg, consts = (
            W[n] for n in ("cosT", "sinT", "ident", "ident16", "identb", "maskA", "maskB", "avg", "consts"))
        xc = sb("xc", [P, KB, T])
        x1 = sb("x1", [P, 2, KB, T], F16)
        x2 = sb("x2", [P, 2, KB, T], F16)
        x1sq = x1[:, :, :, :].rearrange("p a k t -> p (a k t)").bitcast(F32).rearrange("p (k t) -> p k t", k=KB)
        x2sq = x2[:, :, :, :].rearrange("p a k t -> p (a k t)").bitcast(F32).rearrange("p (k t) -> p k t", k=KB)
        h2 = sb("h2", [P, KB, T])
        qs = sb("qs", [P, NQ, T], F16)
        ks = sb("ks", [P, NKV, T], F16)
        rt = sb("rt", [P, 2, 2, 2, T], F16)
        pf = sb("pf", [P, 3, 512])
        ph = sb("ph", [P, 2, 3, 512], F16)
        prod = pf[:, :, :].rearrange("p a c -> p (a c)")[:, 0:4 * T].rearrange("p (a t) -> p a t", a=4)
        rot = ph[:, :, :, :].rearrange("p a b c -> p (a b c)").bitcast(F32)[:, 0:4 * T].rearrange("p (s a t) -> p s a t", s=2, a=2)
        vv = sb("vv", [P, 2, 3, NKV, HD + 1], F16)
        att = sb("att", [P, 10, NKV, HD])
        qb = att[:, :, :, :].rearrange("p n k d -> p (n k d)").bitcast(F16)[:, 0:64 * NQ].rearrange("p (b h q) -> p b h q", b=2, h=NQ)
        mxa = sb("mxa", [P, 2, NKV, 4])
        mxb = sb("mxb", [P, 2, NKV])
        rsum = sb("rsum", [P, 10])
        mt = rt[0:NQ, :, :, :, :].rearrange("p a b c t -> p (a b c t)")[:, 0:1024].rearrange("p (a c) -> p a c", a=2)
        sums = sb("sums", [P, T])
        rstd = sb("rstd", [P, T])
        nt = sb("nt", [P, T])
        gl = sb("gl", [P, 3, EXPERTS])
        g1 = sb("g1_", [P, 3, 1])
        rr = sb("rr", [P, 3, 4, EXPERTS], F16)
        rT = sb("rT", [4 * EXPERTS, T], F16)
        os_ = sb("os_", [P, 2, T])

        pj = [ctx.enter_context(nc.psum_tensor(f"pj{b}", [P, 512], F32)) for b in range(BANKS)]
        sa = [ctx.enter_context(nc.psum_tensor(f"sa{b}", [P, 512], F32)) for b in range(3)]
        po = ctx.enter_context(nc.psum_tensor("po", [P, 512], F32))

        h_loaded, res_loaded, stored = sem("h_loaded"), sem("res_loaded"), sem("stored")
        stacked = [sem(f"stacked{j}") for j in range(QKB)]
        rows_loaded = sem("rows_loaded")
        pj_full = [sem(f"pj_full{b}") for b in range(BANKS)]
        pj_free = [sem(f"pj_free{b}") for b in range(BANKS)]
        sa_full = [sem(f"sa_full{b}") for b in range(3)]
        sa_free = [sem(f"sa_free{b}") for b in range(3)]
        po_full, po_free = sem("po_full"), sem("po_free")
        dchain, achain = sem("dchain"), sem("achain")
        init = sem("init")
        sum_ready, squared, rough = sem("sum_ready"), sem("squared"), sem("rough")
        norm_ready, hi_made, x_ready = sem("norm_ready"), sem("hi_made"), sem("x_ready")
        rot_ready, rot_hi, rope_ready = sem("rot_ready"), sem("rot_hi"), sem("rope_ready")
        v_hi, qb_ready = sem("v_hi"), sem("qb_ready")
        exp_ready, kept, split_hi, split_ready, split_used = sem("exp_ready"), sem("kept"), sem("split_hi"), sem("split_ready"), sem("split_used")
        at_hi = sem("at_hi")
        gexp_in, gexp_out, rout_ready = sem("gexp_in"), sem("gexp_out"), sem("rout_ready")
        y_hi, y_ready = sem("y_hi"), sem("y_ready")
        f_done = sem("f_done")
        block = ctx.enter_context(nc.Block())

        def use(name, p):
            n = USES.index(name)
            return n % BANKS, p * TURNS + n // BANKS + 1, p * TURNS + n // BANKS + CREDIT

        def full(eng, name, p):
            b, value, _ = use(name, p)
            eng.wait_ge(pj_full[b], value)
            return pj[b]

        def read(eng, name, p):
            b, value, _ = use(name, p)
            eng.wait_ge(pj_free[b], value + CREDIT)

        def free(name):
            return pj_free[USES.index(name) % BANKS]

        BB = [slice(256, 288), slice(288, 320)]
        AB = [A0, A1]

        @block.sync
        def _(sp):
            with sp.Fori(0, NPAIR) as p:
                sp.wait_ge(y_ready, KB * p + CREDIT)
                sp.dma_start(xc[:, :, 0:256], h_d[p, :, :, :, :].rearrange("j i b h -> j i (b h)")).then_inc(h_loaded, 16)
                sp.dma_start(xc[:, :, 256:320], D["txt"][p, :, :, :]).then_inc(h_loaded, 16)
                sp.wait_ge(stored, 16 * p + CREDIT)
                sp.dma_start(h2[:, :, 0:256], h_d[p, :, :, :, :].rearrange("j i b h -> j i (b h)")).then_inc(res_loaded, 16)
                sp.dma_start(h2[:, :, 256:320], D["txt"][p, :, :, :]).then_inc(res_loaded, 16)
                for n, j in enumerate((4, 0, 1, 2, 3)):
                    sp.wait_ge(rope_ready, QKB * p + n + 1)
                    parts = (0, 1, 0) if j == 4 else (0, 0, 1)
                    for g, hl in enumerate(parts):
                        for ab in range(2):
                            r = 32 * g + 16 * ab
                            dst = ks[r:r + 16, :, :] if j == 4 else qs[r:r + 16, 8 * j:8 * j + 8, :]
                            sp.dma_start(dst, rt[:, n % 2, ab, hl, :]).then_inc(stacked[n], 16)
                read(sp, "maxT", p)
                for hl in range(2):
                    sp.dma_start(qs[96 + hl:97 + hl, :, 0:256], mt[:, hl, 0:256]).then_inc(rows_loaded, 16)
                    for b in range(2):
                        sp.dma_start(qs[96 + hl:97 + hl, :, BB[b]].rearrange("p (k h) q -> p k h q", h=4),
                                     mt[0:NKV, hl, 256 + 128 * b:384 + 128 * b].rearrange("p (h q) -> p h q", h=4)).then_inc(rows_loaded, 16)
                sp.wait_ge(f_done, KB * (p + 1))
                sp.dma_start(out_d[p, :, :, :], h2[:, :, :]).then_inc(stored, 16)
            sp.wait_ge(stored, 16 * NPAIR + CREDIT)

        @block.tensor
        def _(pe):
            mm = nc.tensor.matmul

            def bank(name, p):
                b, _, value = use(name, p)
                pe.wait_ge(pj_free[b], value)
                return pj[b], pj_full[b]

            def split_product(out, w_hi, w_lo, x, cols=slice(0, T)):
                for k in range(KB):
                    mm(out, w_hi(k), x[:, 0, k, cols], start=(k == 0), stop=False)
                    mm(out, w_hi(k), x[:, 1, k, cols], start=False, stop=False)
                    last = mm(out, w_lo(k), x[:, 0, k, cols], start=False, stop=(k == KB - 1))
                return last

            def average(name, p, n):
                ps, f = bank(name, p)
                pe.wait_ge(sum_ready, 4 * p + n)
                mm(ps[:, 0:T], avg[:, :], sums[:, :], start=True, stop=True).then_inc(f, 1)

            pe.wait_ge(init, 2)
            with pe.Fori(0, NPAIR) as p:
                average("mean1", p, 1)
                average("var1", p, 2)
                pe.wait_ge(x_ready, 2 * p + 1)
                for j in (4, 0, 1, 2, 3):
                    for a in range(2):
                        ps, f = bank(f"qk{j}{'ab'[a]}", p)
                        c = slice(256 * j + 128 * a, 256 * j + 128 * a + 128)
                        split_product(ps[:, 0:T], lambda k: wqk[:, 0, k, c], lambda k: wqk[:, 1, k, c], x1).then_inc(f, 1)
                ps, f = bank("v01", p)
                for t, cols in enumerate((A0, A1, slice(192, 320))):
                    if t == 2:
                        ps, f = bank("v2", p)
                    o = ps[:, 256 * (t % 2):256 * (t % 2) + 256]
                    for k in range(KB):
                        mm(o, x1[:, 0, k, cols], wv[:, 0, k, :], start=(k == 0), stop=False)
                        mm(o, x1[:, 0, k, cols], wv[:, 1, k, :], start=False, stop=False)
                        last = mm(o, x1[:, 1, k, cols], wv[:, 0, k, :], start=False, stop=(k == KB - 1))
                    if t >= 1:
                        last.then_inc(f, 1)
                for kv in range(NKV):
                    if kv % 2 == 0:
                        pe.wait_ge(stacked[kv // 2 + 1], 96 * (p + 1) + CREDIT)
                        pe.wait_ge(qb_ready, 4 * p + kv // 2 + 1)
                    if kv == 0:
                        pe.wait_ge(stacked[0], 96 * (p + 1) + CREDIT)
                    for b in range(2):
                        pe.wait_ge(sa_free[b], 16 * p + kv + CREDIT)
                        s = sa[b][:, :].rearrange("p (h k) -> p h k", h=4)
                        mm(s, identb[:, :], maskA[:, :].unsqueeze(1).broadcast_to([P, 4, P]), start=True, stop=False, skip_group_check=True)
                        for h in range(4):
                            last = mm(s[:, h, :], qs[0:96, 4 * kv + h, AB[b]], ks[0:96, kv, AB[b]], start=False, stop=(h == 3), skip_group_check=True)
                        last.then_inc(sa_full[b], 1)
                    pe.wait_ge(sa_free[2], 16 * p + kv + CREDIT)
                    s = sa[2][:, 0:320].rearrange("p (b k) -> p b k", b=2)
                    mm(s, identb[:, :], maskB[:, :].unsqueeze(1).broadcast_to([P, 2, 160]), start=True, stop=False, skip_group_check=True)
                    for b in range(2):
                        q = qb[0:96, b, 4 * kv:4 * kv + 4, :].rearrange("p h q -> p (h q)")
                        mm(s[:, b, 0:128], q, ks[0:96, kv, AB[b]], start=False, stop=False, skip_group_check=True)
                        last = mm(s[:, b, 128:160], q, ks[0:96, kv, BB[b]], start=False, stop=(b == 1), skip_group_check=True)
                    last.then_inc(sa_full[2], 1)
                ps, f = bank("maxT", p)
                for r in range(3):
                    pe.wait_ge(sa_free[r], 16 * p + NKV + CREDIT)
                for b in range(2):
                    nc.tensor.transpose(ps[0:NQ, 128 * b:128 * b + 128], mxa[:, b].rearrange("p k h -> p (k h)"), ident[:, :])
                for b in range(2):
                    last = nc.tensor.transpose(ps[0:NKV, 256 + 128 * b:384 + 128 * b], mxb[:, b, :], ident[:, :])
                last.then_inc(f, 1)

                def scores(kv):
                    for b in range(2):
                        pe.wait_ge(sa_free[b], 16 * p + 8 + kv + CREDIT)
                        mm(sa[b][:, :].rearrange("p (h q) -> p h q", h=4), ks[0:98, kv, AB[b]], qs[0:98, 4 * kv:4 * kv + 4, AB[b]],
                           start=True, stop=True).then_inc(sa_full[b], 1)
                    pe.wait_ge(sa_free[2], 16 * p + 8 + kv + CREDIT)
                    for b in range(2):
                        mm(sa[2][:, 128 * b:128 * b + 128].rearrange("p (h q) -> p h q", h=4), ks[0:98, kv, AB[b]],
                           qs[0:98, 4 * kv:4 * kv + 4, BB[b]], start=True, stop=True)
                    mm(sa[2][:, 256:512].rearrange("p (b h q) -> p b h q", b=2, h=4), ks[0:98, kv, 192:320],
                       qs[0:98, 4 * kv:4 * kv + 4, BT].rearrange("p h (b q) -> p b h q", b=2), start=True, stop=True).then_inc(sa_full[2], 1)

                def values(kv):
                    pe.wait_ge(po_free, NKV * p + kv + CREDIT)
                    o = po[:, 0:330].rearrange("p (n d) -> p n d", n=10)

                    def weighted(n, terms):
                        for i, (sl, c, t) in enumerate(terms):
                            c = slice(c, c + 128)
                            mm(o[:, n, :], ph[:, 0, sl, c], vv[:, 0, t, kv, :], start=(i == 0), stop=False)
                            mm(o[:, n, :], ph[:, 0, sl, c], vv[:, 1, t, kv, :], start=False, stop=False)
                            last = mm(o[:, n, :], ph[:, 1, sl, c], vv[:, 0, t, kv, :], start=False, stop=(i == len(terms) - 1))
                        return last

                    for b in range(2):
                        pe.wait_ge(split_ready, 3 * (NKV * p + kv) + b + 1)
                        for h in range(4):
                            last = weighted(4 * b + h, [(b, 128 * h, b)])
                        last.then_inc(split_used, 1)
                    pe.wait_ge(split_ready, 3 * (NKV * p + kv) + 3)
                    for b in range(2):
                        last = weighted(8 + b, [(2, 128 * b, b), (2, 256 + 128 * b, 2)])
                    last.then_inc(po_full, 1)

                pe.wait_ge(rows_loaded, 96 * (p + 1))
                read(pe, "v01", p)
                read(pe, "v2", p)
                scores(0)
                for kv in range(NKV):
                    if kv + 1 < NKV:
                        scores(kv + 1)
                    values(kv)
                pe.wait_ge(po_free, NKV * (p + 1) + CREDIT)
                for kh in range(2):
                    for b in range(2):
                        ps, f = bank(f"atA{kh}{b}", p)
                        for h in range(4):
                            last = nc.tensor.transpose(ps[:, 128 * h:128 * h + 128], att[:, 4 * b + h, 4 * kh:4 * kh + 4, :].rearrange("p k d -> p (k d)"), ident[:, :])
                        last.then_inc(f, 1)
                ps, f = bank("atB", p)
                for kh in range(2):
                    for b in range(2):
                        last = nc.tensor.transpose(ps[:, 256 * kh + 128 * b:256 * kh + 128 * b + 128], att[:, 8 + b, 4 * kh:4 * kh + 4, :].rearrange("p k d -> p (k d)"), ident[:, :])
                last.then_inc(f, 1)
                read(pe, "atB", p)
                for m in range(KB):
                    ps, f = bank(f"o{m}", p)
                    c = slice(128 * m, 128 * m + 128)
                    split_product(ps[:, 0:T], lambda k: wo[:, 0, k, c], lambda k: wo[:, 1, k, c], x2).then_inc(f, 1)
                average("mean2", p, 3)
                average("var2", p, 4)
                pe.wait_ge(x_ready, 2 * p + 2)
                ps, f = bank("gate", p)
                for t, cols in enumerate((A0, A1, BT)):
                    n = 64 if t == 2 else P
                    o = ps[0:n, 8 * t:8 * t + 8]
                    for k in range(KB):
                        mm(o, x2[:, 0, k, cols], wg[:, 0, k, :], start=(k == 0), stop=False)
                        mm(o, x2[:, 0, k, cols], wg[:, 1, k, :], start=False, stop=False)
                        last = mm(o, x2[:, 1, k, cols], wg[:, 0, k, :], start=False, stop=(k == KB - 1))
                last.then_inc(f, 1)
                ps, f = bank("routT", p)
                pe.wait_ge(rout_ready, p + 1)
                pt = ps[0:32, 0:160].bitcast(F16)
                for t, cols in enumerate((A0, A1, BT)):
                    n = 64 if t == 2 else P
                    last = nc.tensor.transpose(pt[:, cols], rr[0:n, t, :, :].rearrange("p a e -> p (a e)"), ident16[0:n, 0:n])
                last.then_inc(f, 1)
                read(pe, "routT", p)
                for m in range(KB):
                    ps, f = bank(f"in{m}", p)
                    mm(ps[:, 0:T], experts[:, 0, 128 * m:128 * m + 128], rT[:, :], start=True, stop=True).then_inc(f, 1)
                for m in range(KB):
                    c = slice(128 * m, 128 * m + 128)
                    ps, f = bank(f"os{m}", p)
                    mm(ps[:, 0:T], experts[:, 1, c], rT[:, :], start=True, stop=True).then_inc(f, 1)
                    ps, f = bank(f"f{m}", p)
                    if m == 0:
                        pe.wait_ge(y_ready, KB * (p + 1) + CREDIT)
                    for k in range(KB):
                        mm(ps[:, 0:T], wf[:, k, c], x2[:, 0, k, :], start=(k == 0), stop=False)
                        last = mm(ps[:, 0:T], wf[:, k, c], x2[:, 1, k, :], start=False, stop=(k == KB - 1))
                    last.then_inc(f, 1)

        @block.scalar
        def _(act):
            A = nc.scalar.activation
            nc.scalar.preload_act_table_set("natural_log_exp_and_others")
            with act.Fori(0, NPAIR) as p:
                n_own = [0]

                def own(ins):
                    n_own[0] += 1
                    ins.then_inc(achain, 1)
                    act.wait_ge(achain, 2 * p + n_own[0])

                def norm(i, sq, dst):
                    read(act, f"mean{i}", p)
                    A(sq, xc[:, :, :], ACT.Square).then_inc(squared, 1)
                    ps = full(act, f"var{i}", p)
                    own(A(rstd[:, :], ps[:, 0:T], ACT.Ln, bias=consts[:, 0:1]))
                    A(rstd[:, :], rstd[:, :], ACT.Exp, scale=-0.5).then_inc(rough, 1)
                    act.wait_ge(norm_ready, 2 * p + i)
                    A(dst, xc[:, :, :], ACT.Copy).then_inc(hi_made, 1)

                norm(1, x1sq, x1[:, 0])
                for n, j in enumerate((4, 0, 1, 2, 3)):
                    act.wait_ge(rot_ready, QKB * p + n + 1)
                    if n >= 2:
                        act.wait_ge(stacked[n - 2], 96 * (p + 1) + CREDIT)
                    else:
                        act.wait_ge(stacked[4 - n], 96 * p + CREDIT)
                    A(rt[:, n % 2, :, 0, :], rot[:, n % 2], ACT.Copy).then_inc(rot_hi, 1)
                for t in range(3):
                    if t != 1:
                        ps = full(act, "v01" if t < 2 else "v2", p)
                    A(vv[:, 0, t, :, 0:HD], ps[:, 256 * (t % 2):256 * (t % 2) + 256].rearrange("p (k d) -> p k d", k=NKV),
                      ACT.Copy, scale=1.0 / XS).then_inc(v_hi, 1)
                for kv in range(NKV):
                    for r in range(3):
                        c = 3 * kv + r
                        act.wait_ge(sa_full[r], 16 * p + 8 + kv + 1)
                        if kv >= 1:
                            act.wait_ge(split_ready, 24 * p + c - 2)
                        A(pf[:, r, :], sa[r][:, :], ACT.Exp, scale=fac[:, 0:1]).then_inc(sa_free[r], 1)
                for kh in range(2):
                    for b in range(2):
                        ps = full(act, f"atA{kh}{b}", p)
                        A(x2[:, 0, 4 * kh:4 * kh + 4, AB[b]], ps[:, :].rearrange("p (h q) -> p h q", h=4), ACT.Copy).then_inc(at_hi, 1)
                ps = full(act, "atB", p)
                for kh in range(2):
                    A(x2[:, 0, 4 * kh:4 * kh + 4, BT].rearrange("p h (b q) -> p b h q", b=2),
                      ps[:, 256 * kh:256 * kh + 256].rearrange("p (b h q) -> p b h q", b=2, h=4), ACT.Copy).then_inc(at_hi, 1)
                norm(2, x2sq, x2[:, 0])
                act.wait_ge(gexp_in, p + 1)
                A(gl[:, :, :], gl[:, :, :], ACT.Exp, scale=fac[:, 2:3]).then_inc(gexp_out, 1)
                for m in range(KB):
                    read(act, f"in{m}", p)
                    A(x2[:, 0, m, :], xc[:, m, :], ACT.Copy).then_inc(y_hi, 1)
                for m in range(KB):
                    ps = full(act, f"os{m}", p)
                    if m >= 2:
                        act.wait_ge(f_done, KB * p + m - 1)
                    A(os_[:, m % 2, :], ps[:, 0:T], ACT.Copy, scale=fac[:, 3:4]).then_inc(free(f"os{m}"), 1)
                assert n_own[0] == 2

        @block.gpsimd
        def _(pool):
            g = nc.gpsimd
            for s in (*pj_free, *sa_free, po_free, stored, y_ready, *stacked):
                pool.sem_inc(s, CREDIT)
            g.memset(ks[96:98, :, :], SHIFT).then_inc(init, 1)
            pool.wait_ge(init, 1)
            g.memset(vv[:, 1], 0.0)
            g.memset(vv[:, 0, :, :, HD:HD + 1], 1.0).then_inc(init, 1)
            with pool.Fori(0, NPAIR) as p:
                for kv in range(NKV):
                    exps_done = pool.to_reg(16 * p + 8 + kv + 1 + CREDIT)
                    first_select = pool.to_reg(32 * p + 4 * kv + 3)
                    for r in range(3):
                        pool.wait_ge(init, 2)
                        pool.wait_ge(sa_free[r], exps_done)
                        if r < 2:
                            s = pf[:, r, :].rearrange("p (h q) -> p h q", h=4)
                            g.affine_select(out=s, in_=s, compare_op=ALU.is_ge, fill=0.0, base=0, pattern=[[0, 4], [1, 128]],
                                            channel_multiplier=-1).then_inc(kept, 1)
                        else:
                            s = pf[:, 2, 256:512].rearrange("p (b h q) -> p b h q", b=2, h=4)
                            g.affine_select(out=s, in_=s, compare_op=ALU.is_ge, fill=0.0, base=64, pattern=[[32, 2], [0, 4], [1, 32]],
                                            channel_multiplier=-1).then_inc(kept, 1)
                            pool.wait_ge(init, 2)
                            pool.wait_ge(kept, first_select)
                            g.affine_select(out=s, in_=s, compare_op=ALU.is_ge, fill=0.0, base=-64, pattern=[[-32, 2], [0, 4], [0, 32]],
                                            channel_multiplier=1).then_inc(kept, 1)

        @block.vector
        def _(dve):
            v = nc.vector
            OWN = 29
            v.memset(gl[:, :, :], 0.0)
            with dve.Fori(0, NPAIR) as p:
                n_own = [0]

                def own(ins):
                    n_own[0] += 1
                    ins.then_inc(dchain, 1)
                    dve.wait_ge(dchain, OWN * p + n_own[0])

                def norm(i, src, sq, dst):
                    v.tensor_reduce(sums[:, :], src[:, :, :].rearrange("p k t -> p t k"), AX.X, ALU.add).then_inc(sum_ready, 1)
                    ps = full(dve, f"mean{i}", p)
                    v.tensor_tensor(xc[:, :, :], src[:, :, :], ps[:, 0:T].unsqueeze(1).broadcast_to([P, KB, T]),
                                    ALU.subtract).then_inc(free(f"mean{i}"), 1)
                    dve.wait_ge(squared, 2 * p + i)
                    v.tensor_reduce(sums[:, :], sq.rearrange("p k t -> p t k"), AX.X, ALU.add).then_inc(sum_ready, 1)
                    ps = full(dve, f"var{i}", p)
                    dve.wait_ge(rough, 2 * p + i)
                    own(v.tensor_tensor(sums[:, :], rstd[:, :], rstd[:, :], ALU.mult))
                    v.scalar_tensor_tensor(nt[:, :], ps[:, 0:T], EPS, sums[:, :], ALU.add, ALU.mult).then_inc(free(f"var{i}"), 1)
                    read(dve, f"var{i}", p)
                    own(v.tensor_scalar(nt[:, :], nt[:, :], -0.5, 1.5, ALU.mult, ALU.add))
                    own(v.tensor_tensor(rstd[:, :], rstd[:, :], nt[:, :], ALU.mult))
                    v.scalar_tensor_tensor(xc[:, :, :], xc[:, :, :], XS, rstd[:, :].unsqueeze(1).broadcast_to([P, KB, T]),
                                           ALU.mult, ALU.mult).then_inc(norm_ready, 1)
                    dve.wait_ge(hi_made, 2 * p + i)
                    v.tensor_tensor(dst[:, 1], xc[:, :, :], dst[:, 0], ALU.subtract).then_inc(x_ready, 1)

                dve.wait_ge(h_loaded, 32 * (p + 1))
                norm(1, xc, x1sq, x1)

                def rope_lo(n):
                    dve.wait_ge(rot_hi, QKB * p + n + 1)
                    v.tensor_tensor(rt[:, n % 2, :, 1, :], rot[:, n % 2], rt[:, n % 2, :, 0, :], ALU.subtract).then_inc(rope_ready, 1)

                for n, j in enumerate((4, 0, 1, 2, 3)):
                    pa = full(dve, f"qk{j}a", p)
                    if n >= 1:
                        dve.wait_ge(rot_ready, QKB * p + n)
                    v.tensor_tensor(prod[:, 0], pa[:, 0:T], cosT[:, :], ALU.mult)
                    v.tensor_tensor(prod[:, 2], pa[:, 0:T], sinT[:, :], ALU.mult).then_inc(free(f"qk{j}a"), 1)
                    pb = full(dve, f"qk{j}b", p)
                    v.tensor_tensor(prod[:, 1], pb[:, 0:T], sinT[:, :], ALU.mult)
                    v.tensor_tensor(prod[:, 3], pb[:, 0:T], cosT[:, :], ALU.mult).then_inc(free(f"qk{j}b"), 1)
                    read(dve, f"qk{j}b", p)
                    own(v.tensor_tensor(rot[:, n % 2, 0], prod[:, 0], prod[:, 1], ALU.subtract))
                    v.tensor_tensor(rot[:, n % 2, 1], prod[:, 2], prod[:, 3], ALU.add).then_inc(rot_ready, 1)
                    if n >= 1:
                        rope_lo(n - 1)
                rope_lo(4)
                for t in range(3):
                    if t != 1:
                        ps = full(dve, "v01" if t < 2 else "v2", p)
                    dve.wait_ge(v_hi, 3 * p + (2 if t < 2 else 3))
                    lo = v.scalar_tensor_tensor(vv[:, 1, t, :, 0:HD], ps[:, 256 * (t % 2):256 * (t % 2) + 256].rearrange("p (k d) -> p k d", k=NKV),
                                                  1.0 / XS, vv[:, 0, t, :, 0:HD], ALU.mult, ALU.subtract)
                    if t >= 1:
                        lo.then_inc(free("v01" if t == 1 else "v2"), 1)
                for j in range(4):
                    dve.wait_ge(stacked[j + 1], 96 * (p + 1) + CREDIT)
                    v.tensor_copy(qb[0:96, :, 8 * j:8 * j + 8, :], qs[0:96, 8 * j:8 * j + 8, BT].rearrange("p h (b q) -> p b h q", b=2)).then_inc(qb_ready, 1)
                for kv in range(NKV):
                    for b in range(2):
                        dve.wait_ge(sa_full[b], 16 * p + kv + 1)
                        v.tensor_reduce(mxa[:, b, kv, :], sa[b][:, :].rearrange("p (h k) -> p h k", h=4), AX.X, ALU.max).then_inc(sa_free[b], 1)
                    dve.wait_ge(sa_full[2], 16 * p + kv + 1)
                    v.tensor_reduce(mxb[:, :, kv], sa[2][:, 0:320].rearrange("p (b k) -> p b k", b=2), AX.X, ALU.max).then_inc(sa_free[2], 1)
                ps = full(dve, "maxT", p)
                areas = ((NQ, slice(0, 256)), (NKV, slice(256, 512)))
                for rows, cols in areas:
                    own(v.tensor_scalar(mt[0:rows, 0, cols], ps[0:rows, cols], -1.0 / SHIFT, None, ALU.mult))
                for rows, cols in areas:
                    lo = v.scalar_tensor_tensor(mt[0:rows, 1, cols], ps[0:rows, cols], -1.0 / SHIFT, mt[0:rows, 0, cols], ALU.mult, ALU.subtract)
                lo.then_inc(free("maxT"), 1)

                def attention_out(kv):
                    dve.wait_ge(po_full, NKV * p + kv + 1)
                    o = po[:, 0:330].rearrange("p (n d) -> p n d", n=10)
                    own(v.reciprocal(rsum[:, :].unsqueeze(2), o[:, :, HD:HD + 1]))
                    v.tensor_tensor(att[:, :, kv, :], o[:, :, 0:HD], rsum[:, :].unsqueeze(2).broadcast_to([P, 10, HD]), ALU.mult).then_inc(po_free, 1)

                for kv in range(NKV):
                    for r in range(3):
                        c = 3 * kv + r
                        dve.wait_ge(kept, 32 * p + 4 * kv + (r + 1 if r < 2 else 4))
                        if kv >= 1:
                            if r < 2:
                                dve.wait_ge(split_used, 16 * p + 2 * (kv - 1) + r + 1)
                            else:
                                dve.wait_ge(po_full, NKV * p + kv)
                        v.tensor_copy(ph[:, 0, r, :], pf[:, r, :]).then_inc(split_hi, 1)
                        dve.wait_ge(split_hi, 24 * p + c + 1)
                        v.tensor_tensor(ph[:, 1, r, :], pf[:, r, :], ph[:, 0, r, :], ALU.subtract).then_inc(split_ready, 1)
                    if kv >= 1:
                        attention_out(kv - 1)
                attention_out(NKV - 1)
                for n, (kh, b) in enumerate(((0, 0), (0, 1), (1, 0), (1, 1))):
                    ps = full(dve, f"atA{kh}{b}", p)
                    dve.wait_ge(at_hi, 6 * p + n + 1)
                    v.tensor_tensor(x2[:, 1, 4 * kh:4 * kh + 4, AB[b]], ps[:, :].rearrange("p (h q) -> p h q", h=4),
                                    x2[:, 0, 4 * kh:4 * kh + 4, AB[b]], ALU.subtract).then_inc(free(f"atA{kh}{b}"), 1)
                ps = full(dve, "atB", p)
                dve.wait_ge(at_hi, 6 * (p + 1))
                for kh in range(2):
                    lo = v.tensor_tensor(x2[:, 1, 4 * kh:4 * kh + 4, BT].rearrange("p h (b q) -> p b h q", b=2),
                                         ps[:, 256 * kh:256 * kh + 256].rearrange("p (b h q) -> p b h q", b=2, h=4),
                                         x2[:, 0, 4 * kh:4 * kh + 4, BT].rearrange("p h (b q) -> p b h q", b=2), ALU.subtract)
                lo.then_inc(free("atB"), 1)
                dve.wait_ge(res_loaded, 32 * (p + 1))
                for m in range(KB):
                    ps = full(dve, f"o{m}", p)
                    v.scalar_tensor_tensor(h2[:, m, :], ps[:, 0:T], fac[:, 1:2], h2[:, m, :], ALU.mult, ALU.add).then_inc(free(f"o{m}"), 1)
                read(dve, "o7", p)
                norm(2, h2, x2sq, x2)
                ps = full(dve, "gate", p)
                own(v.tensor_copy(gl[:, 0:2, :], ps[:, 0:16].rearrange("p (t e) -> p t e", t=2)))
                v.tensor_copy(gl[0:64, 2, :], ps[0:64, 16:24]).then_inc(free("gate"), 1)
                read(dve, "gate", p)
                own(v.tensor_reduce(g1[:, :, :], gl[:, :, :], AX.X, ALU.max))
                v.tensor_tensor(gl[:, :, :], gl[:, :, :], g1[:, :, :].broadcast_to([P, 3, EXPERTS]), ALU.subtract).then_inc(gexp_in, 1)
                dve.wait_ge(gexp_out, p + 1)
                own(v.tensor_reduce(g1[:, :, :], gl[:, :, :], AX.X, ALU.add))
                own(v.reciprocal(g1[:, :, :], g1[:, :, :]))
                own(v.tensor_tensor(gl[:, :, :], gl[:, :, :], g1[:, :, :].broadcast_to([P, 3, EXPERTS]), ALU.mult))
                own(v.tensor_copy(rr[:, :, 0, :], gl[:, :, :]))
                own(v.tensor_copy(rr[:, :, 2, :], gl[:, :, :]))
                own(v.tensor_tensor(rr[:, :, 1, :], gl[:, :, :], rr[:, :, 0, :], ALU.subtract))
                v.tensor_tensor(rr[:, :, 3, :], gl[:, :, :], rr[:, :, 0, :], ALU.subtract).then_inc(rout_ready, 1)
                ps = full(dve, "routT", p)
                v.tensor_copy(rT[:, :], ps[0:32, 0:160].bitcast(F16)).then_inc(free("routT"), 1)

                def y_lo(m):
                    dve.wait_ge(y_hi, KB * p + m + 1)
                    v.tensor_tensor(x2[:, 1, m, :], xc[:, m, :], x2[:, 0, m, :], ALU.subtract).then_inc(y_ready, 1)

                for m in range(KB):
                    ps = full(dve, f"in{m}", p)
                    v.tensor_tensor(xc[:, m, :], ps[:, 0:T], xc[:, m, :], ALU.mult).then_inc(free(f"in{m}"), 1)
                    if m >= 1:
                        y_lo(m - 1)
                y_lo(KB - 1)
                for m in range(KB):
                    read(dve, f"os{m}", p)
                    ps = full(dve, f"f{m}", p)
                    v.tensor_tensor(os_[:, m % 2, :], ps[:, 0:T], os_[:, m % 2, :], ALU.mult).then_inc(free(f"f{m}"), 1)
                    read(dve, f"f{m}", p)
                    v.scalar_tensor_tensor(h2[:, m, :], os_[:, m % 2, :], bias[:, m:m + 1], h2[:, m, :], ALU.add, ALU.add).then_inc(f_done, 1)
                assert n_own[0] == OWN, n_own[0]


def fusion_kernel(nc, D, out_d):
    h_d = nc.dram_tensor("tok_result", (NPAIR, P, IH, 2, HEADS), F32, kind="Internal").ap()
    s4d_block(nc, D["par"], D["xr"], D["xi"], D["digit"], D["phase"], h_d)
    rest(nc, D, h_d, out_d)


def kernel(x, txt, L0_tok_log_dt, L0_tok_B, L0_tok_inv_A_real, L0_tok_A_imag, L0_attn_Wq, L0_attn_Wk, L0_attn_Wv,
           L0_attn_Wo, L0_ffn_weight, L0_ffn_bias, L0_ffn_gate_w, L0_ffn_in_channel_scale, L0_ffn_out_channel_scale):
    import concourse.bacc as _bacc
    from concourse.bass_utils import run_bass_kernel_spmd as _run

    def twice(a):
        return np.concatenate([a, a], 0)

    def blocks(w, rows=None):
        w = w if rows is None else w[rows]
        return w.reshape(KB, P, -1).transpose(1, 0, 2)

    x, txt = np.asarray(x), np.asarray(txt)
    log_dt, B, inv_a, a_im = (np.asarray(a) for a in (L0_tok_log_dt, L0_tok_B, L0_tok_inv_A_real, L0_tok_A_imag))
    wq, wk, wv, wo, wf, wb, wg, ics, ocs = (np.asarray(a) for a in (
        L0_attn_Wq, L0_attn_Wk, L0_attn_Wv, L0_attn_Wo, L0_ffn_weight, L0_ffn_bias, L0_ffn_gate_w,
        L0_ffn_in_channel_scale, L0_ffn_out_channel_scale))
    arrays = {}
    arrays["par"] = np.stack([np.tile(log_dt, (P, 1)), twice(inv_a.T), twice(a_im.T), twice(B[..., 0].T), twice(B[..., 1].T)], 1)
    arrays["xr"] = twice(x[..., 0].transpose(2, 1, 0))
    arrays["xi"] = twice(x[..., 1].transpose(2, 1, 0))
    arrays["txt"] = txt.reshape(NPAIR, 2, 32, KB, P).transpose(0, 4, 3, 1, 2).reshape(NPAIR, P, KB, 64)
    j, a, i, h = np.meshgrid(np.arange(4), np.arange(2), np.arange(16), np.arange(8), indexing="ij")
    cols = ((8 * j + h) * HD + 2 * i + a).reshape(-1)
    arrays["wq"] = blocks(wq[:, cols])
    arrays["wk"] = blocks(wk[:, cols[:256]])
    arrays["wv"] = blocks(wv)
    g, hh, kv, d = np.meshgrid(np.arange(2), np.arange(4), np.arange(4), np.arange(HD), indexing="ij")
    arrays["wo"] = blocks(wo, (((4 * g + kv) * 4 + hh) * HD + d).reshape(-1))
    arrays["wf"] = blocks(wf.T)
    arrays["wg"] = blocks(wg.T)
    arrays["we"] = np.stack([np.tile(ics, (4, 1)), np.tile(ocs, (4, 1))], 1)
    arrays["bias"] = wb.reshape(KB, P).T
    arrays["digit"] = np.tile(np.concatenate([np.arange(JL), JL * np.arange(IH)]).astype(np.float32), (P, 1))
    phase = np.zeros((P, 4), np.float32)
    phase[:MODES, 0], phase[:MODES, 1], phase[:, 3] = 0.25, 0.25 * TURN, 0.25 * TURN
    arrays["phase"] = phase
    inv_freq = (1.0 / np.float32(10000.0) ** (np.arange(0, HD, 2, dtype=np.float32) / HD)).astype(np.float32)
    pos = np.concatenate([np.arange(128), np.arange(128), np.arange(128, 160), np.arange(128, 160)]).astype(np.float32)
    ang = np.repeat(inv_freq, 8)[:, None] * pos[None]
    arrays["cos"] = (np.cos(ang) / XS).astype(np.float32)
    arrays["sin"] = (np.sin(ang) / XS).astype(np.float32)
    never = np.float32(-3e38)
    r = np.arange(P)
    mask_b = np.zeros((P, 160), np.float32)
    mask_b[:, 128:] = np.where(np.arange(32)[None] > (r % 32)[:, None], never, 0)
    arrays["masks"] = np.concatenate([np.eye(P, dtype=np.float32), np.full((P, P), 1.0 / DIM, np.float32),
                                      np.where(r[None] > r[:, None], never, 0).astype(np.float32), mask_b], 1)
    consts = np.zeros((P, 8), np.float32)
    consts[:, 0], consts[:16, 1], consts[16:32, 2] = EPS, 1, 1
    arrays["consts"] = consts

    nc = _bacc.Bacc("TRN2", target_bir_lowering=False, num_devices=1)
    feed, D = {}, {}
    for name, value in arrays.items():
        value = np.ascontiguousarray(value)
        feed[f"in_{name}"] = value
        D[name] = nc.dram_tensor(f"in_{name}", value.shape, F32, kind="ExternalInput").ap()
    out_d = nc.dram_tensor("out_0", (NPAIR, P, KB, T), F32, kind="ExternalOutput").ap()
    fusion_kernel(nc, D, out_d)
    got = _run(nc, [feed], core_ids=[0]).results[0]["out_0"]
    got = np.asarray(got).transpose(0, 3, 2, 1).reshape(NPAIR, T, DIM)
    s4 = got[:, :256].reshape(CH, P, DIM)
    text = got[:, 256:].reshape(CH, 32, DIM)
    return np.concatenate([s4, text], 1)
```

```python
import concourse.bass as bass
from concourse import mybir
from contextlib import ExitStack
import numpy as np

F32 = mybir.dt.float32
F16 = mybir.dt.float16
BF16 = mybir.dt.bfloat16
I32 = mybir.dt.int32
ALU = mybir.AluOpType
ACT = mybir.ActivationFunctionType
AX = mybir.AxisListType

P = 128
HEADS = 128
CH = 16
MODES = 64
LEN = 1024
JL = 128
IH = LEN // JL
ROUND = 12582912.0
TURN = 6.283184
HC = 8


def s4d_block(nc, par_d, xr_d, xi_d, digit_d, phase_d, h_d):
    with ExitStack() as ctx:
        def sb(name, shape, dt=F32):
            return ctx.enter_context(nc.sbuf_tensor(name, shape, dt))

        def sem(name):
            return ctx.enter_context(nc.semaphore(name))

        par = sb("s4_par", [P, 5, HEADS])
        xr = sb("s4_xr", [P, HEADS, CH])
        xi = sb("s4_xi", [P, HEADS, CH])
        digit = sb("s4_digit", [P, JL + IH])
        phase = sb("s4_phase", [P, 4])
        dt_ = sb("s4_dt", [P, HEADS])
        ea = sb("s4_ea", [P, HEADS])
        decay = sb("s4_decay", [P, HEADS])
        turns = sb("s4_turns", [P, HEADS])
        ez = sb("s4_ez", [P, HEADS])
        small = sb("s4_small", [P, 12, HEADS])
        smalli = sb("s4_smalli", [P, HEADS], I32)
        pamp = sb("s4_pamp", [P, HEADS, IH])
        y1 = sb("s4_y1", [P, HEADS, IH])
        y2 = sb("s4_y2", [P, HEADS, IH])
        low = sb("s4_low", [P, HEADS, JL])
        whole = sb("s4_whole", [P, HC, JL])
        ang = sb("s4_ang", [P, 2, HC, JL])
        lowp = sb("s4_lowp", [P, 2, HC, JL])
        g1 = sb("s4_g1", [P, 2, HC, IH, CH])
        g2 = sb("s4_g2", [P, 2, HC, IH, CH])
        ptmp = g1[:, :, :, :, :].rearrange("p s h i c -> p (s h i c)").rearrange("p (a h i) -> p a h i", a=2, i=IH)
        pang = g2[:, :, :, :, :].rearrange("p s h i c -> p (s h i c)").rearrange("p (a h i) -> p a h i", a=2, i=IH)
        hall = sb("s4_hall", [P, IH * CH, HEADS])
        ps = [[ctx.enter_context(nc.psum_tensor(f"s4_ps{s}{b}", [P, 4, P], F32)) for b in range(2)] for s in range(2)]

        loaded, loaded_x = sem("s4_loaded"), sem("s4_loaded_x")
        chain = sem("s4_chain")
        expo_in, expo_out = sem("s4_expo_in"), sem("s4_expo_out")
        low_amp = sem("s4_low_amp")
        trig_in, trig_out = sem("s4_trig_in"), sem("s4_trig_out")
        chunk_step = sem("s4_chunk_step")
        y_ready = sem("s4_y_ready")
        ang_in, ang_out = sem("s4_ang_in"), sem("s4_ang_out")
        gi_ready = sem("s4_gi_ready")
        ps_full = [[sem(f"s4_ps_full{s}{b}") for b in range(2)] for s in range(2)]
        ops_free = [ps_full[s][1] for s in range(2)]
        copied = [sem("s4_copied_vector"), sem("s4_copied_scalar")]
        stored = sem("s4_stored")
        block = ctx.enter_context(nc.Block())
        NCHUNK = HEADS // HC

        def copy_out(copy, q, s, b):
            copy(hall[:, :, bass.ds(q * HC + 4 * b, 4)], ps[s][b][:, :, :].rearrange("p h c -> p c h")).then_inc(copied[b], 1)

        @block.sync
        def _(sp):
            sp.dma_start(par[:, :, :], par_d).then_inc(loaded, 16)
            sp.dma_start(digit[:, :], digit_d).then_inc(loaded, 16)
            sp.dma_start(phase[:, :], phase_d).then_inc(loaded, 16)
            sp.dma_start(xr[:, :, :], xr_d).then_inc(loaded_x, 16)
            sp.dma_start(xi[:, :, :], xi_d).then_inc(loaded_x, 16)
            sp.wait_ge(copied[0], NCHUNK + 1)
            sp.wait_ge(copied[1], NCHUNK + 1)
            for pr in range(CH // 2):
                for b in range(2):
                    sp.dma_start(h_d[pr, :, :, b, :], hall[:, 2 * pr + b:IH * CH:CH, :]).then_inc(stored, 16)
            sp.wait_ge(stored, 16 * CH)

        @block.vector
        def _(dve):
            done = [0]

            def link(ins):
                done[0] += 1
                ins.then_inc(chain, 1)
                dve.wait_ge(chain, done[0])

            v = nc.vector
            t = [small[:, k, :] for k in range(12)]

            def exact_exp(out, x):
                a, b, c = t[0], t[1], t[2]
                link(v.tensor_scalar(a, x, 88.0, -87.0, ALU.min, ALU.max))
                link(v.tensor_scalar(b, a, 1.4426950408889634, ROUND, ALU.mult, ALU.add))
                link(v.tensor_scalar(b, b, ROUND, None, ALU.subtract))
                link(v.scalar_tensor_tensor(a, b, -0.693145751953125, a, ALU.mult, ALU.add))
                link(v.scalar_tensor_tensor(a, b, -1.42860682030941723e-6, a, ALU.mult, ALU.add))
                link(v.tensor_scalar(c, a, 1.0 / 5040, None, ALU.mult))
                for k in (720, 120, 24, 6, 2, 1):
                    link(v.scalar_tensor_tensor(c, c, 1.0 / k, a, ALU.add, ALU.mult))
                link(v.tensor_scalar(c, c, 1.0, None, ALU.add))
                link(v.tensor_scalar(b, b, 127.0, 8388608.0, ALU.add, ALU.mult))
                link(v.tensor_copy(smalli[:, :], b))
                link(v.tensor_tensor(out, c, smalli[:, :].bitcast(F32), ALU.mult))

            dve.wait_ge(loaded, 48)
            exact_exp(dt_[:, :], par[:, 0, :])
            exact_exp(ea[:, :], par[:, 1, :])
            link(v.scalar_tensor_tensor(decay[:, :], ea[:, :], -1.0, dt_[:, :], ALU.mult, ALU.mult))
            v.tensor_tensor(pamp[:, :, :], decay[:, :].unsqueeze(2).broadcast_to([P, HEADS, IH]),
                            digit[:, JL:].unsqueeze(1).broadcast_to([P, HEADS, IH]), ALU.mult).then_inc(expo_in, 1)
            link(v.tensor_tensor(turns[:, :], par[:, 2, :], dt_[:, :], ALU.mult))
            link(v.tensor_scalar(turns[:, :], turns[:, :], float(1 / (2 * np.pi)), None, ALU.mult))
            link(v.tensor_scalar(t[3], turns[:, :], ROUND, None, ALU.add))
            link(v.scalar_tensor_tensor(t[3], t[3], ROUND, turns[:, :], ALU.subtract, ALU.subtract))
            link(v.tensor_scalar(turns[:, :], t[3], -1.0, None, ALU.mult))

            def fraction(out, y, shift):
                link(v.tensor_scalar(out, y, shift, ROUND, ALU.add, ALU.add))
                return v.scalar_tensor_tensor(out, out, ROUND, y, ALU.subtract, ALU.subtract)

            fraction(t[4], turns[:, :], 0.0).then_inc(trig_in, 1)
            fraction(t[5], turns[:, :], 0.25).then_inc(trig_in, 1)
            link(v.tensor_tensor(ptmp[:, 0, :, :], turns[:, :].unsqueeze(2).broadcast_to([P, HEADS, IH]),
                                 digit[:, JL:].unsqueeze(1).broadcast_to([P, HEADS, IH]), ALU.mult))
            fraction(pang[:, 0, :, :], ptmp[:, 0, :, :], 0.0).then_inc(trig_in, 1)
            fraction(pang[:, 1, :, :], ptmp[:, 0, :, :], 0.25).then_inc(trig_in, 1)
            exact_exp(ez[:, :], decay[:, :])
            link(v.tensor_tensor(t[6], ea[:, :], ea[:, :], ALU.mult))
            link(v.tensor_tensor(t[7], par[:, 2, :], par[:, 2, :], ALU.mult))
            link(v.tensor_tensor(t[6], t[6], t[7], ALU.add))
            link(v.reciprocal(t[6], t[6]))

            dve.wait_ge(trig_out, 2)
            zr, zi, br, bi = t[8], t[9], par[:, 3, :], par[:, 4, :]
            link(v.tensor_tensor(zr, ez[:, :], t[5], ALU.mult))
            link(v.tensor_tensor(zi, ez[:, :], t[4], ALU.mult))
            link(v.tensor_scalar(zr, zr, 1.0, None, ALU.subtract))
            link(v.tensor_tensor(t[0], br, zr, ALU.mult))
            link(v.tensor_tensor(t[1], bi, zi, ALU.mult))
            link(v.tensor_tensor(t[10], t[0], t[1], ALU.subtract))
            link(v.tensor_tensor(t[0], br, zi, ALU.mult))
            link(v.tensor_tensor(t[1], bi, zr, ALU.mult))
            link(v.tensor_tensor(t[11], t[0], t[1], ALU.add))
            link(v.tensor_tensor(t[0], t[11], par[:, 2, :], ALU.mult))
            link(v.tensor_tensor(t[1], t[10], ea[:, :], ALU.mult))
            link(v.tensor_tensor(t[0], t[0], t[1], ALU.subtract))
            link(v.scalar_tensor_tensor(t[8], t[0], 2.0, t[6], ALU.mult, ALU.mult))
            link(v.tensor_tensor(t[0], t[11], ea[:, :], ALU.mult))
            link(v.tensor_tensor(t[1], t[10], par[:, 2, :], ALU.mult))
            link(v.tensor_tensor(t[0], t[0], t[1], ALU.add))
            link(v.scalar_tensor_tensor(t[9], t[0], -2.0, t[6], ALU.mult, ALU.mult))
            dve.wait_ge(trig_out, 4)
            dve.wait_ge(expo_out, 1)
            fr = t[8].unsqueeze(2).broadcast_to([P, HEADS, IH])
            fi = t[9].unsqueeze(2).broadcast_to([P, HEADS, IH])
            psin, pcos = pang[:, 0, :, :], pang[:, 1, :, :]
            link(v.tensor_tensor(psin, psin, pamp[:, :, :], ALU.mult))
            link(v.tensor_tensor(pcos, pcos, pamp[:, :, :], ALU.mult))
            a, b = ptmp[:, 0, :, :], ptmp[:, 1, :, :]
            link(v.tensor_tensor(a, pcos, fr, ALU.mult))
            link(v.tensor_tensor(b, psin, fi, ALU.mult))
            link(v.tensor_tensor(y1[0:MODES, :, :], a[0:MODES], b[0:MODES], ALU.subtract))
            link(v.tensor_tensor(y2[MODES:P, :, :], b[MODES:P], a[MODES:P], ALU.subtract))
            link(v.tensor_tensor(a, pcos, fi, ALU.mult))
            link(v.tensor_tensor(b, psin, fr, ALU.mult))
            link(v.tensor_tensor(a, a, b, ALU.add))
            link(v.tensor_scalar(y2[0:MODES, :, :], a[0:MODES], -1.0, None, ALU.mult))
            v.tensor_scalar(y1[MODES:P, :, :], a[MODES:P], -1.0, None, ALU.mult).then_inc(y_ready, 1)
            dve.wait_ge(y_ready, 1)
            dve.wait_ge(loaded_x, 32)
            with dve.Fori(0, NCHUNK // 2) as it:
                steps = [0]

                def step(ins):
                    steps[0] += 1
                    ins.then_inc(chunk_step, 1)
                    dve.wait_ge(chunk_step, 10 * it + steps[0])

                for s in range(2):
                    q = 2 * it + s
                    hs = bass.ds(q * HC, HC)
                    step(v.tensor_tensor(whole[:, :, :], turns[:, hs].unsqueeze(2).broadcast_to([P, HC, JL]),
                                         digit[:, 0:JL].unsqueeze(1).broadcast_to([P, HC, JL]), ALU.mult))
                    step(v.tensor_scalar(ang[:, s], whole[:, :, :], phase[:, 0:1], ROUND, ALU.add, ALU.add))
                    v.scalar_tensor_tensor(ang[:, s], ang[:, s], ROUND, whole[:, :, :], ALU.subtract, ALU.subtract).then_inc(ang_in, 1)
                    dve.wait_ge(ops_free[s], it + 1)
                    step(v.tensor_tensor(g1[:, s], xr[:, hs, :].unsqueeze(2).broadcast_to([P, HC, IH, CH]),
                                         y1[:, hs, :].unsqueeze(3).broadcast_to([P, HC, IH, CH]), ALU.mult))
                    dve.wait_ge(gi_ready, q + 1)
                    step(v.tensor_tensor(g1[:, s], g1[:, s], g2[:, s], ALU.add))
                    dve.wait_ge(ang_out, q + 1)
                    step(v.tensor_tensor(lowp[:, s], low[:, hs, :], ang[:, s], ALU.mult))
                    dve.wait_ge(ps_full[s][0], it + 1)
                    copy_out(v.tensor_copy, q, s, 0)
                assert steps[0] == 10

        @block.gpsimd
        def _(pool):
            for s in (*ops_free, *copied):
                pool.sem_inc(s, 1)
            pool.wait_ge(y_ready, 1)
            pool.wait_ge(loaded_x, 32)
            with pool.Fori(0, NCHUNK // 2) as it:
                for s in range(2):
                    q = 2 * it + s
                    hs = bass.ds(q * HC, HC)
                    pool.wait_ge(ops_free[s], it + 1)
                    nc.gpsimd.tensor_tensor(g2[:, s], xi[:, hs, :].unsqueeze(2).broadcast_to([P, HC, IH, CH]),
                                            y2[:, hs, :].unsqueeze(3).broadcast_to([P, HC, IH, CH]), ALU.mult).then_inc(gi_ready, 1)

        @block.scalar
        def _(act):
            s_ = nc.scalar
            act.wait_ge(expo_in, 1)
            s_.activation(pamp[:, :, :], pamp[:, :, :], ACT.Exp).then_inc(expo_out, 1)
            with act.Fori(0, HEADS // 4) as it:
                for k in range(4):
                    s_.activation(low[:, bass.ds(4 * it + k, 1), :], digit[:, 0:JL].unsqueeze(1), ACT.Exp,
                                  scale=decay[:, bass.ds(4 * it + k, 1)]).then_inc(low_amp, 1)
            act.wait_ge(trig_in, 4)
            for k, tile in enumerate((small[:, 4, :], small[:, 5, :], pang[:, 0, :, :], pang[:, 1, :, :])):
                if k % 2:
                    s_.activation(tile, tile, ACT.Sin, scale=-TURN, bias=phase[:, 3:4]).then_inc(trig_out, 1)
                else:
                    s_.activation(tile, tile, ACT.Sin, scale=-TURN).then_inc(trig_out, 1)
            with act.Fori(0, NCHUNK // 2) as it:
                for s in range(2):
                    q = 2 * it + s
                    act.wait_ge(ang_in, q + 1)
                    s_.activation(ang[:, s], ang[:, s], ACT.Sin, scale=-TURN, bias=phase[:, 1:2]).then_inc(ang_out, 1)
                    act.wait_ge(ps_full[s][1], it + 2)
                    copy_out(s_.copy, q, s, 1)

        @block.tensor
        def _(pe):
            with pe.Fori(0, NCHUNK // 2) as it:
                for s in range(2):
                    q = 2 * it + s
                    pe.wait_ge(chunk_step, 10 * it + 5 * s + 5)
                    for b in range(2):
                        pe.wait_ge(copied[b], q + 1)
                        for k in range(4):
                            last = nc.tensor.matmul(ps[s][b][:, k, :], lowp[:, s, 4 * b + k, :],
                                                    g1[:, s, 4 * b + k].rearrange("p i c -> p (i c)"), start=True, stop=True)
                        last.then_inc(ps_full[s][b], 1)

DIM, T, NPAIR, KB = 1024, 320, 8, 8
NQ, NKV, HD = 32, 8, 32
EXPERTS = 8
EPS = 1e-5
XS = 32.0
SHIFT = 4096.0
QKB = 5
A0, A1, BT = slice(0, 128), slice(128, 256), slice(256, 320)

FRONT = ["mean1", "var1", *(f"qk{j}{ab}" for j in (4, 0, 1, 2, 3) for ab in "ab"), "v01", "v2", "maxT"]
USES = ("atA00 atA01 atA10 atA11 atB o0 o1 o2 o3 mean1 o4 o5 var1 o6 o7 qk4a qk4b mean2 qk0a qk0b qk1a qk1b var2 "
        "qk2a qk2b qk3a qk3b gate routT in0 in1 in2 in3 v01 in4 in5 in6 in7 v2 os0 f0 os1 f1 os2 f2 os3 f3 os4 f4 "
        "os5 f5 maxT os6 f6 os7 f7").split()
BANKS = 4
CREDIT = 1
assert len(USES) % BANKS == 0
TURNS = len(USES) // BANKS


class Step:

    def __init__(self, p, back=True, front=True):
        self.p, self.q, self.back, self.front = p, p + 1, back, front

    def use(self, name):
        at = USES.index(name)
        b = at % BANKS
        here = [n for k, n in enumerate(USES) if k < at and k % BANKS == b]
        front_uses = sum(USES.index(n) % BANKS == b for n in FRONT)
        if not self.back:
            return b, sum(n in FRONT for n in here)
        if not self.front:
            here = [n for n in here if n not in FRONT]
        return b, self.p * TURNS + front_uses + len(here)


def rest(nc, D, h_d, out_d):
    with ExitStack() as ctx:
        def sb(name, shape, dt=F32):
            return ctx.enter_context(nc.sbuf_tensor(name, shape, dt))

        def sem(name):
            return ctx.enter_context(nc.semaphore(name))

        wqk = sb("wqk", [P, 2, KB, QKB * 256], F16)
        wv = sb("wv", [P, 2, KB, 256], F16)
        wo = sb("wo", [P, 2, KB, DIM], F16)
        wf = sb("wf", [P, KB, DIM], F16)
        wg = sb("wg", [P, 2, KB, EXPERTS], F16)
        experts = sb("experts", [4 * EXPERTS, 2, DIM], F16)
        inv = sb("inv", [P, 8])
        fac = sb("fac", [P, 8])
        bias = sb("bias", [P, KB])
        cosT, sinT = sb("cosT", [P, T]), sb("sinT", [P, T])
        ident = sb("ident", [P, P])
        ident16 = sb("ident16", [P, P], F16)
        identb = sb("identb", [P, P], BF16)
        maskA = sb("maskA", [P, P], BF16)
        maskB = sb("maskB", [P, 160], BF16)
        avg = sb("avg", [P, P])
        consts = sb("consts", [P, 8])
        weights_block(nc, D, locals())
        pairs_block(nc, D, h_d, out_d, locals())


def weights_block(nc, D, W):
    with ExitStack() as ctx:
        def sb(name, shape, dt=F32):
            return ctx.enter_context(nc.sbuf_tensor(name, shape, dt))

        def sem(name):
            return ctx.enter_context(nc.semaphore(name))

        raw = sb("raw", [P, KB, 1024])
        raw2 = sb("raw2", [P, KB, 1024])
        rawg = sb("rawg", [P, KB, EXPERTS])
        rawe = sb("rawe", [4 * EXPERTS, 2, DIM])
        emask = sb("emask", [P, 2 * P + P + 160])
        mx = sb("wl_largest", [P, 8])
        mxa = sb("wl_largest_all", [P, 8])
        scale = sb("scale", [P, 8])
        ehi = sb("ehi", [4 * EXPERTS, 2, DIM], F16)
        elo = sb("elo", [4 * EXPERTS, 2, DIM], F16)
        wqk, wv, wo, wf, wg, experts, inv, fac = (W[n] for n in ("wqk", "wv", "wo", "wf", "wg", "experts", "inv", "fac"))
        consts = W["consts"]
        ld_c, ld_a, ld_b, ld_e = sem("wl_const"), sem("wl_raw"), sem("wl_raw2"), sem("wl_experts")
        chain, mx_ready, all_ready = sem("wl_chain"), sem("wl_mx"), sem("wl_all")
        sc_ready, hi_ready, lo_ready, sign_ready = sem("wl_scale"), sem("wl_hi"), sem("wl_lo"), sem("wl_sign")
        block = ctx.enter_context(nc.Block())
        raw_t = {"q": (raw, 1024), "k": (raw2, 256), "v": (raw2, 256), "o": (raw, 1024)}

        @block.sync
        def _(sp):
            sp.dma_start(raw[:, :, :], D["wq"]).then_inc(ld_a, 16)
            sp.dma_start(raw2[:, :, 0:256], D["wk"]).then_inc(ld_b, 16)
            sp.dma_start(raw2[:, :, 256:512], D["wv"]).then_inc(ld_b, 16)
            sp.dma_start(rawg[:, :, :], D["wg"]).then_inc(ld_e, 16)
            sp.dma_start(rawe[:, :, :], D["we"]).then_inc(ld_e, 16)
            sp.dma_start(consts[:, :], D["consts"]).then_inc(ld_e, 16)
            sp.dma_start(emask[:, :], D["masks"]).then_inc(ld_c, 16)
            sp.dma_start(W["cosT"][:, :], D["cos"]).then_inc(ld_c, 16)
            sp.dma_start(W["sinT"][:, :], D["sin"]).then_inc(ld_c, 16)
            sp.dma_start(W["bias"][:, :], D["bias"]).then_inc(ld_c, 16)
            sp.wait_ge(lo_ready, 3)
            sp.dma_start(raw[:, :, :], D["wo"]).then_inc(ld_a, 16)
            sp.dma_start(raw2[:, :, :], D["wf"]).then_inc(ld_b, 16)

        @block.gpsimd
        def _(pool):
            for n, cols in ((1, slice(0, 3)), (2, slice(4, 7)), (3, slice(3, 4))):
                pool.wait_ge(mx_ready, n)
                nc.gpsimd.partition_all_reduce(mxa[:, cols], mx[:, cols], P, bass.bass_isa.ReduceOp.max).then_inc(all_ready, 1)

        @block.scalar
        def _(act):
            def hi(dst, src, k):
                nc.scalar.activation(dst, src, ACT.Copy, scale=scale[:, k:k + 1]).then_inc(hi_ready, 1)

            act.wait_ge(sc_ready, 1)
            hi(wqk[:, 0, :, 0:1024], raw[:, :, :], 0)
            hi(wqk[:, 0, :, 1024:1280], raw2[:, :, 0:256], 1)
            hi(wv[:, 0], raw2[:, :, 256:512], 2)
            act.wait_ge(sc_ready, 2)
            hi(wg[:, 0], rawg[:, :, :], 4)
            for e in range(2):
                nc.scalar.activation(ehi[:, e], rawe[:, e], ACT.Copy, scale=scale[0:32, 5 + e:6 + e]).then_inc(hi_ready, 1)
            act.wait_ge(ld_b, 48)
            nc.scalar.activation(wf[:, :, :], raw2[:, :, :], ACT.Sign).then_inc(sign_ready, 1)
            act.wait_ge(sc_ready, 3)
            hi(wo[:, 0], raw[:, :, :], 3)

        @block.vector
        def _(dve):
            v = nc.vector
            done = [0]

            def link(ins):
                done[0] += 1
                ins.then_inc(chain, 1)
                dve.wait_ge(chain, done[0])

            def largest(k, src, rows=slice(0, P)):
                return v.tensor_reduce(mx[rows, k:k + 1], src, AX.XY if len(src.shape) > 2 else AX.X, ALU.max, apply_absolute_value=True)

            def scales(cols):
                link(v.tensor_scalar(mxa[:, cols], mxa[:, cols], 1e-30, 1e30, ALU.max, ALU.min))
                link(v.tensor_scalar(inv[:, cols].bitcast(I32), mxa[:, cols].bitcast(I32), 0x7F800000, None, ALU.bitwise_and))
                v.tensor_scalar(scale[:, cols].bitcast(I32), inv[:, cols].bitcast(I32), -1.0, float(254 << 23), ALU.mult, ALU.add).then_inc(sc_ready, 1)

            def lo(dst, src, hi_, k, rows=slice(0, P)):
                return v.scalar_tensor_tensor(dst, src, scale[rows, k:k + 1], hi_, ALU.mult, ALU.subtract)

            link(v.memset(mx[:, :], 0.0))
            dve.wait_ge(ld_a, 16)
            link(largest(0, raw[:, :, :]))
            dve.wait_ge(ld_b, 32)
            link(largest(1, raw2[:, :, 0:256]))
            largest(2, raw2[:, :, 256:512]).then_inc(mx_ready, 1)
            dve.wait_ge(ld_e, 48)
            link(largest(4, rawg[:, :, :]))
            link(largest(5, rawe[:, 0], slice(0, 32)))
            largest(6, rawe[:, 1], slice(0, 32)).then_inc(mx_ready, 1)
            dve.wait_ge(all_ready, 1)
            scales(slice(0, 3))
            dve.wait_ge(all_ready, 2)
            scales(slice(4, 7))
            dve.wait_ge(sc_ready, 2)
            link(v.tensor_scalar(fac[:, 0:1], inv[:, 0:1], inv[:, 1:2], float(HD ** -0.5), ALU.mult, ALU.mult))
            link(v.tensor_scalar(fac[:, 2:3], inv[:, 4:5], 1.0 / XS, None, ALU.mult))
            link(v.tensor_scalar(fac[:, 3:4], inv[:, 5:6], inv[:, 6:7], 1.0 / XS, ALU.mult, ALU.mult))
            dve.wait_ge(ld_c, 64)
            v.tensor_copy(W["ident"][:, :], emask[:, 0:P])
            v.tensor_copy(W["ident16"][:, :], emask[:, 0:P])
            v.tensor_copy(W["identb"][:, :], emask[:, 0:P])
            v.tensor_copy(W["avg"][:, :], emask[:, P:2 * P])
            v.tensor_copy(W["maskA"][:, :], emask[:, 2 * P:3 * P])
            v.tensor_copy(W["maskB"][:, :], emask[:, 3 * P:])
            dve.wait_ge(hi_ready, 1)
            lo(wqk[:, 1, :, 0:1024], raw[:, :, :], wqk[:, 0, :, 0:1024], 0).then_inc(lo_ready, 1)
            dve.wait_ge(hi_ready, 2)
            lo(wqk[:, 1, :, 1024:1280], raw2[:, :, 0:256], wqk[:, 0, :, 1024:1280], 1).then_inc(lo_ready, 1)
            dve.wait_ge(hi_ready, 3)
            lo(wv[:, 1], raw2[:, :, 256:512], wv[:, 0], 2).then_inc(lo_ready, 1)
            dve.wait_ge(hi_ready, 4)
            link(lo(wg[:, 1], rawg[:, :, :], wg[:, 0], 4))
            dve.wait_ge(hi_ready, 6)
            for e in range(2):
                link(lo(elo[:, e], rawe[:, e], ehi[:, e], 5 + e, slice(0, 32)))
            link(v.tensor_scalar(elo[:, :, :], elo[:, :, :], consts[0:32, 2:3], None, ALU.mult))
            link(v.scalar_tensor_tensor(experts[:, :, :], ehi[:, :, :], consts[0:32, 1:2], elo[:, :, :], ALU.mult, ALU.add))
            dve.wait_ge(ld_a, 32)
            largest(3, raw[:, :, :]).then_inc(mx_ready, 1)
            dve.wait_ge(all_ready, 3)
            scales(slice(3, 4))
            dve.wait_ge(sc_ready, 3)
            link(v.tensor_scalar(fac[:, 1:2], inv[:, 2:3], inv[:, 3:4], None, ALU.mult))
            dve.wait_ge(hi_ready, 7)
            link(lo(wo[:, 1], raw[:, :, :], wo[:, 0], 3))
            dve.wait_ge(sign_ready, 1)

        @block.tensor
        def _(pe):
            pass


def pairs_block(nc, D, h_d, out_d, W):
    with ExitStack() as ctx:
        def sb(name, shape, dt=F32):
            return ctx.enter_context(nc.sbuf_tensor(name, shape, dt))

        def sem(name):
            return ctx.enter_context(nc.semaphore(name))

        wqk, wv, wo, wf, wg, experts, fac, bias = (W[n] for n in ("wqk", "wv", "wo", "wf", "wg", "experts", "fac", "bias"))
        cosT, sinT, ident, ident16, identb, maskA, maskB, avg, consts = (
            W[n] for n in ("cosT", "sinT", "ident", "ident16", "identb", "maskA", "maskB", "avg", "consts"))
        xc = sb("xc", [P, KB, T])
        x1 = sb("x1", [P, 2, KB, T], F16)
        x2 = sb("x2", [P, 2, KB, T], F16)
        x1sq = x1[:, :, :, :].rearrange("p a k t -> p (a k t)").bitcast(F32).rearrange("p (k t) -> p k t", k=KB)
        x2sq = x2[:, :, :, :].rearrange("p a k t -> p (a k t)").bitcast(F32).rearrange("p (k t) -> p k t", k=KB)
        h2 = sb("h2", [P, KB, T])
        qs = sb("qs", [P, NQ, T], F16)
        ks = sb("ks", [P, NKV, T], F16)
        rt = sb("rt", [P, 2, 2, 2, T], F16)
        pf = sb("pf", [P, 3, 512])
        ph = sb("ph", [P, 2, 3, 512], F16)
        prod = pf[:, :, :].rearrange("p a c -> p (a c)")[:, 0:4 * T].rearrange("p (a t) -> p a t", a=4)
        rot = ph[:, :, :, :].rearrange("p a b c -> p (a b c)").bitcast(F32)[:, 0:4 * T].rearrange("p (s a t) -> p s a t", s=2, a=2)
        vv = sb("vv", [P, 2, 3, NKV, HD + 1], F16)
        att = sb("att", [P, 10, NKV, HD])
        qb = att[:, :, :, :].rearrange("p n k d -> p (n k d)").bitcast(F16)[:, 0:64 * NQ].rearrange("p (b h q) -> p b h q", b=2, h=NQ)
        xa = att[:, :, :, :].rearrange("p n k d -> p (n k d)").rearrange("p (k t) -> p k t", k=KB)
        mxa = sb("mxa", [P, 2, NKV, 4])
        mxb = sb("mxb", [P, 2, NKV])
        rsum = sb("rsum", [P, 10])
        mt = rt[0:NQ, :, :, :, :].rearrange("p a b c t -> p (a b c t)")[:, 0:1024].rearrange("p (a c) -> p a c", a=2)
        sums = sb("sums", [P, T])
        rstd = sb("rstd", [P, T])
        nt = sb("nt", [P, T])
        gl = sb("gl", [P, 3, EXPERTS])
        g1 = sb("g1_", [P, 3, 1])
        rr = sb("rr", [P, 3, 4, EXPERTS], F16)
        rT = sb("rT", [4 * EXPERTS, T], F16)
        os_ = sb("os_", [P, 2, T])

        pj = [ctx.enter_context(nc.psum_tensor(f"pj{b}", [P, 512], F32)) for b in range(BANKS)]
        sa = [ctx.enter_context(nc.psum_tensor(f"sa{b}", [P, 512], F32)) for b in range(3)]
        po = ctx.enter_context(nc.psum_tensor("po", [P, 512], F32))

        h_loaded, res_loaded, stored = sem("h_loaded"), sem("res_loaded"), sem("stored")
        stacked = [sem(f"stacked{j}") for j in range(QKB)]
        rows_loaded = sem("rows_loaded")
        pj_full = [sem(f"pj_full{b}") for b in range(BANKS)]
        pj_free = [sem(f"pj_free{b}") for b in range(BANKS)]
        sa_full = [sem(f"sa_full{b}") for b in range(3)]
        sa_free = [sem(f"sa_free{b}") for b in range(3)]
        po_full, po_free = sem("po_full"), sem("po_free")
        dchain, achain = {"front": sem("dchain_front"), "back": sem("dchain_back")}, {i: sem(f"achain{i}") for i in (1, 2)}
        init = sem("init")
        sum_ready, squared, rough, norm_ready, hi_made, x_ready = (
            {i: sem(f"{name}{i}") for i in (1, 2)} for name in ("sum_ready", "squared", "rough", "norm_ready", "hi_made", "x_ready"))
        rot_ready, rot_hi, rope_ready = sem("rot_ready"), sem("rot_hi"), sem("rope_ready")
        v_hi, qb_ready = sem("v_hi"), sem("qb_ready")
        exp_ready, kept, split_hi, split_ready, split_used = sem("exp_ready"), sem("kept"), sem("split_hi"), sem("split_ready"), sem("split_used")
        at_hi = sem("at_hi")
        gexp_in, gexp_out, rout_ready = sem("gexp_in"), sem("gexp_out"), sem("rout_ready")
        y_hi, y_ready = sem("y_hi"), sem("y_ready")
        f_done = sem("f_done")
        block = ctx.enter_context(nc.Block())

        def full(eng, name, s):
            b, n = s.use(name)
            eng.wait_ge(pj_full[b], n + 1)
            return pj[b]

        def read(eng, name, s):
            b, n = s.use(name)
            eng.wait_ge(pj_free[b], n + 1 + CREDIT)

        def free(name):
            return pj_free[USES.index(name) % BANKS]

        def steps(eng, program):
            program(Step(-1, back=False))
            with eng.Fori(0, NPAIR - 1) as p:
                program(Step(p))
            program(Step(NPAIR - 1, front=False))

        BB = [slice(256, 288), slice(288, 320)]
        AB = [A0, A1]

        @block.sync
        def _(sp):
            def step(s):
                p, q = s.p, s.q
                if s.back:
                    sp.wait_ge(stored, 16 * p + CREDIT)
                    sp.dma_start(h2[:, :, 0:256], h_d[p, :, :, :, :].rearrange("j i b h -> j i (b h)")).then_inc(res_loaded, 16)
                    sp.dma_start(h2[:, :, 256:320], D["txt"][p, :, :, :]).then_inc(res_loaded, 16)
                    full(sp, "atB", s)
                if s.front:
                    sp.dma_start(xa[:, :, 0:256], h_d[q, :, :, :, :].rearrange("j i b h -> j i (b h)")).then_inc(h_loaded, 16)
                    sp.dma_start(xa[:, :, 256:320], D["txt"][q, :, :, :]).then_inc(h_loaded, 16)
                    for n, j in enumerate((4, 0, 1, 2, 3)):
                        sp.wait_ge(rope_ready, QKB * q + n + 1)
                        parts = (0, 1, 0) if j == 4 else (0, 0, 1)
                        for g, hl in enumerate(parts):
                            for ab in range(2):
                                r = 32 * g + 16 * ab
                                dst = ks[r:r + 16, :, :] if j == 4 else qs[r:r + 16, 8 * j:8 * j + 8, :]
                                sp.dma_start(dst, rt[:, n % 2, ab, hl, :]).then_inc(stacked[n], 16)
                    read(sp, "maxT", s)
                    for hl in range(2):
                        sp.dma_start(qs[96 + hl:97 + hl, :, 0:256], mt[:, hl, 0:256]).then_inc(rows_loaded, 16)
                        for b in range(2):
                            sp.dma_start(qs[96 + hl:97 + hl, :, BB[b]].rearrange("p (k h) q -> p k h q", h=4),
                                         mt[0:NKV, hl, 256 + 128 * b:384 + 128 * b].rearrange("p (h q) -> p h q", h=4)).then_inc(rows_loaded, 16)
                if s.back:
                    sp.wait_ge(f_done, KB * (p + 1))
                    sp.dma_start(out_d[p, :, :, :], h2[:, :, :]).then_inc(stored, 16)

            steps(sp, step)
            sp.wait_ge(stored, 16 * NPAIR + CREDIT)

        @block.tensor
        def _(pe):
            mm = nc.tensor.matmul

            def bank(name, s):
                b, n = s.use(name)
                pe.wait_ge(pj_free[b], n + CREDIT)
                return pj[b], pj_full[b]

            def split_product(out, w_hi, w_lo, x, cols=slice(0, T)):
                for k in range(KB):
                    mm(out, w_hi(k), x[:, 0, k, cols], start=(k == 0), stop=False)
                    mm(out, w_hi(k), x[:, 1, k, cols], start=False, stop=False)
                    last = mm(out, w_lo(k), x[:, 0, k, cols], start=False, stop=(k == KB - 1))
                return last

            def average(name, s, i, n):
                ps, f = bank(name, s)
                pe.wait_ge(sum_ready[i], 2 * (s.q if i == 1 else s.p) + n)
                mm(ps[:, 0:T], avg[:, :], sums[:, :], start=True, stop=True).then_inc(f, 1)

            pe.wait_ge(init, 2)

            def step(s):
                p, q = s.p, s.q

                def scores(kv):
                    for b in range(2):
                        pe.wait_ge(sa_free[b], 16 * p + 8 + kv + CREDIT)
                        mm(sa[b][:, :].rearrange("p (h q) -> p h q", h=4), ks[0:98, kv, AB[b]], qs[0:98, 4 * kv:4 * kv + 4, AB[b]],
                           start=True, stop=True).then_inc(sa_full[b], 1)
                    pe.wait_ge(sa_free[2], 16 * p + 8 + kv + CREDIT)
                    for b in range(2):
                        mm(sa[2][:, 128 * b:128 * b + 128].rearrange("p (h q) -> p h q", h=4), ks[0:98, kv, AB[b]],
                           qs[0:98, 4 * kv:4 * kv + 4, BB[b]], start=True, stop=True)
                    mm(sa[2][:, 256:512].rearrange("p (b h q) -> p b h q", b=2, h=4), ks[0:98, kv, 192:320],
                       qs[0:98, 4 * kv:4 * kv + 4, BT].rearrange("p h (b q) -> p b h q", b=2), start=True, stop=True).then_inc(sa_full[2], 1)

                def values(kv):
                    pe.wait_ge(po_free, NKV * p + kv + CREDIT)
                    o = po[:, 0:330].rearrange("p (n d) -> p n d", n=10)

                    def weighted(n, terms):
                        for i, (sl, c, t) in enumerate(terms):
                            c = slice(c, c + 128)
                            mm(o[:, n, :], ph[:, 0, sl, c], vv[:, 0, t, kv, :], start=(i == 0), stop=False)
                            mm(o[:, n, :], ph[:, 0, sl, c], vv[:, 1, t, kv, :], start=False, stop=False)
                            last = mm(o[:, n, :], ph[:, 1, sl, c], vv[:, 0, t, kv, :], start=False, stop=(i == len(terms) - 1))
                        return last

                    for b in range(2):
                        pe.wait_ge(split_ready, 3 * (NKV * p + kv) + b + 1)
                        for h in range(4):
                            last = weighted(4 * b + h, [(b, 128 * h, b)])
                        last.then_inc(split_used, 1)
                    pe.wait_ge(split_ready, 3 * (NKV * p + kv) + 3)
                    for b in range(2):
                        last = weighted(8 + b, [(2, 128 * b, b), (2, 256 + 128 * b, 2)])
                    last.then_inc(po_full, 1)

                def attention():
                    pe.wait_ge(rows_loaded, 96 * (p + 1))
                    scores(0)
                    for kv in range(NKV):
                        if kv + 1 < NKV:
                            scores(kv + 1)
                        values(kv)
                    pe.wait_ge(po_free, NKV * (p + 1) + CREDIT)
                    for kh in range(2):
                        for b in range(2):
                            ps, f = bank(f"atA{kh}{b}", s)
                            for h in range(4):
                                last = nc.tensor.transpose(ps[:, 128 * h:128 * h + 128], att[:, 4 * b + h, 4 * kh:4 * kh + 4, :].rearrange("p k d -> p (k d)"), ident[:, :])
                            last.then_inc(f, 1)
                    ps, f = bank("atB", s)
                    for kh in range(2):
                        for b in range(2):
                            last = nc.tensor.transpose(ps[:, 256 * kh + 128 * b:256 * kh + 128 * b + 128], att[:, 8 + b, 4 * kh:4 * kh + 4, :].rearrange("p k d -> p (k d)"), ident[:, :])
                    last.then_inc(f, 1)
                    read(pe, "atB", s)

                def o_product(m):
                    ps, f = bank(f"o{m}", s)
                    c = slice(128 * m, 128 * m + 128)
                    split_product(ps[:, 0:T], lambda k: wo[:, 0, k, c], lambda k: wo[:, 1, k, c], x2).then_inc(f, 1)

                def qk_product(j):
                    for a in range(2):
                        ps, f = bank(f"qk{j}{'ab'[a]}", s)
                        c = slice(256 * j + 128 * a, 256 * j + 128 * a + 128)
                        split_product(ps[:, 0:T], lambda k: wqk[:, 0, k, c], lambda k: wqk[:, 1, k, c], x1).then_inc(f, 1)

                def v_product(t):
                    if t != 1:
                        ps, f = bank("v01" if t < 2 else "v2", s)
                    else:
                        ps, f = pj[s.use("v01")[0]], pj_full[s.use("v01")[0]]
                    cols = (A0, A1, slice(192, 320))[t]
                    o = ps[:, 256 * (t % 2):256 * (t % 2) + 256]
                    for k in range(KB):
                        mm(o, x1[:, 0, k, cols], wv[:, 0, k, :], start=(k == 0), stop=False)
                        mm(o, x1[:, 0, k, cols], wv[:, 1, k, :], start=False, stop=False)
                        last = mm(o, x1[:, 1, k, cols], wv[:, 0, k, :], start=False, stop=(k == KB - 1))
                    if t >= 1:
                        last.then_inc(f, 1)

                def maxima_scores(kv):
                    if kv % 2 == 0:
                        pe.wait_ge(stacked[kv // 2 + 1], 96 * (q + 1) + CREDIT)
                        pe.wait_ge(qb_ready, 4 * q + kv // 2 + 1)
                    if kv == 0:
                        pe.wait_ge(stacked[0], 96 * (q + 1) + CREDIT)
                    for b in range(2):
                        pe.wait_ge(sa_free[b], 16 * q + kv + CREDIT)
                        s = sa[b][:, :].rearrange("p (h k) -> p h k", h=4)
                        mm(s, identb[:, :], maskA[:, :].unsqueeze(1).broadcast_to([P, 4, P]), start=True, stop=False, skip_group_check=True)
                        for h in range(4):
                            last = mm(s[:, h, :], qs[0:96, 4 * kv + h, AB[b]], ks[0:96, kv, AB[b]], start=False, stop=(h == 3), skip_group_check=True)
                        last.then_inc(sa_full[b], 1)
                    pe.wait_ge(sa_free[2], 16 * q + kv + CREDIT)
                    s = sa[2][:, 0:320].rearrange("p (b k) -> p b k", b=2)
                    mm(s, identb[:, :], maskB[:, :].unsqueeze(1).broadcast_to([P, 2, 160]), start=True, stop=False, skip_group_check=True)
                    for b in range(2):
                        texts = qb[0:96, b, 4 * kv:4 * kv + 4, :].rearrange("p h q -> p (h q)")
                        mm(s[:, b, 0:128], texts, ks[0:96, kv, AB[b]], start=False, stop=False, skip_group_check=True)
                        last = mm(s[:, b, 128:160], texts, ks[0:96, kv, BB[b]], start=False, stop=(b == 1), skip_group_check=True)
                    last.then_inc(sa_full[2], 1)

                def maxima_by_head():
                    ps, f = bank("maxT", s)
                    for r in range(3):
                        pe.wait_ge(sa_free[r], 16 * q + NKV + CREDIT)
                    for b in range(2):
                        nc.tensor.transpose(ps[0:NQ, 128 * b:128 * b + 128], mxa[:, b].rearrange("p k h -> p (k h)"), ident[:, :])
                    for b in range(2):
                        last = nc.tensor.transpose(ps[0:NKV, 256 + 128 * b:384 + 128 * b], mxb[:, b, :], ident[:, :])
                    last.then_inc(f, 1)


                def gate_logits():
                    pe.wait_ge(x_ready[2], p + 1)
                    ps, f = bank("gate", s)
                    for t, cols in enumerate((A0, A1, BT)):
                        n = 64 if t == 2 else P
                        o = ps[0:n, 8 * t:8 * t + 8]
                        for k in range(KB):
                            mm(o, x2[:, 0, k, cols], wg[:, 0, k, :], start=(k == 0), stop=False)
                            mm(o, x2[:, 0, k, cols], wg[:, 1, k, :], start=False, stop=False)
                            last = mm(o, x2[:, 1, k, cols], wg[:, 0, k, :], start=False, stop=(k == KB - 1))
                    last.then_inc(f, 1)

                def routing_by_expert():
                    ps, f = bank("routT", s)
                    pe.wait_ge(rout_ready, p + 1)
                    pt = ps[0:32, 0:160].bitcast(F16)
                    for t, cols in enumerate((A0, A1, BT)):
                        n = 64 if t == 2 else P
                        last = nc.tensor.transpose(pt[:, cols], rr[0:n, t, :, :].rearrange("p a e -> p (a e)"), ident16[0:n, 0:n])
                    last.then_inc(f, 1)
                    read(pe, "routT", s)

                def in_scale(m):
                    ps, f = bank(f"in{m}", s)
                    mm(ps[:, 0:T], experts[:, 0, 128 * m:128 * m + 128], rT[:, :], start=True, stop=True).then_inc(f, 1)

                def ffn_product(m):
                    c = slice(128 * m, 128 * m + 128)
                    ps, f = bank(f"os{m}", s)
                    mm(ps[:, 0:T], experts[:, 1, c], rT[:, :], start=True, stop=True).then_inc(f, 1)
                    ps, f = bank(f"f{m}", s)
                    if m == 0:
                        pe.wait_ge(y_ready, KB * (p + 1) + CREDIT)
                    for k in range(KB):
                        mm(ps[:, 0:T], wf[:, k, c], x2[:, 0, k, :], start=(k == 0), stop=False)
                        last = mm(ps[:, 0:T], wf[:, k, c], x2[:, 1, k, :], start=False, stop=(k == KB - 1))
                    last.then_inc(f, 1)

                if s.back:
                    attention()
                for m in range(KB):
                    if s.front and m == 4:
                        average("mean1", s, 1, 1)
                    if s.front and m == 6:
                        average("var1", s, 1, 2)
                    if s.back:
                        o_product(m)
                if s.front:
                    pe.wait_ge(x_ready[1], q + 1)
                    qk_product(4)
                if s.back:
                    average("mean2", s, 2, 1)
                if s.front:
                    qk_product(0)
                    qk_product(1)
                if s.back:
                    average("var2", s, 2, 2)
                if s.front:
                    qk_product(2)
                    qk_product(3)
                if s.back:
                    gate_logits()
                if s.front:
                    maxima_scores(0)
                if s.back:
                    routing_by_expert()
                    for m in range(4):
                        in_scale(m)
                if s.front:
                    v_product(0)
                    v_product(1)
                if s.back:
                    for m in range(4, KB):
                        in_scale(m)
                if s.front:
                    v_product(2)
                for m in range(KB):
                    if s.front:
                        if m < KB - 1:
                            maxima_scores(m + 1)
                        if m == KB - 2:
                            read(pe, "v01", s)
                            read(pe, "v2", s)
                            maxima_by_head()
                    if s.back:
                        ffn_product(m)

            steps(pe, step)

        @block.scalar
        def _(act):
            A = nc.scalar.activation
            nc.scalar.preload_act_table_set("natural_log_exp_and_others")

            def step(s):
                p, q = s.p, s.q

                def squares(i, x, sq):
                    read(act, f"mean{i}", s)
                    A(sq, x, ACT.Square).then_inc(squared[i], 1)

                def rough_rstd(i, pair):
                    ps = full(act, f"var{i}", s)
                    A(rstd[:, :], ps[:, 0:T], ACT.Ln, bias=consts[:, 0:1]).then_inc(achain[i], 1)
                    act.wait_ge(achain[i], pair + 1)
                    A(rstd[:, :], rstd[:, :], ACT.Exp, scale=-0.5).then_inc(rough[i], 1)

                def high(i, pair, x, dst):
                    act.wait_ge(norm_ready[i], pair + 1)
                    A(dst[:, 0], x, ACT.Copy).then_inc(hi_made[i], 1)

                def rope_hi(n):
                    act.wait_ge(rot_ready, QKB * q + n + 1)
                    if n >= 2:
                        act.wait_ge(stacked[n - 2], 96 * (q + 1) + CREDIT)
                    else:
                        act.wait_ge(stacked[4 - n], 96 * q + CREDIT)
                    A(rt[:, n % 2, :, 0, :], rot[:, n % 2], ACT.Copy).then_inc(rot_hi, 1)

                def v_high(t):
                    ps = full(act, "v01" if t < 2 else "v2", s)
                    A(vv[:, 0, t, :, 0:HD], ps[:, 256 * (t % 2):256 * (t % 2) + 256].rearrange("p (k d) -> p k d", k=NKV),
                      ACT.Copy, scale=1.0 / XS).then_inc(v_hi, 1)

                def y_high(m):
                    read(act, f"in{m}", s)
                    A(x2[:, 0, m, :], xc[:, m, :], ACT.Copy).then_inc(y_hi, 1)

                def attention():
                    for kv in range(NKV):
                        for r in range(3):
                            c = 3 * kv + r
                            act.wait_ge(sa_full[r], 16 * p + 8 + kv + 1)
                            if kv >= 1:
                                act.wait_ge(split_ready, 24 * p + c - 2)
                            A(pf[:, r, :], sa[r][:, :], ACT.Exp, scale=fac[:, 0:1]).then_inc(sa_free[r], 1)
                    for kh in range(2):
                        for b in range(2):
                            ps = full(act, f"atA{kh}{b}", s)
                            A(x2[:, 0, 4 * kh:4 * kh + 4, AB[b]], ps[:, :].rearrange("p (h q) -> p h q", h=4), ACT.Copy).then_inc(at_hi, 1)
                    ps = full(act, "atB", s)
                    for kh in range(2):
                        A(x2[:, 0, 4 * kh:4 * kh + 4, BT].rearrange("p h (b q) -> p b h q", b=2),
                          ps[:, 256 * kh:256 * kh + 256].rearrange("p (b h q) -> p b h q", b=2, h=4), ACT.Copy).then_inc(at_hi, 1)

                if s.back:
                    attention()
                if s.front:
                    squares(1, xa, x1sq)
                    rough_rstd(1, q)
                    high(1, q, xa, x1)
                    rope_hi(0)
                if s.back:
                    squares(2, xc[:, :, :], x2sq)
                if s.front:
                    rope_hi(1)
                    rope_hi(2)
                if s.back:
                    rough_rstd(2, p)
                    high(2, p, xc[:, :, :], x2)
                if s.front:
                    rope_hi(3)
                    rope_hi(4)
                if s.back:
                    act.wait_ge(gexp_in, p + 1)
                    A(gl[:, :, :], gl[:, :, :], ACT.Exp, scale=fac[:, 2:3]).then_inc(gexp_out, 1)
                    for m in range(4):
                        y_high(m)
                if s.front:
                    v_high(0)
                    v_high(1)
                if s.back:
                    for m in range(4, KB):
                        y_high(m)
                if s.front:
                    v_high(2)
                if s.back:
                    for m in range(KB):
                        ps = full(act, f"os{m}", s)
                        if m >= 2:
                            act.wait_ge(f_done, KB * p + m - 1)
                        A(os_[:, m % 2, :], ps[:, 0:T], ACT.Copy, scale=fac[:, 3:4]).then_inc(free(f"os{m}"), 1)

            steps(act, step)

        @block.gpsimd
        def _(pool):
            g = nc.gpsimd
            for s in (*pj_free, *sa_free, po_free, stored, y_ready, *stacked):
                pool.sem_inc(s, CREDIT)
            g.memset(ks[96:98, :, :], SHIFT).then_inc(init, 1)
            pool.wait_ge(init, 1)
            g.memset(vv[:, 1], 0.0)
            g.memset(vv[:, 0, :, :, HD:HD + 1], 1.0).then_inc(init, 1)
            with pool.Fori(0, NPAIR) as p:
                for kv in range(NKV):
                    exps_done = pool.to_reg(16 * p + 8 + kv + 1 + CREDIT)
                    first_select = pool.to_reg(32 * p + 4 * kv + 3)
                    for r in range(3):
                        pool.wait_ge(init, 2)
                        pool.wait_ge(sa_free[r], exps_done)
                        if r < 2:
                            s = pf[:, r, :].rearrange("p (h q) -> p h q", h=4)
                            g.affine_select(out=s, in_=s, compare_op=ALU.is_ge, fill=0.0, base=0, pattern=[[0, 4], [1, 128]],
                                            channel_multiplier=-1).then_inc(kept, 1)
                        else:
                            s = pf[:, 2, 256:512].rearrange("p (b h q) -> p b h q", b=2, h=4)
                            g.affine_select(out=s, in_=s, compare_op=ALU.is_ge, fill=0.0, base=64, pattern=[[32, 2], [0, 4], [1, 32]],
                                            channel_multiplier=-1).then_inc(kept, 1)
                            pool.wait_ge(init, 2)
                            pool.wait_ge(kept, first_select)
                            g.affine_select(out=s, in_=s, compare_op=ALU.is_ge, fill=0.0, base=-64, pattern=[[-32, 2], [0, 4], [0, 32]],
                                            channel_multiplier=1).then_inc(kept, 1)

        @block.vector
        def _(dve):
            v = nc.vector
            OWN = {"front": 10, "back": 19}
            v.memset(gl[:, :, :], 0.0)

            def step(s):
                p, q = s.p, s.q
                n_own = {"front": 0, "back": 0}

                def own(part, ins):
                    n_own[part] += 1
                    ins.then_inc(dchain[part], 1)
                    dve.wait_ge(dchain[part], OWN[part] * (q if part == "front" else p) + n_own[part])

                def channel_sums(i, src):
                    v.tensor_reduce(sums[:, :], src.rearrange("p k t -> p t k"), AX.X, ALU.add).then_inc(sum_ready[i], 1)

                def centre(i, src, x):
                    ps = full(dve, f"mean{i}", s)
                    v.tensor_tensor(x, src, ps[:, 0:T].unsqueeze(1).broadcast_to([P, KB, T]), ALU.subtract).then_inc(free(f"mean{i}"), 1)

                def square_sums(i, pair, sq):
                    dve.wait_ge(squared[i], pair + 1)
                    channel_sums(i, sq)

                def normalise(i, pair, x):
                    part = ("front", "back")[i - 1]
                    ps = full(dve, f"var{i}", s)
                    dve.wait_ge(rough[i], pair + 1)
                    own(part, v.tensor_tensor(sums[:, :], rstd[:, :], rstd[:, :], ALU.mult))
                    v.scalar_tensor_tensor(nt[:, :], ps[:, 0:T], EPS, sums[:, :], ALU.add, ALU.mult).then_inc(free(f"var{i}"), 1)
                    read(dve, f"var{i}", s)
                    own(part, v.tensor_scalar(nt[:, :], nt[:, :], -0.5, 1.5, ALU.mult, ALU.add))
                    own(part, v.tensor_tensor(rstd[:, :], rstd[:, :], nt[:, :], ALU.mult))
                    v.scalar_tensor_tensor(x, x, XS, rstd[:, :].unsqueeze(1).broadcast_to([P, KB, T]),
                                           ALU.mult, ALU.mult).then_inc(norm_ready[i], 1)

                def low(i, pair, x, dst):
                    dve.wait_ge(hi_made[i], pair + 1)
                    v.tensor_tensor(dst[:, 1], x, dst[:, 0], ALU.subtract).then_inc(x_ready[i], 1)

                def rope_lo(n):
                    dve.wait_ge(rot_hi, QKB * q + n + 1)
                    v.tensor_tensor(rt[:, n % 2, :, 1, :], rot[:, n % 2], rt[:, n % 2, :, 0, :], ALU.subtract).then_inc(rope_ready, 1)

                def rope(n, j):
                    pa = full(dve, f"qk{j}a", s)
                    if n >= 2:
                        dve.wait_ge(rope_ready, QKB * q + n - 1)
                    if n >= 1:
                        dve.wait_ge(rot_ready, QKB * q + n)
                    v.tensor_tensor(prod[:, 0], pa[:, 0:T], cosT[:, :], ALU.mult)
                    v.tensor_tensor(prod[:, 2], pa[:, 0:T], sinT[:, :], ALU.mult).then_inc(free(f"qk{j}a"), 1)
                    pb = full(dve, f"qk{j}b", s)
                    v.tensor_tensor(prod[:, 1], pb[:, 0:T], sinT[:, :], ALU.mult)
                    v.tensor_tensor(prod[:, 3], pb[:, 0:T], cosT[:, :], ALU.mult).then_inc(free(f"qk{j}b"), 1)
                    read(dve, f"qk{j}b", s)
                    own("front", v.tensor_tensor(rot[:, n % 2, 0], prod[:, 0], prod[:, 1], ALU.subtract))
                    v.tensor_tensor(rot[:, n % 2, 1], prod[:, 2], prod[:, 3], ALU.add).then_inc(rot_ready, 1)

                def queries_of_texts(j):
                    dve.wait_ge(stacked[j + 1], 96 * (q + 1) + CREDIT)
                    v.tensor_copy(qb[0:96, :, 8 * j:8 * j + 8, :], qs[0:96, 8 * j:8 * j + 8, BT].rearrange("p h (b q) -> p b h q", b=2)).then_inc(qb_ready, 1)

                def v_low(t):
                    ps = full(dve, "v01" if t < 2 else "v2", s)
                    dve.wait_ge(v_hi, 3 * q + (2 if t < 2 else 3))
                    lo = v.scalar_tensor_tensor(vv[:, 1, t, :, 0:HD], ps[:, 256 * (t % 2):256 * (t % 2) + 256].rearrange("p (k d) -> p k d", k=NKV),
                                                1.0 / XS, vv[:, 0, t, :, 0:HD], ALU.mult, ALU.subtract)
                    if t >= 1:
                        lo.then_inc(free("v01" if t == 1 else "v2"), 1)

                def maxima(kv):
                    for b in range(2):
                        dve.wait_ge(sa_full[b], 16 * q + kv + 1)
                        v.tensor_reduce(mxa[:, b, kv, :], sa[b][:, :].rearrange("p (h k) -> p h k", h=4), AX.X, ALU.max).then_inc(sa_free[b], 1)
                    dve.wait_ge(sa_full[2], 16 * q + kv + 1)
                    v.tensor_reduce(mxb[:, :, kv], sa[2][:, 0:320].rearrange("p (b k) -> p b k", b=2), AX.X, ALU.max).then_inc(sa_free[2], 1)

                def maxima_split():
                    ps = full(dve, "maxT", s)
                    areas = ((NQ, slice(0, 256)), (NKV, slice(256, 512)))
                    for rows, cols in areas:
                        own("front", v.tensor_scalar(mt[0:rows, 0, cols], ps[0:rows, cols], -1.0 / SHIFT, None, ALU.mult))
                    for rows, cols in areas:
                        lo = v.scalar_tensor_tensor(mt[0:rows, 1, cols], ps[0:rows, cols], -1.0 / SHIFT, mt[0:rows, 0, cols], ALU.mult, ALU.subtract)
                    lo.then_inc(free("maxT"), 1)

                def attention_out(kv):
                    dve.wait_ge(po_full, NKV * p + kv + 1)
                    o = po[:, 0:330].rearrange("p (n d) -> p n d", n=10)
                    own("back", v.reciprocal(rsum[:, :].unsqueeze(2), o[:, :, HD:HD + 1]))
                    v.tensor_tensor(att[:, :, kv, :], o[:, :, 0:HD], rsum[:, :].unsqueeze(2).broadcast_to([P, 10, HD]), ALU.mult).then_inc(po_free, 1)

                def attention():
                    for kv in range(NKV):
                        for r in range(3):
                            c = 3 * kv + r
                            dve.wait_ge(kept, 32 * p + 4 * kv + (r + 1 if r < 2 else 4))
                            if kv >= 1:
                                if r < 2:
                                    dve.wait_ge(split_used, 16 * p + 2 * (kv - 1) + r + 1)
                                else:
                                    dve.wait_ge(po_full, NKV * p + kv)
                            v.tensor_copy(ph[:, 0, r, :], pf[:, r, :]).then_inc(split_hi, 1)
                            dve.wait_ge(split_hi, 24 * p + c + 1)
                            v.tensor_tensor(ph[:, 1, r, :], pf[:, r, :], ph[:, 0, r, :], ALU.subtract).then_inc(split_ready, 1)
                        if kv >= 1:
                            attention_out(kv - 1)
                    attention_out(NKV - 1)
                    for n, (kh, b) in enumerate(((0, 0), (0, 1), (1, 0), (1, 1))):
                        ps = full(dve, f"atA{kh}{b}", s)
                        dve.wait_ge(at_hi, 6 * p + n + 1)
                        v.tensor_tensor(x2[:, 1, 4 * kh:4 * kh + 4, AB[b]], ps[:, :].rearrange("p (h q) -> p h q", h=4),
                                        x2[:, 0, 4 * kh:4 * kh + 4, AB[b]], ALU.subtract).then_inc(free(f"atA{kh}{b}"), 1)
                    ps = full(dve, "atB", s)
                    dve.wait_ge(at_hi, 6 * (p + 1))
                    for kh in range(2):
                        lo = v.tensor_tensor(x2[:, 1, 4 * kh:4 * kh + 4, BT].rearrange("p h (b q) -> p b h q", b=2),
                                             ps[:, 256 * kh:256 * kh + 256].rearrange("p (b h q) -> p b h q", b=2, h=4),
                                             x2[:, 0, 4 * kh:4 * kh + 4, BT].rearrange("p h (b q) -> p b h q", b=2), ALU.subtract)
                    lo.then_inc(free("atB"), 1)

                def residual(m):
                    if m == 0:
                        dve.wait_ge(res_loaded, 32 * (p + 1))
                    ps = full(dve, f"o{m}", s)
                    v.scalar_tensor_tensor(h2[:, m, :], ps[:, 0:T], fac[:, 1:2], h2[:, m, :], ALU.mult, ALU.add).then_inc(free(f"o{m}"), 1)

                def routing():
                    ps = full(dve, "gate", s)
                    own("back", v.tensor_copy(gl[:, 0:2, :], ps[:, 0:16].rearrange("p (t e) -> p t e", t=2)))
                    v.tensor_copy(gl[0:64, 2, :], ps[0:64, 16:24]).then_inc(free("gate"), 1)
                    read(dve, "gate", s)
                    own("back", v.tensor_reduce(g1[:, :, :], gl[:, :, :], AX.X, ALU.max))
                    v.tensor_tensor(gl[:, :, :], gl[:, :, :], g1[:, :, :].broadcast_to([P, 3, EXPERTS]), ALU.subtract).then_inc(gexp_in, 1)
                    dve.wait_ge(gexp_out, p + 1)
                    own("back", v.tensor_reduce(g1[:, :, :], gl[:, :, :], AX.X, ALU.add))
                    own("back", v.reciprocal(g1[:, :, :], g1[:, :, :]))
                    own("back", v.tensor_tensor(gl[:, :, :], gl[:, :, :], g1[:, :, :].broadcast_to([P, 3, EXPERTS]), ALU.mult))
                    own("back", v.tensor_copy(rr[:, :, 0, :], gl[:, :, :]))
                    own("back", v.tensor_copy(rr[:, :, 2, :], gl[:, :, :]))
                    own("back", v.tensor_tensor(rr[:, :, 1, :], gl[:, :, :], rr[:, :, 0, :], ALU.subtract))
                    v.tensor_tensor(rr[:, :, 3, :], gl[:, :, :], rr[:, :, 0, :], ALU.subtract).then_inc(rout_ready, 1)
                    ps = full(dve, "routT", s)
                    v.tensor_copy(rT[:, :], ps[0:32, 0:160].bitcast(F16)).then_inc(free("routT"), 1)

                def y_lo(m):
                    dve.wait_ge(y_hi, KB * p + m + 1)
                    v.tensor_tensor(x2[:, 1, m, :], xc[:, m, :], x2[:, 0, m, :], ALU.subtract).then_inc(y_ready, 1)

                def scaled_in(m):
                    ps = full(dve, f"in{m}", s)
                    v.tensor_tensor(xc[:, m, :], ps[:, 0:T], xc[:, m, :], ALU.mult).then_inc(free(f"in{m}"), 1)

                def ffn_out(m):
                    read(dve, f"os{m}", s)
                    ps = full(dve, f"f{m}", s)
                    v.tensor_tensor(os_[:, m % 2, :], ps[:, 0:T], os_[:, m % 2, :], ALU.mult).then_inc(free(f"f{m}"), 1)
                    read(dve, f"f{m}", s)
                    v.scalar_tensor_tensor(h2[:, m, :], os_[:, m % 2, :], bias[:, m:m + 1], h2[:, m, :], ALU.add, ALU.add).then_inc(f_done, 1)

                def back(part, *args):
                    if s.back:
                        part(*args)

                def front(part, *args):
                    if s.front:
                        part(*args)

                back(attention)
                back(residual, 0)
                back(residual, 1)
                if s.front:
                    dve.wait_ge(h_loaded, 32 * (q + 1))
                front(channel_sums, 1, xa)
                back(residual, 2)
                back(residual, 3)
                front(centre, 1, xa, xa)
                back(residual, 4)
                front(square_sums, 1, q, x1sq)
                back(residual, 5)
                front(normalise, 1, q, xa)
                back(residual, 6)
                front(low, 1, q, xa, x1)
                back(residual, 7)
                if s.back:
                    read(dve, "o7", s)
                back(channel_sums, 2, h2[:, :, :])
                front(rope, 0, 4)
                back(centre, 2, h2[:, :, :], xc[:, :, :])
                front(rope, 1, 0)
                front(rope_lo, 0)
                back(square_sums, 2, p, x2sq)
                front(rope, 2, 1)
                front(rope_lo, 1)
                back(normalise, 2, p, xc[:, :, :])
                front(rope, 3, 2)
                front(rope_lo, 2)
                back(low, 2, p, xc[:, :, :], x2)
                front(rope, 4, 3)
                front(rope_lo, 3)
                front(rope_lo, 4)
                front(queries_of_texts, 0)
                back(routing)
                front(queries_of_texts, 1)
                for m in range(4):
                    back(scaled_in, m)
                    if m >= 1:
                        back(y_lo, m - 1)
                front(maxima, 0)
                back(y_lo, 3)
                for m in range(4, KB):
                    if m == KB - 1:
                        front(v_low, 0)
                        front(v_low, 1)
                    back(scaled_in, m)
                    if m >= 5:
                        back(y_lo, m - 1)
                back(y_lo, KB - 1)
                front(v_low, 2)
                front(queries_of_texts, 2)
                front(queries_of_texts, 3)
                for m in range(KB):
                    if m < KB - 1:
                        front(maxima, m + 1)
                    if m == KB - 2:
                        front(maxima_split)
                    back(ffn_out, m)
                assert not s.front or n_own["front"] == OWN["front"], n_own
                assert not s.back or n_own["back"] == OWN["back"], n_own

            steps(dve, step)


def fusion_kernel(nc, D, out_d):
    h_d = nc.dram_tensor("tok_result", (NPAIR, P, IH, 2, HEADS), F32, kind="Internal").ap()
    s4d_block(nc, D["par"], D["xr"], D["xi"], D["digit"], D["phase"], h_d)
    rest(nc, D, h_d, out_d)


def kernel(x, txt, L0_tok_log_dt, L0_tok_B, L0_tok_inv_A_real, L0_tok_A_imag, L0_attn_Wq, L0_attn_Wk, L0_attn_Wv,
           L0_attn_Wo, L0_ffn_weight, L0_ffn_bias, L0_ffn_gate_w, L0_ffn_in_channel_scale, L0_ffn_out_channel_scale):
    import concourse.bacc as _bacc
    from concourse.bass_utils import run_bass_kernel_spmd as _run

    def twice(a):
        return np.concatenate([a, a], 0)

    def blocks(w, rows=None):
        w = w if rows is None else w[rows]
        return w.reshape(KB, P, -1).transpose(1, 0, 2)

    x, txt = np.asarray(x), np.asarray(txt)
    log_dt, B, inv_a, a_im = (np.asarray(a) for a in (L0_tok_log_dt, L0_tok_B, L0_tok_inv_A_real, L0_tok_A_imag))
    wq, wk, wv, wo, wf, wb, wg, ics, ocs = (np.asarray(a) for a in (
        L0_attn_Wq, L0_attn_Wk, L0_attn_Wv, L0_attn_Wo, L0_ffn_weight, L0_ffn_bias, L0_ffn_gate_w,
        L0_ffn_in_channel_scale, L0_ffn_out_channel_scale))
    arrays = {}
    arrays["par"] = np.stack([np.tile(log_dt, (P, 1)), twice(inv_a.T), twice(a_im.T), twice(B[..., 0].T), twice(B[..., 1].T)], 1)
    arrays["xr"] = twice(x[..., 0].transpose(2, 1, 0))
    arrays["xi"] = twice(x[..., 1].transpose(2, 1, 0))
    arrays["txt"] = txt.reshape(NPAIR, 2, 32, KB, P).transpose(0, 4, 3, 1, 2).reshape(NPAIR, P, KB, 64)
    j, a, i, h = np.meshgrid(np.arange(4), np.arange(2), np.arange(16), np.arange(8), indexing="ij")
    cols = ((8 * j + h) * HD + 2 * i + a).reshape(-1)
    arrays["wq"] = blocks(wq[:, cols])
    arrays["wk"] = blocks(wk[:, cols[:256]])
    arrays["wv"] = blocks(wv)
    g, hh, kv, d = np.meshgrid(np.arange(2), np.arange(4), np.arange(4), np.arange(HD), indexing="ij")
    arrays["wo"] = blocks(wo, (((4 * g + kv) * 4 + hh) * HD + d).reshape(-1))
    arrays["wf"] = blocks(wf.T)
    arrays["wg"] = blocks(wg.T)
    arrays["we"] = np.stack([np.tile(ics, (4, 1)), np.tile(ocs, (4, 1))], 1)
    arrays["bias"] = wb.reshape(KB, P).T
    arrays["digit"] = np.tile(np.concatenate([np.arange(JL), JL * np.arange(IH)]).astype(np.float32), (P, 1))
    phase = np.zeros((P, 4), np.float32)
    phase[:MODES, 0], phase[:MODES, 1], phase[:, 3] = 0.25, 0.25 * TURN, 0.25 * TURN
    arrays["phase"] = phase
    inv_freq = (1.0 / np.float32(10000.0) ** (np.arange(0, HD, 2, dtype=np.float32) / HD)).astype(np.float32)
    pos = np.concatenate([np.arange(128), np.arange(128), np.arange(128, 160), np.arange(128, 160)]).astype(np.float32)
    ang = np.repeat(inv_freq, 8)[:, None] * pos[None]
    arrays["cos"] = (np.cos(ang) / XS).astype(np.float32)
    arrays["sin"] = (np.sin(ang) / XS).astype(np.float32)
    never = np.float32(-3e38)
    r = np.arange(P)
    mask_b = np.zeros((P, 160), np.float32)
    mask_b[:, 128:] = np.where(np.arange(32)[None] > (r % 32)[:, None], never, 0)
    arrays["masks"] = np.concatenate([np.eye(P, dtype=np.float32), np.full((P, P), 1.0 / DIM, np.float32),
                                      np.where(r[None] > r[:, None], never, 0).astype(np.float32), mask_b], 1)
    consts = np.zeros((P, 8), np.float32)
    consts[:, 0], consts[:16, 1], consts[16:32, 2] = EPS, 1, 1
    arrays["consts"] = consts

    nc = _bacc.Bacc("TRN2", target_bir_lowering=False, num_devices=1)
    feed, D = {}, {}
    for name, value in arrays.items():
        value = np.ascontiguousarray(value)
        feed[f"in_{name}"] = value
        D[name] = nc.dram_tensor(f"in_{name}", value.shape, F32, kind="ExternalInput").ap()
    out_d = nc.dram_tensor("out_0", (NPAIR, P, KB, T), F32, kind="ExternalOutput").ap()
    fusion_kernel(nc, D, out_d)
    got = _run(nc, [feed], core_ids=[0]).results[0]["out_0"]
    got = np.asarray(got).transpose(0, 3, 2, 1).reshape(NPAIR, T, DIM)
    s4 = got[:, :256].reshape(CH, P, DIM)
    text = got[:, 256:].reshape(CH, 32, DIM)
    return np.concatenate([s4, text], 1)
```

```python
import concourse.bass as bass
from concourse import mybir
from contextlib import ExitStack
import numpy as np

F32 = mybir.dt.float32
F16 = mybir.dt.float16
BF16 = mybir.dt.bfloat16
I32 = mybir.dt.int32
ALU = mybir.AluOpType
ACT = mybir.ActivationFunctionType
AX = mybir.AxisListType

P = 128
HEADS = 128
CH = 16
MODES = 64
LEN = 1024
JL = 128
IH = LEN // JL
ROUND = 12582912.0
TURN = 6.283184
HC = 8


def s4d_block(nc, par_d, xr_d, xi_d, digit_d, phase_d, h_d):
    with ExitStack() as ctx:
        def sb(name, shape, dt=F32):
            return ctx.enter_context(nc.sbuf_tensor(name, shape, dt))

        def sem(name):
            return ctx.enter_context(nc.semaphore(name))

        par = sb("s4_par", [P, 5, HEADS])
        xr = sb("s4_xr", [P, HEADS, CH])
        xi = sb("s4_xi", [P, HEADS, CH])
        digit = sb("s4_digit", [P, JL + IH])
        phase = sb("s4_phase", [P, 4])
        dtea = sb("s4_dtea", [P, 2, HEADS])
        dt_, ea = dtea[:, 0, :], dtea[:, 1, :]
        decay = sb("s4_decay", [P, HEADS])
        turns = sb("s4_turns", [P, HEADS])
        ez = sb("s4_ez", [P, HEADS])
        small = sb("s4_small", [P, 12, HEADS])
        smalli = sb("s4_smalli", [P, 2, HEADS], I32)
        pamp = sb("s4_pamp", [P, HEADS, IH])
        y1 = sb("s4_y1", [P, HEADS, IH])
        y2 = sb("s4_y2", [P, HEADS, IH])
        low = sb("s4_low", [P, HEADS, JL])
        whole = sb("s4_whole", [P, HC, JL])
        ang = sb("s4_ang", [P, 2, HC, JL])
        lowp = sb("s4_lowp", [P, 2, HC, JL])
        g1 = sb("s4_g1", [P, 2, HC, IH, CH])
        g2 = sb("s4_g2", [P, 2, HC, IH, CH])
        ptmp = g1[:, :, :, :, :].rearrange("p s h i c -> p (s h i c)").rearrange("p (a h i) -> p a h i", a=2, i=IH)
        pang = g2[:, :, :, :, :].rearrange("p s h i c -> p (s h i c)").rearrange("p (a h i) -> p a h i", a=2, i=IH)
        hall = sb("s4_hall", [P, IH * CH, HEADS])
        ps = [[ctx.enter_context(nc.psum_tensor(f"s4_ps{s}{b}", [P, 4, P], F32)) for b in range(2)] for s in range(2)]

        loaded, loaded_x = sem("s4_loaded"), sem("s4_loaded_x")
        chain = sem("s4_chain")
        expo_in, expo_out = sem("s4_expo_in"), sem("s4_expo_out")
        low_amp = sem("s4_low_amp")
        trig_in, trig_out = sem("s4_trig_in"), sem("s4_trig_out")
        y_ready, low_product = sem("s4_y_ready"), sem("s4_low_product")
        whole_ready, ang_rounded, ang_in, ang_out = sem("s4_whole_ready"), sem("s4_ang_rounded"), sem("s4_ang_in"), sem("s4_ang_out")
        gr_ready, gi_ready, g_ready, low_ready = sem("s4_gr_ready"), sem("s4_gi_ready"), sem("s4_g_ready"), sem("s4_low_ready")
        multiplied, copied = sem("s4_multiplied"), sem("s4_copied")
        stored = sem("s4_stored")
        block = ctx.enter_context(nc.Block())
        NCHUNK = HEADS // HC
        FREE = 2

        @block.sync
        def _(sp):
            sp.dma_start(par[:, :, :], par_d).then_inc(loaded, 16)
            sp.dma_start(digit[:, :], digit_d).then_inc(loaded, 16)
            sp.dma_start(phase[:, :], phase_d).then_inc(loaded, 16)
            sp.dma_start(xr[:, :, :], xr_d).then_inc(loaded_x, 16)
            sp.dma_start(xi[:, :, :], xi_d).then_inc(loaded_x, 16)
            for half in range(2):
                sp.wait_ge(copied, NCHUNK // 2 * (half + 1) + FREE)
                heads = slice(HEADS // 2 * half, HEADS // 2 * (half + 1))
                for pr in range(CH // 2):
                    for b in range(2):
                        sp.dma_start(h_d[pr, :, :, b, heads], hall[:, 2 * pr + b:IH * CH:CH, heads]).then_inc(stored, 16)
            sp.wait_ge(stored, 2 * 16 * CH)

        @block.vector
        def _(dve):
            done = [0]

            def link(ins):
                done[0] += 1
                ins.then_inc(chain, 1)
                dve.wait_ge(chain, done[0])

            v = nc.vector
            t = [small[:, k, :] for k in range(12)]

            def exact_exp(out, x, n):
                a, b, c = (small[:, n * k:n * k + n, :] for k in range(3))
                link(v.tensor_scalar(a, x, 88.0, -87.0, ALU.min, ALU.max))
                link(v.tensor_scalar(b, a, 1.4426950408889634, ROUND, ALU.mult, ALU.add))
                link(v.tensor_scalar(b, b, ROUND, None, ALU.subtract))
                link(v.scalar_tensor_tensor(a, b, -0.693145751953125, a, ALU.mult, ALU.add))
                link(v.scalar_tensor_tensor(a, b, -1.42860682030941723e-6, a, ALU.mult, ALU.add))
                link(v.tensor_scalar(c, a, 1.0 / 5040, None, ALU.mult))
                for k in (720, 120, 24, 6, 2, 1):
                    link(v.scalar_tensor_tensor(c, c, 1.0 / k, a, ALU.add, ALU.mult))
                link(v.tensor_scalar(c, c, 1.0, None, ALU.add))
                link(v.tensor_scalar(b, b, 127.0, 8388608.0, ALU.add, ALU.mult))
                link(v.tensor_copy(smalli[:, 0:n, :], b))
                link(v.tensor_tensor(out, c, smalli[:, 0:n, :].bitcast(F32), ALU.mult))

            dve.wait_ge(loaded, 48)
            exact_exp(dtea[:, :, :], par[:, 0:2, :], 2)
            link(v.scalar_tensor_tensor(decay[:, :], ea, -1.0, dt_, ALU.mult, ALU.mult))
            v.tensor_tensor(pamp[:, :, :], decay[:, :].unsqueeze(2).broadcast_to([P, HEADS, IH]),
                            digit[:, JL:].unsqueeze(1).broadcast_to([P, HEADS, IH]), ALU.mult).then_inc(expo_in, 1)
            link(v.tensor_tensor(turns[:, :], par[:, 2, :], dt_, ALU.mult))
            link(v.tensor_scalar(turns[:, :], turns[:, :], float(1 / (2 * np.pi)), None, ALU.mult))
            link(v.tensor_scalar(t[3], turns[:, :], ROUND, None, ALU.add))
            link(v.scalar_tensor_tensor(t[3], t[3], ROUND, turns[:, :], ALU.subtract, ALU.subtract))
            link(v.tensor_scalar(turns[:, :], t[3], -1.0, None, ALU.mult))

            def fraction(out, y, shift):
                link(v.tensor_scalar(out, y, shift, ROUND, ALU.add, ALU.add))
                return v.scalar_tensor_tensor(out, out, ROUND, y, ALU.subtract, ALU.subtract)

            fraction(t[4], turns[:, :], 0.0).then_inc(trig_in, 1)
            fraction(t[5], turns[:, :], 0.25).then_inc(trig_in, 1)
            link(v.tensor_tensor(ptmp[:, 0, :, :], turns[:, :].unsqueeze(2).broadcast_to([P, HEADS, IH]),
                                 digit[:, JL:].unsqueeze(1).broadcast_to([P, HEADS, IH]), ALU.mult))
            fraction(pang[:, 0, :, :], ptmp[:, 0, :, :], 0.0).then_inc(trig_in, 1)
            fraction(pang[:, 1, :, :], ptmp[:, 0, :, :], 0.25).then_inc(trig_in, 1)
            exact_exp(ez[:, :].unsqueeze(1), decay[:, :].unsqueeze(1), 1)
            link(v.tensor_tensor(t[6], ea, ea, ALU.mult))
            link(v.tensor_tensor(t[7], par[:, 2, :], par[:, 2, :], ALU.mult))
            link(v.tensor_tensor(t[6], t[6], t[7], ALU.add))
            link(v.reciprocal(t[6], t[6]))

            dve.wait_ge(trig_out, 2)
            zr, zi, br, bi = t[8], t[9], par[:, 3, :], par[:, 4, :]
            link(v.tensor_tensor(zr, ez[:, :], t[5], ALU.mult))
            link(v.tensor_tensor(zi, ez[:, :], t[4], ALU.mult))
            link(v.tensor_scalar(zr, zr, 1.0, None, ALU.subtract))
            link(v.tensor_tensor(t[0], br, zr, ALU.mult))
            link(v.tensor_tensor(t[1], bi, zi, ALU.mult))
            link(v.tensor_tensor(t[10], t[0], t[1], ALU.subtract))
            link(v.tensor_tensor(t[0], br, zi, ALU.mult))
            link(v.tensor_tensor(t[1], bi, zr, ALU.mult))
            link(v.tensor_tensor(t[11], t[0], t[1], ALU.add))
            link(v.tensor_tensor(t[0], t[11], par[:, 2, :], ALU.mult))
            link(v.tensor_tensor(t[1], t[10], ea, ALU.mult))
            link(v.tensor_tensor(t[0], t[0], t[1], ALU.subtract))
            link(v.scalar_tensor_tensor(t[8], t[0], 2.0, t[6], ALU.mult, ALU.mult))
            link(v.tensor_tensor(t[0], t[11], ea, ALU.mult))
            link(v.tensor_tensor(t[1], t[10], par[:, 2, :], ALU.mult))
            link(v.tensor_tensor(t[0], t[0], t[1], ALU.add))
            link(v.scalar_tensor_tensor(t[9], t[0], -2.0, t[6], ALU.mult, ALU.mult))
            dve.wait_ge(trig_out, 4)
            dve.wait_ge(expo_out, 1)
            fr = t[8].unsqueeze(2).broadcast_to([P, HEADS, IH])
            fi = t[9].unsqueeze(2).broadcast_to([P, HEADS, IH])
            psin, pcos = pang[:, 0, :, :], pang[:, 1, :, :]
            link(v.tensor_tensor(psin, psin, pamp[:, :, :], ALU.mult))
            link(v.tensor_tensor(pcos, pcos, pamp[:, :, :], ALU.mult))
            a, b = ptmp[:, 0, :, :], ptmp[:, 1, :, :]
            link(v.tensor_tensor(a, pcos, fr, ALU.mult))
            link(v.tensor_tensor(b, psin, fi, ALU.mult))
            link(v.tensor_tensor(y1[0:MODES, :, :], a[0:MODES], b[0:MODES], ALU.subtract))
            link(v.tensor_tensor(y2[MODES:P, :, :], b[MODES:P], a[MODES:P], ALU.subtract))
            link(v.tensor_tensor(a, pcos, fi, ALU.mult))
            link(v.tensor_tensor(b, psin, fr, ALU.mult))
            link(v.tensor_tensor(a, a, b, ALU.add))
            link(v.tensor_scalar(y2[0:MODES, :, :], a[0:MODES], -1.0, None, ALU.mult))
            v.tensor_scalar(y1[MODES:P, :, :], a[MODES:P], -1.0, None, ALU.mult).then_inc(y_ready, 1)
            dve.wait_ge(y_ready, 1)
            dve.wait_ge(loaded_x, 32)

            def angle(q, s):
                dve.wait_ge(whole_ready, q + 1)
                dve.wait_ge(low_ready, q + 1)
                v.tensor_scalar(ang[:, s], whole[:, :, :], phase[:, 0:1], ROUND, ALU.add, ALU.add).then_inc(ang_rounded, 1)
                dve.wait_ge(ang_rounded, q + 1)
                v.scalar_tensor_tensor(ang[:, s], ang[:, s], ROUND, whole[:, :, :], ALU.subtract, ALU.subtract).then_inc(ang_in, 1)

            def operands(q, s):
                hs = bass.ds(q * HC, HC)
                dve.wait_ge(multiplied, q + 1)
                v.tensor_tensor(g1[:, s], xr[:, hs, :].unsqueeze(2).broadcast_to([P, HC, IH, CH]),
                                y1[:, hs, :].unsqueeze(3).broadcast_to([P, HC, IH, CH]), ALU.mult).then_inc(gr_ready, 1)
                dve.wait_ge(gr_ready, q + 1)
                dve.wait_ge(gi_ready, q + 1)
                v.tensor_tensor(g1[:, s], g1[:, s], g2[:, s], ALU.add).then_inc(g_ready, 1)
                dve.wait_ge(ang_out, q + 1)
                v.tensor_tensor(lowp[:, s], low[:, hs, :], ang[:, s], ALU.mult).then_inc(low_ready, 1)

            angle(0, 0)
            with dve.Fori(0, NCHUNK // 2 - 1) as it:
                for s in range(2):
                    angle(2 * it + s + 1, 1 - s)
                    operands(2 * it + s, s)
            angle(NCHUNK - 1, 1)
            for s in range(2):
                operands(NCHUNK - 2 + s, s)

        @block.gpsimd
        def _(pool):
            for s in (ang_in, g_ready, low_ready, multiplied, copied):
                pool.sem_inc(s, FREE)
            pool.wait_ge(expo_in, 1)
            half = slice(HEADS // 2, HEADS)
            nc.gpsimd.tensor_tensor(low[:, half, :], decay[:, half].unsqueeze(2).broadcast_to([P, HEADS // 2, JL]),
                                    digit[:, 0:JL].unsqueeze(1).broadcast_to([P, HEADS // 2, JL]), ALU.mult).then_inc(low_product, 1)
            pool.wait_ge(y_ready, 1)
            pool.wait_ge(loaded_x, 32)
            with pool.Fori(0, NCHUNK // 2) as it:
                for s in range(2):
                    q = 2 * it + s
                    hs = bass.ds(q * HC, HC)
                    pool.wait_ge(ang_in, q + FREE)
                    nc.gpsimd.tensor_tensor(whole[:, :, :], turns[:, hs].unsqueeze(2).broadcast_to([P, HC, JL]),
                                            digit[:, 0:JL].unsqueeze(1).broadcast_to([P, HC, JL]), ALU.mult).then_inc(whole_ready, 1)
                    pool.wait_ge(g_ready, q + 1)
                    nc.gpsimd.tensor_tensor(g2[:, s], xi[:, hs, :].unsqueeze(2).broadcast_to([P, HC, IH, CH]),
                                            y2[:, hs, :].unsqueeze(3).broadcast_to([P, HC, IH, CH]), ALU.mult).then_inc(gi_ready, 1)

        @block.scalar
        def _(act):
            s_ = nc.scalar
            act.wait_ge(expo_in, 1)
            s_.activation(pamp[:, :, :], pamp[:, :, :], ACT.Exp).then_inc(expo_out, 1)

            def low_amplitudes(first, heads):
                with act.Fori(first // 4, (first + heads) // 4) as it:
                    for k in range(4):
                        s_.activation(low[:, bass.ds(4 * it + k, 1), :], digit[:, 0:JL].unsqueeze(1), ACT.Exp,
                                      scale=decay[:, bass.ds(4 * it + k, 1)]).then_inc(low_amp, 1)

            low_amplitudes(0, HEADS // 4)
            act.wait_ge(trig_in, 4)
            for k, tile in enumerate((small[:, 4, :], small[:, 5, :], pang[:, 0, :, :], pang[:, 1, :, :])):
                if k % 2:
                    s_.activation(tile, tile, ACT.Sin, scale=-TURN, bias=phase[:, 3:4]).then_inc(trig_out, 1)
                else:
                    s_.activation(tile, tile, ACT.Sin, scale=-TURN).then_inc(trig_out, 1)
            low_amplitudes(HEADS // 4, HEADS // 4)
            act.wait_ge(low_product, 1)
            s_.activation(low[:, HEADS // 2:, :], low[:, HEADS // 2:, :], ACT.Exp).then_inc(low_amp, 1)

            def sines(q, s):
                act.wait_ge(ang_in, q + 1 + FREE)
                s_.activation(ang[:, s], ang[:, s], ACT.Sin, scale=-TURN, bias=phase[:, 1:2]).then_inc(ang_out, 1)

            def copy_out(q, s):
                act.wait_ge(multiplied, q + 1 + FREE)
                for b in range(2):
                    last = s_.copy(hall[:, :, bass.ds(q * HC + 4 * b, 4)], ps[s][b][:, :, :].rearrange("p h c -> p c h"))
                last.then_inc(copied, 1)

            sines(0, 0)
            with act.Fori(0, NCHUNK // 2 - 1) as it:
                for s in range(2):
                    sines(2 * it + s + 1, 1 - s)
                    copy_out(2 * it + s, s)
            sines(NCHUNK - 1, 1)
            for s in range(2):
                copy_out(NCHUNK - 2 + s, s)

        @block.tensor
        def _(pe):
            with pe.Fori(0, NCHUNK // 2) as it:
                for s in range(2):
                    q = 2 * it + s
                    pe.wait_ge(low_ready, q + 1 + FREE)
                    pe.wait_ge(copied, q + 1)
                    for k in range(HC):
                        last = nc.tensor.matmul(ps[s][k // 4][:, k % 4, :], lowp[:, s, k, :],
                                                g1[:, s, k].rearrange("p i c -> p (i c)"), start=True, stop=True)
                    last.then_inc(multiplied, 1)

DIM, T, NPAIR, KB = 1024, 320, 8, 8
NQ, NKV, HD = 32, 8, 32
EXPERTS = 8
EPS = 1e-5
XS = 32.0
SHIFT = 4096.0
QKB = 5
A0, A1, BT = slice(0, 128), slice(128, 256), slice(256, 320)

FRONT = ["mean1", "var1", *(f"qk{j}{ab}" for j in (4, 0, 1, 2, 3) for ab in "ab"), "v01", "v2", "maxT"]
USES = ("pv0 pv1 pv2 pv3 pv4 pv5 pv6 atA00 atA01 pv7 atA10 atA11 atB mean1 o0 o1 o2 o3 o4 var1 o5 o6 o7 qk4a mean2 qk4b qk0a qk0b var2 qk1a qk1b "
        "qk2a qk2b gate qk3a qk3b routT in0 in1 in2 in3 v01 in4 in5 in6 in7 v2 os0 f0 os1 f1 os2 f2 os3 f3 os4 f4 "
        "maxT os5 f5 os6 f6 os7 f7").split()
BANKS = 4
FIRST_SUM = NKV - KB // 2
HALVES = (slice(0, KB // 2), slice(KB // 2, KB))
CREDIT = 1
assert len(USES) % BANKS == 0
TURNS = len(USES) // BANKS


class Step:

    def __init__(self, p, back=True, front=True):
        self.p, self.q, self.back, self.front = p, p + 1, back, front

    def use(self, name):
        at = USES.index(name)
        b = at % BANKS
        here = [n for k, n in enumerate(USES) if k < at and k % BANKS == b]
        front_uses = sum(USES.index(n) % BANKS == b for n in FRONT)
        if not self.back:
            return b, sum(n in FRONT for n in here)
        if not self.front:
            here = [n for n in here if n not in FRONT]
        return b, self.p * TURNS + front_uses + len(here)


def rest(nc, D, h_d, out_d):
    with ExitStack() as ctx:
        def sb(name, shape, dt=F32):
            return ctx.enter_context(nc.sbuf_tensor(name, shape, dt))

        def sem(name):
            return ctx.enter_context(nc.semaphore(name))

        wqk = sb("wqk", [P, 2, KB, QKB * 256], F16)
        wv = sb("wv", [P, 2, KB, 256], F16)
        wo = sb("wo", [P, 2, KB, DIM], F16)
        wf = sb("wf", [P, KB, DIM], F16)
        wg = sb("wg", [P, 2, KB, EXPERTS], F16)
        experts = sb("experts", [4 * EXPERTS, 2, DIM], F16)
        inv = sb("inv", [P, 8])
        fac = sb("fac", [P, 8])
        bias = sb("bias", [P, KB])
        cosT, sinT = sb("cosT", [P, T]), sb("sinT", [P, T])
        ident = sb("ident", [P, P])
        ident16 = sb("ident16", [P, P], F16)
        identb = sb("identb", [P, P], BF16)
        maskA = sb("maskA", [P, P], BF16)
        maskB = sb("maskB", [P, 32], BF16)
        maskK = sb("maskK", [P, P + 64], BF16)
        avg = sb("avg", [P, P])
        consts = sb("consts", [P, 8])
        weights_block(nc, D, locals())
        pairs_block(nc, D, h_d, out_d, locals())


def weights_block(nc, D, W):
    with ExitStack() as ctx:
        def sb(name, shape, dt=F32):
            return ctx.enter_context(nc.sbuf_tensor(name, shape, dt))

        def sem(name):
            return ctx.enter_context(nc.semaphore(name))

        raw = sb("raw", [P, KB, 1024])
        rawkv = sb("rawkv", [P, KB, 512])
        rawo = sb("rawo", [P, KB, 1024])
        rawg = sb("rawg", [P, KB, EXPERTS])
        rawe = sb("rawe", [4 * EXPERTS, 2, DIM])
        emask = sb("emask", [P, 4 * P + 32 + 64])
        mx = sb("wl_largest", [P, 8])
        mxa = sb("wl_largest_all", [P, 8])
        scale = sb("scale", [P, 8])
        ehi = sb("ehi", [4 * EXPERTS, 2, DIM], F16)
        elo = sb("elo", [4 * EXPERTS, 2, DIM], F16)
        wqk, wv, wo, wf, wg, experts, inv, fac = (W[n] for n in ("wqk", "wv", "wo", "wf", "wg", "experts", "inv", "fac"))
        consts = W["consts"]
        ld_c, ld_kv, ld_o, ld_f, ld_e = (sem(f"wl_{name}") for name in ("const", "wkv", "wo", "wf", "experts"))
        ld_q = [sem("wl_wq0"), sem("wl_wq1")]
        mxq = sb("wl_largest_q", [P, 2])
        chain, mx_ready, all_ready = sem("wl_chain"), sem("wl_mx"), sem("wl_all")
        sc_ready, hi_ready, lo_ready, sign_ready = sem("wl_scale"), sem("wl_hi"), sem("wl_lo"), sem("wl_sign")
        block = ctx.enter_context(nc.Block())

        @block.sync
        def _(sp):
            for half in range(2):
                blocks = slice(KB // 2 * half, KB // 2 * (half + 1))
                sp.dma_start(raw[:, blocks, :], D["wq"][:, blocks, :]).then_inc(ld_q[half], 16)
            sp.dma_start(rawkv[:, :, 0:256], D["wk"]).then_inc(ld_kv, 16)
            sp.dma_start(rawkv[:, :, 256:512], D["wv"]).then_inc(ld_kv, 16)
            sp.dma_start(rawg[:, :, :], D["wg"]).then_inc(ld_e, 16)
            sp.dma_start(rawe[:, :, :], D["we"]).then_inc(ld_e, 16)
            sp.dma_start(consts[:, :], D["consts"]).then_inc(ld_e, 16)
            sp.dma_start(emask[:, :], D["masks"]).then_inc(ld_c, 16)
            sp.dma_start(W["cosT"][:, :], D["cos"]).then_inc(ld_c, 16)
            sp.dma_start(W["sinT"][:, :], D["sin"]).then_inc(ld_c, 16)
            sp.dma_start(W["bias"][:, :], D["bias"]).then_inc(ld_c, 16)
            sp.dma_start(rawo[:, :, :], D["wo"]).then_inc(ld_o, 16)
            sp.wait_ge(lo_ready, 1)
            sp.dma_start(raw[:, :, :], D["wf"]).then_inc(ld_f, 16)

        @block.gpsimd
        def _(pool):
            for n, cols in ((1, slice(0, 1)), (2, slice(1, 3)), (3, slice(4, 7)), (4, slice(3, 4))):
                pool.wait_ge(mx_ready, n)
                nc.gpsimd.partition_all_reduce(mxa[:, cols], mx[:, cols], P, bass.bass_isa.ReduceOp.max).then_inc(all_ready, 1)

        @block.scalar
        def _(act):
            def hi(dst, src, k):
                nc.scalar.activation(dst, src, ACT.Copy, scale=scale[:, k:k + 1]).then_inc(hi_ready, 1)

            act.wait_ge(sc_ready, 1)
            hi(wqk[:, 0, :, 0:1024], raw[:, :, :], 0)
            act.wait_ge(sc_ready, 2)
            hi(wqk[:, 0, :, 1024:1280], rawkv[:, :, 0:256], 1)
            hi(wv[:, 0], rawkv[:, :, 256:512], 2)
            act.wait_ge(sc_ready, 3)
            hi(wg[:, 0], rawg[:, :, :], 4)
            for e in range(2):
                nc.scalar.activation(ehi[:, e], rawe[:, e], ACT.Copy, scale=scale[0:32, 5 + e:6 + e]).then_inc(hi_ready, 1)
            act.wait_ge(sc_ready, 4)
            hi(wo[:, 0], rawo[:, :, :], 3)
            act.wait_ge(ld_f, 16)
            nc.scalar.activation(wf[:, :, :], raw[:, :, :], ACT.Sign).then_inc(sign_ready, 1)

        @block.vector
        def _(dve):
            v = nc.vector
            done = [0]

            def link(ins):
                done[0] += 1
                ins.then_inc(chain, 1)
                dve.wait_ge(chain, done[0])

            def largest(k, src, rows=slice(0, P)):
                return v.tensor_reduce(mx[rows, k:k + 1], src, AX.XY if len(src.shape) > 2 else AX.X, ALU.max, apply_absolute_value=True)

            def scales(cols):
                link(v.tensor_scalar(mxa[:, cols], mxa[:, cols], 1e-30, 1e30, ALU.max, ALU.min))
                link(v.tensor_scalar(inv[:, cols].bitcast(I32), mxa[:, cols].bitcast(I32), 0x7F800000, None, ALU.bitwise_and))
                v.tensor_scalar(scale[:, cols].bitcast(I32), inv[:, cols].bitcast(I32), -1.0, float(254 << 23), ALU.mult, ALU.add).then_inc(sc_ready, 1)

            def lo(dst, src, hi_, k, rows=slice(0, P)):
                return v.scalar_tensor_tensor(dst, src, scale[rows, k:k + 1], hi_, ALU.mult, ALU.subtract)

            link(v.memset(mx[:, :], 0.0))
            for half in range(2):
                dve.wait_ge(ld_q[half], 16)
                link(v.tensor_reduce(mxq[:, half:half + 1], raw[:, KB // 2 * half:KB // 2 * (half + 1), :], AX.XY, ALU.max, apply_absolute_value=True))
            v.tensor_reduce(mx[:, 0:1], mxq[:, :], AX.X, ALU.max).then_inc(mx_ready, 1)
            dve.wait_ge(ld_kv, 32)
            link(largest(1, rawkv[:, :, 0:256]))
            largest(2, rawkv[:, :, 256:512]).then_inc(mx_ready, 1)
            dve.wait_ge(all_ready, 1)
            scales(slice(0, 1))
            dve.wait_ge(all_ready, 2)
            scales(slice(1, 3))
            dve.wait_ge(ld_e, 48)
            link(largest(4, rawg[:, :, :]))
            link(largest(5, rawe[:, 0], slice(0, 32)))
            largest(6, rawe[:, 1], slice(0, 32)).then_inc(mx_ready, 1)
            dve.wait_ge(ld_c, 64)
            v.tensor_copy(W["ident"][:, :], emask[:, 0:P])
            v.tensor_copy(W["ident16"][:, :], emask[:, 0:P])
            v.tensor_copy(W["identb"][:, :], emask[:, 0:P])
            v.tensor_copy(W["avg"][:, :], emask[:, P:2 * P])
            v.tensor_copy(W["maskA"][:, :], emask[:, 2 * P:3 * P])
            v.tensor_copy(W["maskB"][:, :], emask[:, 3 * P:3 * P + 32])
            v.tensor_copy(W["maskK"][:, :], emask[:, 3 * P + 32:])
            dve.wait_ge(all_ready, 3)
            scales(slice(4, 7))
            dve.wait_ge(sc_ready, 3)
            link(v.tensor_scalar(fac[:, 0:1], inv[:, 0:1], inv[:, 1:2], float(HD ** -0.5), ALU.mult, ALU.mult))
            link(v.tensor_scalar(fac[:, 2:3], inv[:, 4:5], 1.0 / XS, None, ALU.mult))
            link(v.tensor_scalar(fac[:, 3:4], inv[:, 5:6], inv[:, 6:7], 1.0 / XS, ALU.mult, ALU.mult))
            dve.wait_ge(hi_ready, 1)
            lo(wqk[:, 1, :, 0:1024], raw[:, :, :], wqk[:, 0, :, 0:1024], 0).then_inc(lo_ready, 1)
            dve.wait_ge(ld_o, 16)
            largest(3, rawo[:, :, :]).then_inc(mx_ready, 1)
            dve.wait_ge(hi_ready, 2)
            lo(wqk[:, 1, :, 1024:1280], rawkv[:, :, 0:256], wqk[:, 0, :, 1024:1280], 1).then_inc(lo_ready, 1)
            dve.wait_ge(all_ready, 4)
            scales(slice(3, 4))
            dve.wait_ge(hi_ready, 3)
            lo(wv[:, 1], rawkv[:, :, 256:512], wv[:, 0], 2).then_inc(lo_ready, 1)
            dve.wait_ge(sc_ready, 4)
            link(v.tensor_scalar(fac[:, 1:2], inv[:, 2:3], inv[:, 3:4], None, ALU.mult))
            dve.wait_ge(hi_ready, 4)
            link(lo(wg[:, 1], rawg[:, :, :], wg[:, 0], 4))
            dve.wait_ge(hi_ready, 6)
            for e in range(2):
                link(lo(elo[:, e], rawe[:, e], ehi[:, e], 5 + e, slice(0, 32)))
            link(v.tensor_scalar(elo[:, :, :], elo[:, :, :], consts[0:32, 2:3], None, ALU.mult))
            link(v.scalar_tensor_tensor(experts[:, :, :], ehi[:, :, :], consts[0:32, 1:2], elo[:, :, :], ALU.mult, ALU.add))
            dve.wait_ge(hi_ready, 7)
            link(lo(wo[:, 1], rawo[:, :, :], wo[:, 0], 3))
            dve.wait_ge(sign_ready, 1)

        @block.tensor
        def _(pe):
            pass


def pairs_block(nc, D, h_d, out_d, W):
    with ExitStack() as ctx:
        def sb(name, shape, dt=F32):
            return ctx.enter_context(nc.sbuf_tensor(name, shape, dt))

        def sem(name):
            return ctx.enter_context(nc.semaphore(name))

        wqk, wv, wo, wf, wg, experts, fac, bias = (W[n] for n in ("wqk", "wv", "wo", "wf", "wg", "experts", "fac", "bias"))
        cosT, sinT, ident, ident16, identb, maskA, maskB, maskK, avg, consts = (
            W[n] for n in ("cosT", "sinT", "ident", "ident16", "identb", "maskA", "maskB", "maskK", "avg", "consts"))
        xc = sb("xc", [P, KB, T])
        x1 = sb("x1", [P, 2, KB, T], F16)
        x2 = sb("x2", [P, 2, KB, T], F16)
        x1sq = x1[:, :, :, :].rearrange("p a k t -> p (a k t)").bitcast(F32).rearrange("p (k t) -> p k t", k=KB)
        x2sq = x2[:, :, :, :].rearrange("p a k t -> p (a k t)").bitcast(F32).rearrange("p (k t) -> p k t", k=KB)
        h2 = sb("h2", [P, KB, T])
        qs = sb("qs", [P, NQ, T], F16)
        ks = sb("ks", [P, NKV, T], F16)
        rt = sb("rt", [P, 2, 2, 2, T], F16)
        pf = sb("pf", [P, 3, 512])
        ph = sb("ph", [P, 2, 3, 512], F16)
        prod = pf[:, :, :].rearrange("p a c -> p (a c)")[:, 0:4 * T].rearrange("p (a t) -> p a t", a=4)
        rot = ph[:, :, :, :].rearrange("p a b c -> p (a b c)").bitcast(F32)[:, 0:4 * T].rearrange("p (s a t) -> p s a t", s=2, a=2)
        vv = sb("vv", [P, 2, 3, NKV, HD + 1], F16)
        att = sb("att", [P, 10, NKV, HD])
        qb = att[:, :, :, :].rearrange("p n k d -> p (n k d)").bitcast(F16)[:, 0:64 * NQ].rearrange("p (b h q) -> p b h q", b=2, h=NQ)
        mxa = sb("mxa", [P, 2, NKV, 4])
        mxb = sb("mxb", [P, 2, NKV])
        rsum = sb("rsum", [P, 10])
        mt = rt[0:NQ, :, :, :, :].rearrange("p a b c t -> p (a b c t)")[:, 0:1024].rearrange("p (a c) -> p a c", a=2)
        sums = sb("sums", [P, T])
        rstd = sb("rstd", [P, T])
        nt = sb("nt", [P, T])
        gl = sb("gl", [P, 3, EXPERTS])
        g1 = sb("g1_", [P, 3, 1])
        rr = sb("rr", [P, 3, 4, EXPERTS], F16)
        rT = sb("rT", [4 * EXPERTS, T], F16)
        os_ = sb("os_", [P, 2, T])

        pj = [ctx.enter_context(nc.psum_tensor(f"pj{b}", [P, 512], F32)) for b in range(BANKS)]
        sa = [ctx.enter_context(nc.psum_tensor(f"sa{b}", [P, 512], F32)) for b in range(3)]

        h_loaded, res_loaded, stored = sem("h_loaded"), sem("res_loaded"), sem("stored")
        stacked = [sem(f"stacked{j}") for j in range(QKB)]
        rows_loaded = sem("rows_loaded")
        pj_full = [sem(f"pj_full{b}") for b in range(BANKS)]
        pj_free = [sem(f"pj_free{b}") for b in range(BANKS)]
        sa_full = [sem(f"sa_full{b}") for b in range(3)]
        sa_free = [sem(f"sa_free{b}") for b in range(3)]
        dchain, achain = {"front": sem("dchain_front"), "back": sem("dchain_back")}, {i: sem(f"achain{i}") for i in (1, 2)}
        init = sem("init")
        sum_ready, squared, rough, norm_ready, hi_made, x_ready = (
            {i: sem(f"{name}{i}") for i in (1, 2)} for name in ("sum_ready", "squared", "rough", "norm_ready", "hi_made", "x_ready"))
        rot_ready, rot_hi, rope_ready = sem("rot_ready"), sem("rot_hi"), sem("rope_ready")
        v_hi, qb_ready = sem("v_hi"), sem("qb_ready")
        split_hi, split_ready = ([sem(f"{name}{r}") for r in range(3)] for name in ("split_hi", "split_ready"))
        split_used = [sem("split_used0"), sem("split_used1")]
        at_hi = sem("at_hi")
        summed = sem("summed")
        gexp_in, gexp_out, rout_ready = sem("gexp_in"), sem("gexp_out"), sem("rout_ready")
        y_hi, y_ready = sem("y_hi"), sem("y_ready")
        f_done = sem("f_done")
        block = ctx.enter_context(nc.Block())

        def full(eng, name, s):
            b, n = s.use(name)
            eng.wait_ge(pj_full[b], n + 1)
            return pj[b]

        def read(eng, name, s):
            b, n = s.use(name)
            eng.wait_ge(pj_free[b], n + 1 + CREDIT)

        def free(name):
            return pj_free[USES.index(name) % BANKS]

        def steps(eng, program):
            program(Step(-1, back=False))
            with eng.Fori(0, NPAIR - 1) as p:
                program(Step(p))
            program(Step(NPAIR - 1, front=False))

        BB = [slice(256, 288), slice(288, 320)]
        AB = [A0, A1]

        @block.sync
        def _(sp):
            def step(s):
                p, q = s.p, s.q
                if s.front and s.back:
                    sp.wait_ge(y_ready, KB * p + CREDIT)
                if s.front:
                    sp.dma_start(xc[:, :, 0:256], h_d[q, :, :, :, :].rearrange("j i b h -> j i (b h)")).then_inc(h_loaded, 16)
                    sp.dma_start(xc[:, :, 256:320], D["txt"][q, :, :, :]).then_inc(h_loaded, 16)
                if s.back:
                    sp.wait_ge(stored, 16 * p + CREDIT)
                    sp.dma_start(h2[:, :, 0:256], h_d[p, :, :, :, :].rearrange("j i b h -> j i (b h)")).then_inc(res_loaded, 16)
                    sp.dma_start(h2[:, :, 256:320], D["txt"][p, :, :, :]).then_inc(res_loaded, 16)
                if s.front:
                    for n, j in enumerate((4, 0, 1, 2, 3)):
                        sp.wait_ge(rope_ready, QKB * q + n + 1)
                        parts = (0, 1, 0) if j == 4 else (0, 0, 1)
                        for g, hl in enumerate(parts):
                            for ab in range(2):
                                r = 32 * g + 16 * ab
                                dst = ks[r:r + 16, :, :] if j == 4 else qs[r:r + 16, 8 * j:8 * j + 8, :]
                                sp.dma_start(dst, rt[:, n % 2, ab, hl, :]).then_inc(stacked[n], 16)
                    read(sp, "maxT", s)
                    for hl in range(2):
                        sp.dma_start(qs[96 + hl:97 + hl, :, 0:256], mt[:, hl, 0:256]).then_inc(rows_loaded, 16)
                        for b in range(2):
                            sp.dma_start(qs[96 + hl:97 + hl, :, BB[b]].rearrange("p (k h) q -> p k h q", h=4),
                                         mt[0:NKV, hl, 256 + 128 * b:384 + 128 * b].rearrange("p (h q) -> p h q", h=4)).then_inc(rows_loaded, 16)
                if s.back:
                    sp.wait_ge(f_done, KB * (p + 1))
                    sp.dma_start(out_d[p, :, :, :], h2[:, :, :]).then_inc(stored, 16)

            steps(sp, step)
            sp.wait_ge(stored, 16 * NPAIR + CREDIT)

        @block.tensor
        def _(pe):
            mm = nc.tensor.matmul

            def bank(name, s):
                b, n = s.use(name)
                pe.wait_ge(pj_free[b], n + CREDIT)
                return pj[b], pj_full[b]

            def split_product(out, w_hi, w_lo, x, cols=slice(0, T)):
                for k in range(KB):
                    mm(out, w_hi(k), x[:, 0, k, cols], start=(k == 0), stop=False)
                    mm(out, w_hi(k), x[:, 1, k, cols], start=False, stop=False)
                    last = mm(out, w_lo(k), x[:, 0, k, cols], start=False, stop=(k == KB - 1))
                return last

            def average(name, s, i, n):
                ps, f = bank(name, s)
                pe.wait_ge(sum_ready[i], 2 * (s.q if i == 1 else s.p) + n)
                mm(ps[:, 0:T], avg[:, :], sums[:, :], start=True, stop=True).then_inc(f, 1)

            pe.wait_ge(init, 2)

            def step(s):
                p, q = s.p, s.q

                def transposes(kh):
                    for b in range(2):
                        ps, f = bank(f"atA{kh}{b}", s)
                        for h in range(4):
                            last = nc.tensor.transpose(ps[:, 128 * h:128 * h + 128], att[:, 4 * b + h, 4 * kh:4 * kh + 4, :].rearrange("p k d -> p (k d)"), ident[:, :])
                        last.then_inc(f, 1)

                def scores(kv):
                    for b in range(2):
                        pe.wait_ge(sa_free[b], 16 * p + 8 + kv + CREDIT)
                        s_ = sa[b][:, :].rearrange("p (h q) -> p h q", h=4)
                        mm(s_, identb[:, :], maskK[:, 0:P].unsqueeze(1).broadcast_to([P, 4, P]), start=True, stop=False, skip_group_check=True)
                        mm(s_, ks[0:98, kv, AB[b]], qs[0:98, 4 * kv:4 * kv + 4, AB[b]],
                           start=False, stop=True, skip_group_check=True).then_inc(sa_full[b], 1)
                    pe.wait_ge(sa_free[2], 16 * p + 8 + kv + CREDIT)
                    for b in range(2):
                        mm(sa[2][:, 128 * b:128 * b + 128].rearrange("p (h q) -> p h q", h=4), ks[0:98, kv, AB[b]],
                           qs[0:98, 4 * kv:4 * kv + 4, BB[b]], start=True, stop=True, skip_group_check=True)
                    s_ = sa[2][:, 256:512].rearrange("p (b h q) -> p b h q", b=2, h=4)
                    mm(s_, identb[:, :], maskK[:, P:].rearrange("p (b q) -> p b q", b=2).unsqueeze(2).broadcast_to([P, 2, 4, 32]),
                       start=True, stop=False, skip_group_check=True)
                    mm(s_, ks[0:98, kv, 192:320], qs[0:98, 4 * kv:4 * kv + 4, BT].rearrange("p h (b q) -> p b h q", b=2),
                       start=False, stop=True, skip_group_check=True).then_inc(sa_full[2], 1)

                def values(kv):
                    ps, f = bank(f"pv{kv}", s)
                    o = ps[:, 0:330].rearrange("p (n d) -> p n d", n=10)

                    def weighted(n, terms):
                        for i, (sl, c, t) in enumerate(terms):
                            c = slice(c, c + 128)
                            mm(o[:, n, :], ph[:, 0, sl, c], vv[:, 0, t, kv, :], start=(i == 0), stop=False)
                            mm(o[:, n, :], ph[:, 0, sl, c], vv[:, 1, t, kv, :], start=False, stop=False)
                            last = mm(o[:, n, :], ph[:, 1, sl, c], vv[:, 0, t, kv, :], start=False, stop=(i == len(terms) - 1))
                        return last

                    for b in range(2):
                        pe.wait_ge(split_ready[b], NKV * p + kv + 1)
                        for h in range(4):
                            last = weighted(4 * b + h, [(b, 128 * h, b)])
                        last.then_inc(split_used[b], 1)
                    pe.wait_ge(split_ready[2], NKV * p + kv + 1)
                    for b in range(2):
                        last = weighted(8 + b, [(2, 128 * b, b), (2, 256 + 128 * b, 2)])
                    last.then_inc(f, 1)

                def attention():
                    pe.wait_ge(rows_loaded, 96 * (p + 1))
                    scores(0)
                    for kv in range(NKV):
                        if kv + 1 < NKV:
                            scores(kv + 1)
                        values(kv)
                        if kv == NKV - 2:
                            read(pe, "pv3", s)
                            transposes(0)
                    read(pe, "pv7", s)
                    transposes(1)
                    ps, f = bank("atB", s)
                    for kh in range(2):
                        for b in range(2):
                            last = nc.tensor.transpose(ps[:, 256 * kh + 128 * b:256 * kh + 128 * b + 128], att[:, 8 + b, 4 * kh:4 * kh + 4, :].rearrange("p k d -> p (k d)"), ident[:, :])
                    last.then_inc(f, 1)
                    read(pe, "atB", s)

                def o_product(m):
                    ps, f = bank(f"o{m}", s)
                    c = slice(128 * m, 128 * m + 128)
                    split_product(ps[:, 0:T], lambda k: wo[:, 0, k, c], lambda k: wo[:, 1, k, c], x2).then_inc(f, 1)

                def qk_product(j, halves=(0, 1)):
                    for a in halves:
                        ps, f = bank(f"qk{j}{'ab'[a]}", s)
                        c = slice(256 * j + 128 * a, 256 * j + 128 * a + 128)
                        split_product(ps[:, 0:T], lambda k: wqk[:, 0, k, c], lambda k: wqk[:, 1, k, c], x1).then_inc(f, 1)

                def v_product(t):
                    if t != 1:
                        ps, f = bank("v01" if t < 2 else "v2", s)
                    else:
                        ps, f = pj[s.use("v01")[0]], pj_full[s.use("v01")[0]]
                    cols = (A0, A1, slice(192, 320))[t]
                    o = ps[:, 256 * (t % 2):256 * (t % 2) + 256]
                    for k in range(KB):
                        mm(o, x1[:, 0, k, cols], wv[:, 0, k, :], start=(k == 0), stop=False)
                        mm(o, x1[:, 0, k, cols], wv[:, 1, k, :], start=False, stop=False)
                        last = mm(o, x1[:, 1, k, cols], wv[:, 0, k, :], start=False, stop=(k == KB - 1))
                    if t >= 1:
                        last.then_inc(f, 1)

                def maxima_scores(kv):
                    if kv % 2 == 0:
                        pe.wait_ge(stacked[kv // 2 + 1], 96 * (q + 1) + CREDIT)
                        pe.wait_ge(qb_ready, 4 * q + kv // 2 + 1)
                    if kv == 0:
                        pe.wait_ge(stacked[0], 96 * (q + 1) + CREDIT)
                    for b in range(2):
                        pe.wait_ge(sa_free[b], 16 * q + kv + CREDIT)
                        s = sa[b][:, :].rearrange("p (h k) -> p h k", h=4)
                        mm(s, identb[:, :], maskA[:, :].unsqueeze(1).broadcast_to([P, 4, P]), start=True, stop=False, skip_group_check=True)
                        for h in range(4):
                            last = mm(s[:, h, :], qs[0:96, 4 * kv + h, AB[b]], ks[0:96, kv, AB[b]], start=False, stop=(h == 3), skip_group_check=True)
                        last.then_inc(sa_full[b], 1)
                    pe.wait_ge(sa_free[2], 16 * q + kv + CREDIT)
                    s = sa[2][:, 0:320].rearrange("p (b k) -> p b k", b=2)
                    mm(s[:, :, 128:160], identb[:, :], maskB[:, :].unsqueeze(1).broadcast_to([P, 2, 32]), start=True, stop=False, skip_group_check=True)
                    for b in range(2):
                        texts = qb[0:96, b, 4 * kv:4 * kv + 4, :].rearrange("p h q -> p (h q)")
                        mm(s[:, b, 0:128], texts, ks[0:96, kv, AB[b]], start=True, stop=False, skip_group_check=True)
                        last = mm(s[:, b, 128:160], texts, ks[0:96, kv, BB[b]], start=False, stop=(b == 1), skip_group_check=True)
                    last.then_inc(sa_full[2], 1)

                def maxima_by_head():
                    ps, f = bank("maxT", s)
                    for r in range(3):
                        pe.wait_ge(sa_free[r], 16 * q + NKV + CREDIT)
                    for b in range(2):
                        nc.tensor.transpose(ps[0:NQ, 128 * b:128 * b + 128], mxa[:, b].rearrange("p k h -> p (k h)"), ident[:, :])
                    for b in range(2):
                        last = nc.tensor.transpose(ps[0:NKV, 256 + 128 * b:384 + 128 * b], mxb[:, b, :], ident[:, :])
                    last.then_inc(f, 1)


                def gate_logits():
                    pe.wait_ge(x_ready[2], 2 * (p + 1))
                    ps, f = bank("gate", s)
                    for t, cols in enumerate((A0, A1, BT)):
                        n = 64 if t == 2 else P
                        o = ps[0:n, 8 * t:8 * t + 8]
                        for k in range(KB):
                            mm(o, x2[:, 0, k, cols], wg[:, 0, k, :], start=(k == 0), stop=False)
                            mm(o, x2[:, 0, k, cols], wg[:, 1, k, :], start=False, stop=False)
                            last = mm(o, x2[:, 1, k, cols], wg[:, 0, k, :], start=False, stop=(k == KB - 1))
                    last.then_inc(f, 1)

                def routing_by_expert():
                    ps, f = bank("routT", s)
                    pe.wait_ge(rout_ready, p + 1)
                    pt = ps[0:32, 0:160].bitcast(F16)
                    for t, cols in enumerate((A0, A1, BT)):
                        n = 64 if t == 2 else P
                        last = nc.tensor.transpose(pt[:, cols], rr[0:n, t, :, :].rearrange("p a e -> p (a e)"), ident16[0:n, 0:n])
                    last.then_inc(f, 1)
                    read(pe, "routT", s)

                def in_scale(m):
                    ps, f = bank(f"in{m}", s)
                    mm(ps[:, 0:T], experts[:, 0, 128 * m:128 * m + 128], rT[:, :], start=True, stop=True).then_inc(f, 1)

                def ffn_product(m):
                    c = slice(128 * m, 128 * m + 128)
                    ps, f = bank(f"os{m}", s)
                    mm(ps[:, 0:T], experts[:, 1, c], rT[:, :], start=True, stop=True).then_inc(f, 1)
                    ps, f = bank(f"f{m}", s)
                    for k in range(KB):
                        if m == 0:
                            pe.wait_ge(y_ready, KB * p + k + 1 + CREDIT)
                        mm(ps[:, 0:T], wf[:, k, c], x2[:, 0, k, :], start=(k == 0), stop=False)
                        last = mm(ps[:, 0:T], wf[:, k, c], x2[:, 1, k, :], start=False, stop=(k == KB - 1))
                    last.then_inc(f, 1)

                if s.back:
                    attention()
                if s.front:
                    average("mean1", s, 1, 1)
                for m in range(KB):
                    if s.front and m == 5:
                        average("var1", s, 1, 2)
                    if s.back:
                        o_product(m)
                if s.front:
                    pe.wait_ge(x_ready[1], 2 * (q + 1))
                    qk_product(4, [0])
                if s.back:
                    average("mean2", s, 2, 1)
                if s.front:
                    qk_product(4, [1])
                    qk_product(0)
                if s.back:
                    average("var2", s, 2, 2)
                if s.front:
                    qk_product(1)
                    qk_product(2)
                if s.back:
                    gate_logits()
                if s.front:
                    qk_product(3)
                if s.back:
                    routing_by_expert()
                if s.front:
                    maxima_scores(0)
                if s.back:
                    for m in range(4):
                        in_scale(m)
                if s.front:
                    v_product(0)
                    v_product(1)
                if s.back:
                    for m in range(4, KB - 1):
                        in_scale(m)
                if s.front:
                    maxima_scores(1)
                if s.back:
                    in_scale(KB - 1)
                if s.front:
                    v_product(2)
                for m in range(KB):
                    if s.front:
                        if m < KB - 2:
                            maxima_scores(m + 2)
                        if m == KB - 3:
                            read(pe, "v01", s)
                            read(pe, "v2", s)
                            maxima_by_head()
                    if s.back:
                        ffn_product(m)

            steps(pe, step)

        @block.scalar
        def _(act):
            A = nc.scalar.activation
            nc.scalar.preload_act_table_set("natural_log_exp_and_others")

            def step(s):
                p, q = s.p, s.q

                def squares(i, x, sq):
                    read(act, f"mean{i}", s)
                    A(sq, x, ACT.Square).then_inc(squared[i], 1)

                def rough_rstd(i, pair):
                    ps = full(act, f"var{i}", s)
                    A(rstd[:, :], ps[:, 0:T], ACT.Ln, bias=consts[:, 0:1]).then_inc(achain[i], 1)
                    act.wait_ge(achain[i], pair + 1)
                    A(rstd[:, :], rstd[:, :], ACT.Exp, scale=-0.5).then_inc(rough[i], 1)

                def high(i, pair, x, dst):
                    for n, k in enumerate(HALVES):
                        act.wait_ge(norm_ready[i], 2 * pair + n + 1)
                        A(dst[:, 0, k], x[:, k], ACT.Copy).then_inc(hi_made[i], 1)

                def rope_hi(n):
                    act.wait_ge(rot_ready, QKB * q + n + 1)
                    if n >= 2:
                        act.wait_ge(stacked[n - 2], 96 * (q + 1) + CREDIT)
                    else:
                        act.wait_ge(stacked[4 - n], 96 * q + CREDIT)
                    A(rt[:, n % 2, :, 0, :], rot[:, n % 2], ACT.Copy).then_inc(rot_hi, 1)

                def v_high(t):
                    ps = full(act, "v01" if t < 2 else "v2", s)
                    A(vv[:, 0, t, :, 0:HD], ps[:, 256 * (t % 2):256 * (t % 2) + 256].rearrange("p (k d) -> p k d", k=NKV),
                      ACT.Copy, scale=1.0 / XS).then_inc(v_hi, 1)

                def y_high(m):
                    read(act, f"in{m}", s)
                    A(x2[:, 0, m, :], xc[:, m, :], ACT.Copy).then_inc(y_hi, 1)

                def attention():
                    for kv in range(NKV):
                        for r in range(3):
                            act.wait_ge(sa_full[r], 16 * p + 8 + kv + 1)
                            if kv >= 1:
                                act.wait_ge(split_ready[r], NKV * p + kv)
                            A(pf[:, r, :], sa[r][:, :], ACT.Exp, scale=fac[:, 0:1]).then_inc(sa_free[r], 1)
                        if kv >= 1:
                            full(act, f"pv{kv - 1}", s)
                        act.wait_ge(sa_free[2], 16 * p + 8 + kv + 1 + CREDIT)
                        A(ph[:, 0, 2, :], pf[:, 2, :], ACT.Copy).then_inc(split_hi[2], 1)
                    for kh in range(2):
                        for b in range(2):
                            ps = full(act, f"atA{kh}{b}", s)
                            A(x2[:, 0, 4 * kh:4 * kh + 4, AB[b]], ps[:, :].rearrange("p (h q) -> p h q", h=4), ACT.Copy).then_inc(at_hi, 1)
                    ps = full(act, "atB", s)
                    for kh in range(2):
                        A(x2[:, 0, 4 * kh:4 * kh + 4, BT].rearrange("p h (b q) -> p b h q", b=2),
                          ps[:, 256 * kh:256 * kh + 256].rearrange("p (b h q) -> p b h q", b=2, h=4), ACT.Copy).then_inc(at_hi, 1)

                if s.back:
                    attention()
                if s.front:
                    squares(1, xc[:, :, :], x1sq)
                    rough_rstd(1, q)
                    high(1, q, xc[:, :, :], x1)
                if s.back:
                    squares(2, xc[:, :, :], x2sq)
                if s.front:
                    rope_hi(0)
                    rope_hi(1)
                if s.back:
                    rough_rstd(2, p)
                    high(2, p, xc[:, :, :], x2)
                if s.front:
                    rope_hi(2)
                    rope_hi(3)
                if s.back:
                    act.wait_ge(gexp_in, p + 1)
                    A(gl[:, :, :], gl[:, :, :], ACT.Exp, scale=fac[:, 2:3]).then_inc(gexp_out, 1)
                if s.front:
                    rope_hi(4)
                if s.back:
                    for m in range(4):
                        y_high(m)
                if s.front:
                    v_high(0)
                    v_high(1)
                if s.back:
                    for m in range(4, KB):
                        y_high(m)
                if s.front:
                    v_high(2)
                if s.back:
                    for m in range(KB):
                        ps = full(act, f"os{m}", s)
                        if m >= 2:
                            act.wait_ge(f_done, KB * p + m - 1)
                        A(os_[:, m % 2, :], ps[:, 0:T], ACT.Copy, scale=fac[:, 3:4]).then_inc(free(f"os{m}"), 1)

            steps(act, step)

        @block.gpsimd
        def _(pool):
            g = nc.gpsimd
            for s in (*pj_free, *sa_free, stored, y_ready, *stacked):
                pool.sem_inc(s, CREDIT)
            g.memset(ks[96:98, :, :], SHIFT).then_inc(init, 1)
            pool.wait_ge(init, 1)
            g.memset(vv[:, 1], 0.0)
            g.memset(vv[:, 0, :, :, HD:HD + 1], 1.0).then_inc(init, 1)

            def step(s):
                p, q = s.p, s.q
                for kv in range(NKV):
                    if s.front and s.back and kv == FIRST_SUM:
                        pool.wait_ge(h_loaded, 32 * (q + 1))
                    for k in range(2 * (kv - FIRST_SUM), min(2 * (kv - FIRST_SUM) + 2, KB - 1)) if s.front and s.back and kv >= FIRST_SUM else ():
                        if k >= 1:
                            pool.wait_ge(summed, (KB - 2) * p + k)
                        add = g.tensor_tensor(sums[:, :], xc[:, 0, :] if k == 0 else sums[:, :], xc[:, k + 1, :], ALU.add)
                        add.then_inc(sum_ready[1] if k == KB - 2 else summed, 1)
                    if s.back:
                        pool.wait_ge(split_hi[2], NKV * p + kv + 1)
                        g.tensor_tensor(ph[:, 1, 2, :], pf[:, 2, :], ph[:, 0, 2, :], ALU.subtract).then_inc(split_ready[2], 1)

                def rotate(n):
                    read(pool, f"qk{(4, 0, 1, 2, 3)[n]}b", s)
                    if n >= 2:
                        pool.wait_ge(rope_ready, QKB * q + n - 1)
                    g.tensor_tensor(rot[:, n % 2, 0], prod[:, 0], prod[:, 1], ALU.subtract)
                    g.tensor_tensor(rot[:, n % 2, 1], prod[:, 2], prod[:, 3], ALU.add).then_inc(rot_ready, 1)

                def rope_lo(n):
                    pool.wait_ge(rot_hi, QKB * q + n + 1)
                    g.tensor_tensor(rt[:, n % 2, :, 1, :], rot[:, n % 2], rt[:, n % 2, :, 0, :], ALU.subtract).then_inc(rope_ready, 1)

                if s.front:
                    rotate(0)
                    rotate(1)
                    rope_lo(0)
                    rotate(2)
                    rope_lo(1)
                    rotate(3)
                    rope_lo(2)
                if s.front:
                    rotate(4)
                    rope_lo(3)
                    rope_lo(4)
                if s.back:
                    for m in range(KB):
                        pool.wait_ge(y_hi, KB * p + m + 1)
                        g.tensor_tensor(x2[:, 1, m, :], xc[:, m, :], x2[:, 0, m, :], ALU.subtract).then_inc(y_ready, 1)

            steps(pool, step)

        @block.vector
        def _(dve):
            v = nc.vector
            OWN = {"front": 5, "back": 19}
            v.memset(gl[:, :, :], 0.0)

            def step(s):
                p, q = s.p, s.q
                n_own = {"front": 0, "back": 0}

                def own(part, ins):
                    n_own[part] += 1
                    ins.then_inc(dchain[part], 1)
                    dve.wait_ge(dchain[part], OWN[part] * (q if part == "front" else p) + n_own[part])

                def channel_sums(i, src):
                    v.tensor_reduce(sums[:, :], src.rearrange("p k t -> p t k"), AX.X, ALU.add).then_inc(sum_ready[i], 1)

                def centre(i, src, x):
                    ps = full(dve, f"mean{i}", s)
                    v.tensor_tensor(x, src, ps[:, 0:T].unsqueeze(1).broadcast_to([P, KB, T]), ALU.subtract).then_inc(free(f"mean{i}"), 1)

                def square_sums(i, pair, sq):
                    dve.wait_ge(squared[i], pair + 1)
                    channel_sums(i, sq)

                def normalise(i, pair, x):
                    part = ("front", "back")[i - 1]
                    ps = full(dve, f"var{i}", s)
                    dve.wait_ge(rough[i], pair + 1)
                    own(part, v.tensor_tensor(sums[:, :], rstd[:, :], rstd[:, :], ALU.mult))
                    v.scalar_tensor_tensor(nt[:, :], ps[:, 0:T], EPS, sums[:, :], ALU.add, ALU.mult).then_inc(free(f"var{i}"), 1)
                    read(dve, f"var{i}", s)
                    own(part, v.tensor_scalar(nt[:, :], nt[:, :], -0.5, 1.5, ALU.mult, ALU.add))
                    own(part, v.tensor_tensor(rstd[:, :], rstd[:, :], nt[:, :], ALU.mult))
                    for k in HALVES:
                        v.scalar_tensor_tensor(x[:, k], x[:, k], XS, rstd[:, :].unsqueeze(1).broadcast_to([P, KB // 2, T]),
                                               ALU.mult, ALU.mult).then_inc(norm_ready[i], 1)

                def low(i, pair, x, dst):
                    for n, k in enumerate(HALVES):
                        dve.wait_ge(hi_made[i], 2 * pair + n + 1)
                        v.tensor_tensor(dst[:, 1, k], x[:, k], dst[:, 0, k], ALU.subtract).then_inc(x_ready[i], 1)

                def rope(n, j):
                    pa = full(dve, f"qk{j}a", s)
                    if n >= 1:
                        dve.wait_ge(rot_ready, QKB * q + n)
                    v.tensor_tensor(prod[:, 0], pa[:, 0:T], cosT[:, :], ALU.mult)
                    v.tensor_tensor(prod[:, 2], pa[:, 0:T], sinT[:, :], ALU.mult).then_inc(free(f"qk{j}a"), 1)
                    pb = full(dve, f"qk{j}b", s)
                    v.tensor_tensor(prod[:, 1], pb[:, 0:T], sinT[:, :], ALU.mult)
                    v.tensor_tensor(prod[:, 3], pb[:, 0:T], cosT[:, :], ALU.mult).then_inc(free(f"qk{j}b"), 1)

                def queries_of_texts(j):
                    dve.wait_ge(stacked[j + 1], 96 * (q + 1) + CREDIT)
                    v.tensor_copy(qb[0:96, :, 8 * j:8 * j + 8, :], qs[0:96, 8 * j:8 * j + 8, BT].rearrange("p h (b q) -> p b h q", b=2)).then_inc(qb_ready, 1)

                def v_low(t):
                    ps = full(dve, "v01" if t < 2 else "v2", s)
                    dve.wait_ge(v_hi, 3 * q + (2 if t < 2 else 3))
                    lo = v.scalar_tensor_tensor(vv[:, 1, t, :, 0:HD], ps[:, 256 * (t % 2):256 * (t % 2) + 256].rearrange("p (k d) -> p k d", k=NKV),
                                                1.0 / XS, vv[:, 0, t, :, 0:HD], ALU.mult, ALU.subtract)
                    if t >= 1:
                        lo.then_inc(free("v01" if t == 1 else "v2"), 1)

                def maxima(kv):
                    for b in range(2):
                        dve.wait_ge(sa_full[b], 16 * q + kv + 1)
                        v.tensor_reduce(mxa[:, b, kv, :], sa[b][:, :].rearrange("p (h k) -> p h k", h=4), AX.X, ALU.max).then_inc(sa_free[b], 1)
                    dve.wait_ge(sa_full[2], 16 * q + kv + 1)
                    v.tensor_reduce(mxb[:, :, kv], sa[2][:, 0:320].rearrange("p (b k) -> p b k", b=2), AX.X, ALU.max).then_inc(sa_free[2], 1)

                def maxima_split():
                    ps = full(dve, "maxT", s)
                    areas = ((NQ, slice(0, 256)), (NKV, slice(256, 512)))
                    for rows, cols in areas:
                        own("front", v.tensor_scalar(mt[0:rows, 0, cols], ps[0:rows, cols], -1.0 / SHIFT, None, ALU.mult))
                    for rows, cols in areas:
                        lo = v.scalar_tensor_tensor(mt[0:rows, 1, cols], ps[0:rows, cols], -1.0 / SHIFT, mt[0:rows, 0, cols], ALU.mult, ALU.subtract)
                    lo.then_inc(free("maxT"), 1)

                def attention_out(kv):
                    ps = full(dve, f"pv{kv}", s)
                    o = ps[:, 0:330].rearrange("p (n d) -> p n d", n=10)
                    own("back", v.reciprocal(rsum[:, :].unsqueeze(2), o[:, :, HD:HD + 1]))
                    v.tensor_tensor(att[:, :, kv, :], o[:, :, 0:HD], rsum[:, :].unsqueeze(2).broadcast_to([P, 10, HD]), ALU.mult).then_inc(free(f"pv{kv}"), 1)

                def attention():
                    for kv in range(NKV):
                        for r in range(2):
                            dve.wait_ge(sa_free[r], 16 * p + 8 + kv + 1 + CREDIT)
                            if kv >= 1:
                                dve.wait_ge(split_used[r], NKV * p + kv)
                            v.tensor_copy(ph[:, 0, r, :], pf[:, r, :]).then_inc(split_hi[r], 1)
                            dve.wait_ge(split_hi[r], NKV * p + kv + 1)
                            v.tensor_tensor(ph[:, 1, r, :], pf[:, r, :], ph[:, 0, r, :], ALU.subtract).then_inc(split_ready[r], 1)
                            if r == 0 and kv >= 1:
                                attention_out(kv - 1)
                    for n, (kh, b) in enumerate(((0, 0), (0, 1), (1, 0), (1, 1))):
                        if n == 2:
                            attention_out(NKV - 1)
                        ps = full(dve, f"atA{kh}{b}", s)
                        dve.wait_ge(at_hi, 6 * p + n + 1)
                        v.tensor_tensor(x2[:, 1, 4 * kh:4 * kh + 4, AB[b]], ps[:, :].rearrange("p (h q) -> p h q", h=4),
                                        x2[:, 0, 4 * kh:4 * kh + 4, AB[b]], ALU.subtract).then_inc(free(f"atA{kh}{b}"), 1)
                    ps = full(dve, "atB", s)
                    dve.wait_ge(at_hi, 6 * (p + 1))
                    for kh in range(2):
                        lo = v.tensor_tensor(x2[:, 1, 4 * kh:4 * kh + 4, BT].rearrange("p h (b q) -> p b h q", b=2),
                                             ps[:, 256 * kh:256 * kh + 256].rearrange("p (b h q) -> p b h q", b=2, h=4),
                                             x2[:, 0, 4 * kh:4 * kh + 4, BT].rearrange("p h (b q) -> p b h q", b=2), ALU.subtract)
                    lo.then_inc(free("atB"), 1)

                def residual(m):
                    if m == 0:
                        dve.wait_ge(res_loaded, 32 * (p + 1))
                    ps = full(dve, f"o{m}", s)
                    v.scalar_tensor_tensor(h2[:, m, :], ps[:, 0:T], fac[:, 1:2], h2[:, m, :], ALU.mult, ALU.add).then_inc(free(f"o{m}"), 1)

                def routing():
                    ps = full(dve, "gate", s)
                    own("back", v.tensor_copy(gl[:, 0:2, :], ps[:, 0:16].rearrange("p (t e) -> p t e", t=2)))
                    v.tensor_copy(gl[0:64, 2, :], ps[0:64, 16:24]).then_inc(free("gate"), 1)
                    read(dve, "gate", s)
                    own("back", v.tensor_reduce(g1[:, :, :], gl[:, :, :], AX.X, ALU.max))
                    v.tensor_tensor(gl[:, :, :], gl[:, :, :], g1[:, :, :].broadcast_to([P, 3, EXPERTS]), ALU.subtract).then_inc(gexp_in, 1)
                    dve.wait_ge(gexp_out, p + 1)
                    own("back", v.tensor_reduce(g1[:, :, :], gl[:, :, :], AX.X, ALU.add))
                    own("back", v.reciprocal(g1[:, :, :], g1[:, :, :]))
                    own("back", v.tensor_tensor(gl[:, :, :], gl[:, :, :], g1[:, :, :].broadcast_to([P, 3, EXPERTS]), ALU.mult))
                    own("back", v.tensor_copy(rr[:, :, 0, :], gl[:, :, :]))
                    own("back", v.tensor_copy(rr[:, :, 2, :], gl[:, :, :]))
                    own("back", v.tensor_tensor(rr[:, :, 1, :], gl[:, :, :], rr[:, :, 0, :], ALU.subtract))
                    v.tensor_tensor(rr[:, :, 3, :], gl[:, :, :], rr[:, :, 0, :], ALU.subtract).then_inc(rout_ready, 1)

                def routing_copy():
                    ps = full(dve, "routT", s)
                    v.tensor_copy(rT[:, :], ps[0:32, 0:160].bitcast(F16)).then_inc(free("routT"), 1)

                def scaled_in(m):
                    ps = full(dve, f"in{m}", s)
                    v.tensor_tensor(xc[:, m, :], ps[:, 0:T], xc[:, m, :], ALU.mult).then_inc(free(f"in{m}"), 1)

                def ffn_out(m):
                    read(dve, f"os{m}", s)
                    ps = full(dve, f"f{m}", s)
                    v.tensor_tensor(os_[:, m % 2, :], ps[:, 0:T], os_[:, m % 2, :], ALU.mult).then_inc(free(f"f{m}"), 1)
                    read(dve, f"f{m}", s)
                    v.scalar_tensor_tensor(h2[:, m, :], os_[:, m % 2, :], bias[:, m:m + 1], h2[:, m, :], ALU.add, ALU.add).then_inc(f_done, 1)

                def back(part, *args):
                    if s.back:
                        part(*args)

                def front(part, *args):
                    if s.front:
                        part(*args)

                back(attention)
                if s.front:
                    dve.wait_ge(h_loaded, 32 * (q + 1))
                if not s.back:
                    channel_sums(1, xc[:, :, :])
                front(centre, 1, xc[:, :, :], xc[:, :, :])
                back(residual, 0)
                back(residual, 1)
                front(square_sums, 1, q, x1sq)
                back(residual, 2)
                back(residual, 3)
                front(normalise, 1, q, xc[:, :, :])
                back(residual, 4)
                back(residual, 5)
                front(low, 1, q, xc[:, :, :], x1)
                back(residual, 6)
                back(residual, 7)
                if s.back:
                    read(dve, "o7", s)
                back(channel_sums, 2, h2[:, :, :])
                back(centre, 2, h2[:, :, :], xc[:, :, :])
                front(rope, 0, 4)
                back(square_sums, 2, p, x2sq)
                front(rope, 1, 0)
                back(normalise, 2, p, xc[:, :, :])
                front(rope, 2, 1)
                back(low, 2, p, xc[:, :, :], x2)
                front(rope, 3, 2)
                back(routing)
                front(queries_of_texts, 0)
                back(routing_copy)
                front(rope, 4, 3)
                for m in range(4):
                    back(scaled_in, m)
                front(queries_of_texts, 1)
                front(maxima, 0)
                for m in range(4, KB):
                    if m == KB - 1:
                        front(v_low, 0)
                        front(v_low, 1)
                    back(scaled_in, m)
                front(v_low, 2)
                for m in range(KB):
                    if m == 0:
                        front(maxima, 1)
                    if m < KB - 2:
                        front(maxima, m + 2)
                    if m == KB - 3:
                        front(maxima_split)
                    back(ffn_out, m)
                    if m in (0, 2):
                        front(queries_of_texts, 2 + m // 2)
                assert not s.front or n_own["front"] == OWN["front"], n_own
                assert not s.back or n_own["back"] == OWN["back"], n_own

            steps(dve, step)


def fusion_kernel(nc, D, out_d):
    h_d = nc.dram_tensor("tok_result", (NPAIR, P, IH, 2, HEADS), F32, kind="Internal").ap()
    s4d_block(nc, D["par"], D["xr"], D["xi"], D["digit"], D["phase"], h_d)
    rest(nc, D, h_d, out_d)


def kernel(x, txt, L0_tok_log_dt, L0_tok_B, L0_tok_inv_A_real, L0_tok_A_imag, L0_attn_Wq, L0_attn_Wk, L0_attn_Wv,
           L0_attn_Wo, L0_ffn_weight, L0_ffn_bias, L0_ffn_gate_w, L0_ffn_in_channel_scale, L0_ffn_out_channel_scale):
    import concourse.bacc as _bacc
    from concourse.bass_utils import run_bass_kernel_spmd as _run

    def twice(a):
        return np.concatenate([a, a], 0)

    def blocks(w, rows=None):
        w = w if rows is None else w[rows]
        return w.reshape(KB, P, -1).transpose(1, 0, 2)

    x, txt = np.asarray(x), np.asarray(txt)
    log_dt, B, inv_a, a_im = (np.asarray(a) for a in (L0_tok_log_dt, L0_tok_B, L0_tok_inv_A_real, L0_tok_A_imag))
    wq, wk, wv, wo, wf, wb, wg, ics, ocs = (np.asarray(a) for a in (
        L0_attn_Wq, L0_attn_Wk, L0_attn_Wv, L0_attn_Wo, L0_ffn_weight, L0_ffn_bias, L0_ffn_gate_w,
        L0_ffn_in_channel_scale, L0_ffn_out_channel_scale))
    arrays = {}
    arrays["par"] = np.stack([np.tile(log_dt, (P, 1)), twice(inv_a.T), twice(a_im.T), twice(B[..., 0].T), twice(B[..., 1].T)], 1)
    arrays["xr"] = twice(x[..., 0].transpose(2, 1, 0))
    arrays["xi"] = twice(x[..., 1].transpose(2, 1, 0))
    arrays["txt"] = txt.reshape(NPAIR, 2, 32, KB, P).transpose(0, 4, 3, 1, 2).reshape(NPAIR, P, KB, 64)
    j, a, i, h = np.meshgrid(np.arange(4), np.arange(2), np.arange(16), np.arange(8), indexing="ij")
    cols = ((8 * j + h) * HD + 2 * i + a).reshape(-1)
    arrays["wq"] = blocks(wq[:, cols])
    arrays["wk"] = blocks(wk[:, cols[:256]])
    arrays["wv"] = blocks(wv)
    g, hh, kv, d = np.meshgrid(np.arange(2), np.arange(4), np.arange(4), np.arange(HD), indexing="ij")
    arrays["wo"] = blocks(wo, (((4 * g + kv) * 4 + hh) * HD + d).reshape(-1))
    arrays["wf"] = blocks(wf.T)
    arrays["wg"] = blocks(wg.T)
    arrays["we"] = np.stack([np.tile(ics, (4, 1)), np.tile(ocs, (4, 1))], 1)
    arrays["bias"] = wb.reshape(KB, P).T
    arrays["digit"] = np.tile(np.concatenate([np.arange(JL), JL * np.arange(IH)]).astype(np.float32), (P, 1))
    phase = np.zeros((P, 4), np.float32)
    phase[:MODES, 0], phase[:MODES, 1], phase[:, 3] = 0.25, 0.25 * TURN, 0.25 * TURN
    arrays["phase"] = phase
    inv_freq = (1.0 / np.float32(10000.0) ** (np.arange(0, HD, 2, dtype=np.float32) / HD)).astype(np.float32)
    pos = np.concatenate([np.arange(128), np.arange(128), np.arange(128, 160), np.arange(128, 160)]).astype(np.float32)
    ang = np.repeat(inv_freq, 8)[:, None] * pos[None]
    arrays["cos"] = (np.cos(ang) / XS).astype(np.float32)
    arrays["sin"] = (np.sin(ang) / XS).astype(np.float32)
    never = np.float32(-3e38)
    r = np.arange(P)
    mask_b = np.where(np.arange(32)[None] > (r % 32)[:, None], never, 0).astype(np.float32)
    b_key, k = (r - 64) // 32, (r - 64) % 32
    b_query, query = np.arange(64) // 32, np.arange(64) % 32
    mask_t = np.where((b_key[:, None] == b_query[None]) & (k[:, None] <= query[None]), np.float32(0), never).astype(np.float32)
    arrays["masks"] = np.concatenate([np.eye(P, dtype=np.float32), np.full((P, P), 1.0 / DIM, np.float32),
                                      np.where(r[None] > r[:, None], never, 0).astype(np.float32), mask_b,
                                      np.where(r[:, None] > r[None], never, 0).astype(np.float32), mask_t], 1)
    consts = np.zeros((P, 8), np.float32)
    consts[:, 0], consts[:16, 1], consts[16:32, 2] = EPS, 1, 1
    arrays["consts"] = consts

    nc = _bacc.Bacc("TRN2", target_bir_lowering=False, num_devices=1)
    feed, D = {}, {}
    for name, value in arrays.items():
        value = np.ascontiguousarray(value)
        feed[f"in_{name}"] = value
        D[name] = nc.dram_tensor(f"in_{name}", value.shape, F32, kind="ExternalInput").ap()
    out_d = nc.dram_tensor("out_0", (NPAIR, P, KB, T), F32, kind="ExternalOutput").ap()
    fusion_kernel(nc, D, out_d)
    got = _run(nc, [feed], core_ids=[0]).results[0]["out_0"]
    got = np.asarray(got).transpose(0, 3, 2, 1).reshape(NPAIR, T, DIM)
    s4 = got[:, :256].reshape(CH, P, DIM)
    text = got[:, 256:].reshape(CH, 32, DIM)
    return np.concatenate([s4, text], 1)
```
